# Optimizing a Trainium2 kernel written in Bass

```python
import numpy as np
import jax
import jax.numpy as jnp

def _softmax(x, axis=-1):
    return jax.nn.softmax(x, axis=axis)

def _gelu(x):
    return jax.nn.gelu(x, approximate=True)

def _silu(x):
    return jax.nn.silu(x)

def _sigmoid(x):
    return jax.nn.sigmoid(x)

def _layernorm(x, axis=-1, eps=1e-05):
    m = jnp.mean(x, axis=axis, keepdims=True)
    v = jnp.var(x, axis=axis, keepdims=True)
    return (x - m) / jnp.sqrt(v + eps)

def _scatter_add(tgt, idx, src, axis=0):
    return tgt.at[idx].add(src)

def _segment_sum(src, seg, n):
    return jax.ops.segment_sum(src, seg, n)
kernel_name = 'mk_xattn_ffn_d4_seqx_r8_013205'

def setup_inputs(seed: int=0):
    np.random.seed(seed)
    _w = jnp.asarray

    def _rec_inputs():
        import jax
        import jax.numpy as jnp
        _rk = jax.random.key(seed)
        x = 0.0003765 + 1 * jax.random.normal(jax.random.fold_in(_rk, 1), (4, 512, 128), jnp.float32)
        _lenS = 512 - jax.random.randint(jax.random.fold_in(_rk, 7), (4,), 0, max(1, 512 // 4) + 1, jnp.int32)
        _lenS2 = 77 - jax.random.randint(jax.random.fold_in(_rk, 8), (4,), 0, max(1, 77 // 4) + 1, jnp.int32)
        _ctx_1024P = jax.random.normal(jax.random.fold_in(_rk, 11), (4, 16, 128), jnp.float32)
        _ctx_1024c = jax.random.dirichlet(jax.random.fold_in(_rk, 511), 0.3 * jnp.ones((16,), jnp.float32), (4, 77))
        _ctx_1024t = jnp.einsum('bsk,bkd->bsd', _ctx_1024c, _ctx_1024P)
        _ctx_1024t = _ctx_1024t * jax.lax.rsqrt(jnp.mean(jnp.square(_ctx_1024t)) + 1e-12) * 0.953939
        ctx_1024 = -0.000292821 + 1.00034 * (_ctx_1024t + 0.3 * jax.random.normal(jax.random.fold_in(_rk, 611), (4, 77, 128), jnp.float32))
        itok_BxS_0_1023 = jax.random.randint(jax.random.fold_in(_rk, 13), (4, 512), 0, 128, jnp.int32)
        itok_BxS2_0_2047 = jax.random.randint(jax.random.fold_in(_rk, 14), (4, 77), 0, 256, jnp.int32)
        _validS = jnp.arange(512)[None, :] < _lenS[:, None]
        _validS2 = jnp.arange(77)[None, :] < _lenS2[:, None]
        _causal = jnp.tril(jnp.ones((512, 512), dtype=bool))
        mask_Bx1xSxS2_if1 = jnp.where(jnp.ones((4, 1, 512, 77), dtype=bool), 1, 0).astype(jnp.int32)
        return (x, ctx_1024, itok_BxS_0_1023, itok_BxS2_0_2047, mask_Bx1xSxS2_if1)
    x, ctx_1024, itok_BxS_0_1023, itok_BxS2_0_2047, mask_Bx1xSxS2_if1 = _rec_inputs()

    def _L0_xattn_setup():
        import jax, jax.numpy as jnp
        import numpy as np
        EMBED_SIZE = 128
        HEADS = 16
        HEAD_DIM = EMBED_SIZE // HEADS
        key = jax.random.key(seed)
        k1, k2, k3, k4, k5 = jax.random.split(key, 5)
        N, S = (2, 256)
        values = jax.random.normal(k1, (N, S, EMBED_SIZE), dtype=jnp.float32)
        keys = jax.random.normal(k2, (N, S, EMBED_SIZE), dtype=jnp.float32)
        query = jax.random.normal(k3, (N, S, EMBED_SIZE), dtype=jnp.float32)
        mask = jnp.ones((N, 1, S, S), dtype=jnp.int32)
        W_out = jax.random.normal(k4, (EMBED_SIZE, EMBED_SIZE), dtype=jnp.float32) / np.sqrt(EMBED_SIZE)
        b_out = jax.random.normal(k5, (EMBED_SIZE,), dtype=jnp.float32) * 0.01
        return {'values': values, 'keys': keys, 'query': query, 'mask': mask, 'W_out': W_out, 'b_out': b_out}
    _L0_xattn_all = _L0_xattn_setup()
    _L0_xattn_in = {k: v for k, v in _L0_xattn_all.items() if k in ('W_out', 'b_out')}
    del _L0_xattn_all

    def _L0_ffn_setup():
        import jax, jax.numpy as jnp
        import numpy as np
        from jax import lax
        D = 128
        H = 512
        E = 8
        TOPK = 2
        key = jax.random.key(seed)
        ks = jax.random.split(key, 7)
        s = 0.02
        return {'x': jax.random.normal(ks[0], (2, 256, D), dtype=jnp.float32), 'W1': jax.random.normal(ks[1], (E, D, H), dtype=jnp.float32) * s, 'b1': jnp.zeros((E, H), dtype=jnp.float32), 'W2': jax.random.normal(ks[2], (E, H, D), dtype=jnp.float32) * s, 'b2': jnp.zeros((E, D), dtype=jnp.float32), 'Wr': jax.random.normal(ks[3], (D, E), dtype=jnp.float32) * s, 'br': jnp.zeros((E,), dtype=jnp.float32)}
    _L0_ffn_all = _L0_ffn_setup()
    _L0_ffn_in = {k: v for k, v in _L0_ffn_all.items() if k in ('W1', 'b1', 'W2', 'b2', 'Wr', 'br')}
    del _L0_ffn_all

    def _L1_xattn_setup():
        import jax, jax.numpy as jnp
        import numpy as np
        DIM_IN = 128
        DIM_QK = 128
        DIM_V = 128
        key = jax.random.key(seed)
        ks = jax.random.split(key, 8)
        s = DIM_IN ** (-0.5)
        return {'x': jax.random.normal(ks[0], (16, 256, DIM_IN), dtype=jnp.float32), 'encoder_output': jax.random.normal(ks[1], (16, 256, DIM_IN), dtype=jnp.float32), 'W_q': jax.random.normal(ks[2], (DIM_IN, DIM_QK), dtype=jnp.float32) * s, 'b_q': jnp.zeros((DIM_QK,), dtype=jnp.float32), 'W_k': jax.random.normal(ks[3], (DIM_IN, DIM_QK), dtype=jnp.float32) * s, 'b_k': jnp.zeros((DIM_QK,), dtype=jnp.float32), 'W_v': jax.random.normal(ks[4], (DIM_IN, DIM_V), dtype=jnp.float32) * s, 'b_v': jnp.zeros((DIM_V,), dtype=jnp.float32)}
    _L1_xattn_all = _L1_xattn_setup()
    _L1_xattn_in = {k: v for k, v in _L1_xattn_all.items() if k in ('W_q', 'b_q', 'W_k', 'b_k', 'W_v', 'b_v')}
    del _L1_xattn_all

    def _L1_ffn_setup():
        import jax, jax.numpy as jnp
        import numpy as np
        D = 128
        H = 256
        E = 8
        TOP_K = 2
        N_SHARED = 1
        B, S = (2, 128)
        key = jax.random.key(seed)
        ks = jax.random.split(key, 12)
        sc = 0.02
        return {'hidden': jax.random.normal(ks[0], (B, S, D), jnp.float32), 'router_w': jax.random.normal(ks[1], (D, E), jnp.float32) * sc, 'router_b': jnp.zeros((E,), jnp.float32), 'sw1': jax.random.normal(ks[2], (D, H), jnp.float32) * sc, 'sb1': jnp.zeros((H,), jnp.float32), 'sw2': jax.random.normal(ks[3], (H, D), jnp.float32) * sc, 'sb2': jnp.zeros((D,), jnp.float32), 'rw1': jax.random.normal(ks[4], (E, D, H), jnp.float32) * sc, 'rb1': jnp.zeros((E, H), jnp.float32), 'rw2': jax.random.normal(ks[5], (E, H, D), jnp.float32) * sc, 'rb2': jnp.zeros((E, D), jnp.float32)}
    _L1_ffn_all = _L1_ffn_setup()
    _L1_ffn_in = {k: v for k, v in _L1_ffn_all.items() if k in ('router_w', 'router_b', 'sw1', 'sb1', 'sw2', 'sb2', 'rw1', 'rb1', 'rw2', 'rb2')}
    del _L1_ffn_all

    def _L2_xattn_setup():
        import jax, jax.numpy as jnp
        import numpy as np
        DIM = 128
        H = 16
        HD = DIM // H
        SCALE = HD ** (-0.5)
        LAMBDA_INIT = 0.1
        EPS = 1e-06

        def _split_heads(x, B, N):
            return x.reshape(B, N, H, HD).transpose(0, 2, 1, 3)
        key0 = jax.random.key(seed)
        ks = jax.random.split(key0, 12)
        B, Nq, Nk = (2, 128, 256)
        w = 0.02
        inp = {'query': jax.random.normal(ks[0], (B, Nq, DIM), jnp.float32), 'key': jax.random.normal(ks[1], (B, Nk, DIM), jnp.float32), 'value': jax.random.normal(ks[2], (B, Nk, DIM), jnp.float32), 'qpos': jax.random.randint(ks[3], (B, Nq), 0, Nq, jnp.int32), 'kpos': jax.random.randint(ks[4], (B, Nk), 0, Nk, jnp.int32), 'q1_w': jax.random.normal(ks[5], (DIM, DIM), jnp.float32) * w, 'q2_w': jax.random.normal(ks[6], (DIM, DIM), jnp.float32) * w, 'kv1_w': jax.random.normal(ks[7], (2 * DIM, DIM), jnp.float32) * w, 'kv2_w': jax.random.normal(ks[8], (2 * DIM, DIM), jnp.float32) * w, 'proj_w': jax.random.normal(ks[9], (DIM, DIM), jnp.float32) * w, 'proj_b': jnp.zeros((DIM,), jnp.float32), 'norm_w': jnp.ones((DIM,), jnp.float32), 'lambda_1': jnp.ones((1, H, 1, 1), jnp.float32), 'lambda_2': jnp.full((1, H, 1, 1), 1.0 - LAMBDA_INIT * (1.0 / 12.0), jnp.float32)}
        return inp
    _L2_xattn_all = _L2_xattn_setup()
    _L2_xattn_in = {k: v for k, v in _L2_xattn_all.items() if k in ('q1_w', 'q2_w', 'kv1_w', 'kv2_w', 'proj_w', 'proj_b', 'norm_w', 'lambda_1', 'lambda_2')}
    del _L2_xattn_all

    def _L2_ffn_setup():
        import jax, jax.numpy as jnp
        import numpy as np
        E = 8
        K = 2
        CF = 1.2
        D = 128
        F = 512
        B, S = (4, 128)
        key = jax.random.key(seed)
        ks = jax.random.split(key, 4)

        def init(k, shape, fan_in):
            return jax.random.normal(k, shape, jnp.float32) * (1.0 / np.sqrt(fan_in))
        return {'x': jax.random.normal(ks[0], (B, S, D), jnp.float32), 'Wg': init(ks[1], (D, E), D), 'bg': jnp.zeros((E,), jnp.float32), 'W1': init(ks[2], (E, D, F), D), 'b1': jnp.zeros((E, F), jnp.float32), 'W2': init(ks[3], (E, F, D), F), 'b2': jnp.zeros((E, D), jnp.float32)}
    _L2_ffn_all = _L2_ffn_setup()
    _L2_ffn_in = {k: v for k, v in _L2_ffn_all.items() if k in ('Wg', 'bg', 'W1', 'b1', 'W2', 'b2')}
    del _L2_ffn_all

    def _L3_xattn_setup():
        import jax, jax.numpy as jnp
        import numpy as np
        D_MODEL = 128
        NUM_HEADS = 16
        HEAD_DIM = D_MODEL // NUM_HEADS
        SCALE = HEAD_DIM ** (-0.5)
        BIAS_LEN = 128
        ROPE_BASE = 10000.0
        LN_EPS = 1e-05

        def _layernorm(x, gamma, beta):
            mu = jnp.mean(x, axis=-1, keepdims=True)
            var = jnp.mean(jnp.square(x - mu), axis=-1, keepdims=True)
            return (x - mu) * jax.lax.rsqrt(var + LN_EPS) * gamma + beta

        def _rope(x, cos, sin):
            half = HEAD_DIM // 2
            c = cos[None, None, :, :]
            s = sin[None, None, :, :]
            x_even, x_odd = (x[..., :half], x[..., half:])
            return jnp.concatenate([x_even * c - x_odd * s, x_even * s + x_odd * c], axis=-1)

        def _temporal_bias(L_q, L_kv):
            pos = jnp.arange(BIAS_LEN, dtype=jnp.float32)
            dist = jnp.abs(pos[None, :] - pos[:, None])
            bias = jnp.exp(-dist * 0.1) - dist * 0.05
            if L_q <= BIAS_LEN and L_kv <= BIAS_LEN:
                return bias[:L_q, :L_kv]
            return jax.image.resize(bias, (L_q, L_kv), method='bilinear')
        key = jax.random.key(seed)
        ks = jax.random.split(key, 8)
        B, Lq, Lkv = (8, 64, 64)
        return {'decoder_hidden': jax.random.normal(ks[0], (B, Lq, D_MODEL), jnp.float32), 'encoder_output': jax.random.normal(ks[1], (B, Lkv, D_MODEL), jnp.float32), 'Wqkv': jax.random.normal(ks[2], (3 * D_MODEL, D_MODEL), jnp.float32) * 0.02, 'Wout': jax.random.normal(ks[3], (D_MODEL, D_MODEL), jnp.float32) * 0.02, 'b_out': jnp.zeros((D_MODEL,), jnp.float32), 'Wgate': jax.random.normal(ks[4], (D_MODEL, D_MODEL), jnp.float32) * 0.02, 'b_gate': jnp.zeros((D_MODEL,), jnp.float32), 'gamma': jnp.ones((D_MODEL,), jnp.float32), 'beta': jnp.zeros((D_MODEL,), jnp.float32)}
    _L3_xattn_all = _L3_xattn_setup()
    _L3_xattn_in = {k: v for k, v in _L3_xattn_all.items() if k in ('Wqkv', 'Wout', 'b_out', 'Wgate', 'b_gate', 'gamma', 'beta')}
    del _L3_xattn_all

    def _L3_ffn_setup():
        import jax, jax.numpy as jnp
        import numpy as np
        EPS = 1e-06
        TOP_K = 2
        key = jax.random.key(seed)
        k0, k1, k2, k3, k4 = jax.random.split(key, 5)
        B, S, H, I, E = (1, 256, 128, 448, 8)
        return {'hidden_states': jax.random.normal(k0, (B, S, H), jnp.float32), 'rms_weight': jnp.ones((H,), jnp.float32), 'gate_w': jax.random.normal(k1, (E, H), jnp.float32) * H ** (-0.5), 'w1': jax.random.normal(k2, (E, I, H), jnp.float32) * H ** (-0.5), 'w2': jax.random.normal(k3, (E, H, I), jnp.float32) * I ** (-0.5), 'w3': jax.random.normal(k4, (E, I, H), jnp.float32) * H ** (-0.5)}
    _L3_ffn_all = _L3_ffn_setup()
    _L3_ffn_in = {k: v for k, v in _L3_ffn_all.items() if k in ('rms_weight', 'gate_w', 'w1', 'w2', 'w3')}
    del _L3_ffn_all
    return {'x': x, 'ctx_1024': ctx_1024, 'itok_BxS_0_1023': itok_BxS_0_1023, 'itok_BxS2_0_2047': itok_BxS2_0_2047, 'mask_Bx1xSxS2_if1': mask_Bx1xSxS2_if1, 'L0_xattn_W_out': _L0_xattn_in['W_out'], 'L0_xattn_b_out': _L0_xattn_in['b_out'], 'L0_ffn_W1': _L0_ffn_in['W1'], 'L0_ffn_b1': _L0_ffn_in['b1'], 'L0_ffn_W2': _L0_ffn_in['W2'], 'L0_ffn_b2': _L0_ffn_in['b2'], 'L0_ffn_Wr': _L0_ffn_in['Wr'], 'L0_ffn_br': _L0_ffn_in['br'], 'L1_xattn_W_q': _L1_xattn_in['W_q'], 'L1_xattn_b_q': _L1_xattn_in['b_q'], 'L1_xattn_W_k': _L1_xattn_in['W_k'], 'L1_xattn_b_k': _L1_xattn_in['b_k'], 'L1_xattn_W_v': _L1_xattn_in['W_v'], 'L1_xattn_b_v': _L1_xattn_in['b_v'], 'L1_ffn_router_w': _L1_ffn_in['router_w'], 'L1_ffn_router_b': _L1_ffn_in['router_b'], 'L1_ffn_sw1': _L1_ffn_in['sw1'], 'L1_ffn_sb1': _L1_ffn_in['sb1'], 'L1_ffn_sw2': _L1_ffn_in['sw2'], 'L1_ffn_sb2': _L1_ffn_in['sb2'], 'L1_ffn_rw1': _L1_ffn_in['rw1'], 'L1_ffn_rb1': _L1_ffn_in['rb1'], 'L1_ffn_rw2': _L1_ffn_in['rw2'], 'L1_ffn_rb2': _L1_ffn_in['rb2'], 'L2_xattn_q1_w': _L2_xattn_in['q1_w'], 'L2_xattn_q2_w': _L2_xattn_in['q2_w'], 'L2_xattn_kv1_w': _L2_xattn_in['kv1_w'], 'L2_xattn_kv2_w': _L2_xattn_in['kv2_w'], 'L2_xattn_proj_w': _L2_xattn_in['proj_w'], 'L2_xattn_proj_b': _L2_xattn_in['proj_b'], 'L2_xattn_norm_w': _L2_xattn_in['norm_w'], 'L2_xattn_lambda_1': _L2_xattn_in['lambda_1'], 'L2_xattn_lambda_2': _L2_xattn_in['lambda_2'], 'L2_ffn_Wg': _L2_ffn_in['Wg'], 'L2_ffn_bg': _L2_ffn_in['bg'], 'L2_ffn_W1': _L2_ffn_in['W1'], 'L2_ffn_b1': _L2_ffn_in['b1'], 'L2_ffn_W2': _L2_ffn_in['W2'], 'L2_ffn_b2': _L2_ffn_in['b2'], 'L3_xattn_Wqkv': _L3_xattn_in['Wqkv'], 'L3_xattn_Wout': _L3_xattn_in['Wout'], 'L3_xattn_b_out': _L3_xattn_in['b_out'], 'L3_xattn_Wgate': _L3_xattn_in['Wgate'], 'L3_xattn_b_gate': _L3_xattn_in['b_gate'], 'L3_xattn_gamma': _L3_xattn_in['gamma'], 'L3_xattn_beta': _L3_xattn_in['beta'], 'L3_ffn_rms_weight': _L3_ffn_in['rms_weight'], 'L3_ffn_gate_w': _L3_ffn_in['gate_w'], 'L3_ffn_w1': _L3_ffn_in['w1'], 'L3_ffn_w2': _L3_ffn_in['w2'], 'L3_ffn_w3': _L3_ffn_in['w3']}

def reference(x, ctx_1024, itok_BxS_0_1023, itok_BxS2_0_2047, mask_Bx1xSxS2_if1, L0_xattn_W_out, L0_xattn_b_out, L0_ffn_W1, L0_ffn_b1, L0_ffn_W2, L0_ffn_b2, L0_ffn_Wr, L0_ffn_br, L1_xattn_W_q, L1_xattn_b_q, L1_xattn_W_k, L1_xattn_b_k, L1_xattn_W_v, L1_xattn_b_v, L1_ffn_router_w, L1_ffn_router_b, L1_ffn_sw1, L1_ffn_sb1, L1_ffn_sw2, L1_ffn_sb2, L1_ffn_rw1, L1_ffn_rb1, L1_ffn_rw2, L1_ffn_rb2, L2_xattn_q1_w, L2_xattn_q2_w, L2_xattn_kv1_w, L2_xattn_kv2_w, L2_xattn_proj_w, L2_xattn_proj_b, L2_xattn_norm_w, L2_xattn_lambda_1, L2_xattn_lambda_2, L2_ffn_Wg, L2_ffn_bg, L2_ffn_W1, L2_ffn_b1, L2_ffn_W2, L2_ffn_b2, L3_xattn_Wqkv, L3_xattn_Wout, L3_xattn_b_out, L3_xattn_Wgate, L3_xattn_b_gate, L3_xattn_gamma, L3_xattn_beta, L3_ffn_rms_weight, L3_ffn_gate_w, L3_ffn_w1, L3_ffn_w2, L3_ffn_w3):
    import jax
    import jax.numpy as jnp

    def _L0_xattn_ref(values, keys, query, mask, W_out, b_out):
        import jax, jax.numpy as jnp
        import numpy as np
        EMBED_SIZE = 128
        HEADS = 16
        HEAD_DIM = EMBED_SIZE // HEADS
        N, Q = (query.shape[0], query.shape[1])
        K = keys.shape[1]
        v = values.reshape(N, K, HEADS, HEAD_DIM)
        k = keys.reshape(N, K, HEADS, HEAD_DIM)
        q = query.reshape(N, Q, HEADS, HEAD_DIM)
        energy = jnp.einsum('nqhd,nkhd->nhqk', q, k)
        energy = jnp.where(mask == 0, jnp.float32(-1e+20), energy)
        attention = jax.nn.softmax(energy / jnp.sqrt(jnp.float32(EMBED_SIZE)), axis=3)
        out = jnp.einsum('nhqk,nkhd->nqhd', attention, v).reshape(N, Q, EMBED_SIZE)
        return out @ W_out.T + b_out

    def _L0_ffn_ref(x, W1, b1, W2, b2, Wr, br):
        import jax, jax.numpy as jnp
        import numpy as np
        from jax import lax
        D = 128
        H = 512
        E = 8
        TOPK = 2
        B, S, _ = x.shape
        xf = x.reshape(-1, D)
        logits = xf @ Wr + br
        topv, _ = lax.top_k(logits, TOPK)
        thresh = topv[:, TOPK - 1:TOPK]
        masked = jnp.where(logits >= thresh, logits, -jnp.inf)
        weights = jax.nn.softmax(masked, axis=-1)
        h = jax.nn.gelu(jnp.einsum('td,edh->eth', xf, W1) + b1[:, None, :], approximate=False)
        expert_out = jnp.einsum('eth,ehd->etd', h, W2) + b2[:, None, :]
        out = jnp.einsum('etd,te->td', expert_out, weights)
        return out.reshape(B, S, D)

    def _L1_xattn_ref(x, encoder_output, W_q, b_q, W_k, b_k, W_v, b_v):
        import jax, jax.numpy as jnp
        import numpy as np
        DIM_IN = 128
        DIM_QK = 128
        DIM_V = 128
        Q = x @ W_q + b_q
        K = encoder_output @ W_k + b_k
        V = encoder_output @ W_v + b_v
        scores = jnp.einsum('bqd,bkd->bqk', Q, K) * K.shape[-1] ** (-0.5)
        weights = jax.nn.softmax(scores, axis=-1)
        H = jnp.einsum('bqk,bkv->bqv', weights, V)
        return H

    def _L1_ffn_ref(hidden, router_w, router_b, sw1, sb1, sw2, sb2, rw1, rb1, rw2, rb2):
        import jax, jax.numpy as jnp
        import numpy as np
        D = 128
        H = 256
        E = 8
        TOP_K = 2
        N_SHARED = 1
        B, S = (2, 128)
        b, s, d = hidden.shape
        T = b * s
        flat = hidden.reshape(T, d)
        router_logits = flat @ router_w + router_b
        router_probs = jax.nn.softmax(router_logits, axis=-1)
        topk_probs, topk_idx = jax.lax.top_k(router_probs, TOP_K)
        weights = jnp.zeros_like(router_probs).at[jnp.arange(T)[:, None], topk_idx].add(topk_probs)
        sh = jax.nn.gelu(flat @ sw1 + sb1, approximate=False)
        shared_out = (sh @ sw2 + sb2) / N_SHARED
        h1 = jax.nn.gelu(jnp.einsum('td,edh->teh', flat, rw1) + rb1[None], approximate=False)
        expert_out = jnp.einsum('teh,ehd->ted', h1, rw2) + rb2[None]
        mixed = jnp.einsum('ted,te->td', expert_out, weights)
        return (shared_out + mixed).reshape(b, s, d)

    def _L2_xattn_ref(query, key, value, qpos, kpos, q1_w, q2_w, kv1_w, kv2_w, proj_w, proj_b, norm_w, lambda_1, lambda_2):
        import jax, jax.numpy as jnp
        import numpy as np
        DIM = 128
        H = 16
        HD = DIM // H
        SCALE = HD ** (-0.5)
        LAMBDA_INIT = 0.1
        EPS = 1e-06

        def _split_heads(x, B, N):
            return x.reshape(B, N, H, HD).transpose(0, 2, 1, 3)
        B, Nq, C = query.shape
        Nk = key.shape[1]
        q1 = _split_heads(query @ q1_w.T, B, Nq)
        q2 = _split_heads(query @ q2_w.T, B, Nq)
        kv1 = (key @ kv1_w.T).reshape(B, Nk, 2, H, HD).transpose(2, 0, 3, 1, 4)
        k1, v1 = (kv1[0], kv1[1])
        kv2 = (key @ kv2_w.T).reshape(B, Nk, 2, H, HD).transpose(2, 0, 3, 1, 4)
        k2 = kv2[0]
        attn1 = jax.nn.softmax(jnp.einsum('bhqd,bhkd->bhqk', q1, k1) * SCALE, axis=-1)
        attn2 = jax.nn.softmax(jnp.einsum('bhqd,bhkd->bhqk', q2, k2) * SCALE, axis=-1)
        lambda_full = lambda_1 - lambda_2 + LAMBDA_INIT
        diff_attn = attn1 - lambda_full * attn2
        x = jnp.einsum('bhqk,bhkd->bhqd', diff_attn, v1)
        x = x.transpose(0, 2, 1, 3).reshape(B, Nq, C)
        xf = x.astype(jnp.float32)
        xf = xf * jax.lax.rsqrt(jnp.mean(xf * xf, axis=-1, keepdims=True) + EPS) * norm_w
        x = xf.astype(x.dtype)
        return x @ proj_w.T + proj_b

    def _L2_ffn_ref(x, Wg, bg, W1, b1, W2, b2):
        import jax, jax.numpy as jnp
        import numpy as np
        E = 8
        K = 2
        CF = 1.2
        D = 128
        F = 512
        B, S = (4, 128)
        Bx, Sx, Dx = x.shape
        T = Bx * Sx
        xt = x.reshape(T, Dx)
        logits = xt @ Wg + bg
        probs = jax.nn.softmax(logits, axis=-1)
        gate_vals, exp_idx = jax.lax.top_k(probs, K)
        gate_vals = gate_vals / jnp.sum(gate_vals, axis=-1, keepdims=True)
        capacity = int(np.ceil(CF * T * K / E))
        eidx = exp_idx.T.reshape(-1)
        gv = gate_vals.T.reshape(-1)
        oh = jax.nn.one_hot(eidx, E, dtype=jnp.int32)
        pos = jnp.sum((jnp.cumsum(oh, axis=0) - oh) * oh, axis=-1)
        keep = pos < capacity
        pos_c = jnp.where(keep, pos, capacity)
        xk = jnp.tile(xt, (K, 1))
        buf = jnp.zeros((E, capacity + 1, Dx), x.dtype)
        buf = buf.at[eidx, pos_c].add(jnp.where(keep[:, None], xk, 0.0))
        buf = buf[:, :capacity]
        h = jax.nn.gelu(jnp.einsum('ecd,edf->ecf', buf, W1) + b1[:, None, :], approximate=True)
        ye = jnp.einsum('ecf,efd->ecd', h, W2) + b2[:, None, :]
        ye = jnp.concatenate([ye, jnp.zeros((E, 1, Dx), ye.dtype)], axis=1)
        gathered = ye[eidx, pos_c] * (gv * keep.astype(gv.dtype))[:, None]
        out = jnp.sum(gathered.reshape(K, T, Dx), axis=0)
        return out.reshape(Bx, Sx, Dx)

    def _L3_xattn_ref(decoder_hidden, encoder_output, Wqkv, Wout, b_out, Wgate, b_gate, gamma, beta):
        import jax, jax.numpy as jnp
        import numpy as np
        D_MODEL = 128
        NUM_HEADS = 16
        HEAD_DIM = D_MODEL // NUM_HEADS
        SCALE = HEAD_DIM ** (-0.5)
        BIAS_LEN = 128
        ROPE_BASE = 10000.0
        LN_EPS = 1e-05

        def _layernorm(x, gamma, beta):
            mu = jnp.mean(x, axis=-1, keepdims=True)
            var = jnp.mean(jnp.square(x - mu), axis=-1, keepdims=True)
            return (x - mu) * jax.lax.rsqrt(var + LN_EPS) * gamma + beta

        def _rope(x, cos, sin):
            half = HEAD_DIM // 2
            c = cos[None, None, :, :]
            s = sin[None, None, :, :]
            x_even, x_odd = (x[..., :half], x[..., half:])
            return jnp.concatenate([x_even * c - x_odd * s, x_even * s + x_odd * c], axis=-1)

        def _temporal_bias(L_q, L_kv):
            pos = jnp.arange(BIAS_LEN, dtype=jnp.float32)
            dist = jnp.abs(pos[None, :] - pos[:, None])
            bias = jnp.exp(-dist * 0.1) - dist * 0.05
            if L_q <= BIAS_LEN and L_kv <= BIAS_LEN:
                return bias[:L_q, :L_kv]
            return jax.image.resize(bias, (L_q, L_kv), method='bilinear')
        B, L_q, _ = decoder_hidden.shape
        L_kv = encoder_output.shape[1]
        residual = decoder_hidden
        q_in = _layernorm(decoder_hidden, gamma, beta)
        kv_in = _layernorm(encoder_output, gamma, beta)
        q = q_in @ Wqkv[:D_MODEL].T
        k = kv_in @ Wqkv[D_MODEL:2 * D_MODEL].T
        v = kv_in @ Wqkv[2 * D_MODEL:].T
        q = q.reshape(B, L_q, NUM_HEADS, HEAD_DIM).transpose(0, 2, 1, 3)
        k = k.reshape(B, L_kv, NUM_HEADS, HEAD_DIM).transpose(0, 2, 1, 3)
        v = v.reshape(B, L_kv, NUM_HEADS, HEAD_DIM).transpose(0, 2, 1, 3)
        L = max(L_q, L_kv)
        inv_freq = 1.0 / ROPE_BASE ** (jnp.arange(0, HEAD_DIM, 2, dtype=jnp.float32) / HEAD_DIM)
        freqs = jnp.arange(L, dtype=jnp.float32)[:, None] * inv_freq[None, :]
        cos, sin = (jnp.cos(freqs), jnp.sin(freqs))
        q = _rope(q, cos[:L_q], sin[:L_q])
        k = _rope(k, cos[:L_kv], sin[:L_kv])
        scores = jnp.einsum('bhqd,bhkd->bhqk', q, k) * SCALE
        scores = scores + _temporal_bias(L_q, L_kv)[None, None, :, :]
        attn = jax.nn.softmax(scores, axis=-1)
        attended = jnp.einsum('bhqk,bhkd->bhqd', attn, v)
        attended = attended.transpose(0, 2, 1, 3).reshape(B, L_q, D_MODEL)
        attended = attended @ Wout.T + b_out
        gate = jax.nn.sigmoid(attended @ Wgate.T + b_gate)
        output = gate * attended + (1.0 - gate) * residual
        return output

    def _L3_ffn_ref(hidden_states, rms_weight, gate_w, w1, w2, w3):
        import jax, jax.numpy as jnp
        import numpy as np
        EPS = 1e-06
        TOP_K = 2
        B, S, H = hidden_states.shape
        E = gate_w.shape[0]
        x = hidden_states.astype(jnp.float32)
        var = jnp.mean(x * x, axis=-1, keepdims=True)
        h = rms_weight * (x * jax.lax.rsqrt(var + EPS))
        logits = jnp.einsum('bsh,eh->bse', h, gate_w)
        scores = jax.nn.softmax(logits.astype(jnp.float32), axis=-1)
        top_w, top_i = jax.lax.top_k(scores, TOP_K)
        top_w = top_w / jnp.sum(top_w, axis=-1, keepdims=True)
        top_w = top_w.astype(h.dtype)
        hf = h.reshape(-1, H)
        oh = jax.nn.one_hot(top_i.reshape(-1, TOP_K), E, dtype=h.dtype)
        cw = jnp.einsum('tke,tk->te', oh, top_w.reshape(-1, TOP_K))
        a = jnp.einsum('th,eih->eti', hf, w1)
        g = jnp.einsum('th,eih->eti', hf, w3)
        eo = jnp.einsum('eti,ehi->eth', jax.nn.silu(a) * g, w2)
        out = jnp.einsum('eth,te->th', eo, cw)
        return hidden_states + out.reshape(B, S, H)
    x = x + _L0_xattn_ref(ctx_1024, ctx_1024, _layernorm(x, axis=-1), mask_Bx1xSxS2_if1, L0_xattn_W_out, L0_xattn_b_out)
    x = x + _L0_ffn_ref(_layernorm(x, axis=-1), L0_ffn_W1, L0_ffn_b1, L0_ffn_W2, L0_ffn_b2, L0_ffn_Wr, L0_ffn_br)
    x = x + _L1_xattn_ref(_layernorm(x, axis=-1), ctx_1024, L1_xattn_W_q, L1_xattn_b_q, L1_xattn_W_k, L1_xattn_b_k, L1_xattn_W_v, L1_xattn_b_v)
    x = x + _L1_ffn_ref(_layernorm(x, axis=-1), L1_ffn_router_w, L1_ffn_router_b, L1_ffn_sw1, L1_ffn_sb1, L1_ffn_sw2, L1_ffn_sb2, L1_ffn_rw1, L1_ffn_rb1, L1_ffn_rw2, L1_ffn_rb2)
    x = x + _L2_xattn_ref(_layernorm(x, axis=-1), ctx_1024, ctx_1024, itok_BxS_0_1023, itok_BxS2_0_2047, L2_xattn_q1_w, L2_xattn_q2_w, L2_xattn_kv1_w, L2_xattn_kv2_w, L2_xattn_proj_w, L2_xattn_proj_b, L2_xattn_norm_w, L2_xattn_lambda_1, L2_xattn_lambda_2)
    x = x + _L2_ffn_ref(_layernorm(x, axis=-1), L2_ffn_Wg, L2_ffn_bg, L2_ffn_W1, L2_ffn_b1, L2_ffn_W2, L2_ffn_b2)
    x = x + _L3_xattn_ref(_layernorm(x, axis=-1), ctx_1024, L3_xattn_Wqkv, L3_xattn_Wout, L3_xattn_b_out, L3_xattn_Wgate, L3_xattn_b_gate, L3_xattn_gamma, L3_xattn_beta)
    x = x + _L3_ffn_ref(_layernorm(x, axis=-1), L3_ffn_rms_weight, L3_ffn_gate_w, L3_ffn_w1, L3_ffn_w2, L3_ffn_w3)
    return x

_drawn_inputs = setup_inputs


def setup_inputs(seed=0):
    import zlib

    import numpy as np

    out = dict(_drawn_inputs(seed))
    spreads = {'L0_ffn_b1': (0.0, 0.1),
     'L0_ffn_b2': (0.0, 0.1),
     'L0_ffn_br': (0.0, 0.1),
     'L1_xattn_b_q': (0.0, 0.1),
     'L1_xattn_b_k': (0.0, 0.8),
     'L1_xattn_b_v': (0.0, 0.1),
     'L1_ffn_router_b': (0.0, 0.1),
     'L1_ffn_sb1': (0.0, 0.1),
     'L1_ffn_sb2': (0.0, 0.1),
     'L1_ffn_rb1': (0.0, 0.413),
     'L1_ffn_rb2': (0.0, 0.1),
     'L2_xattn_proj_b': (0.0, 0.1),
     'L2_xattn_norm_w': (1.0, 0.2),
     'L2_xattn_lambda_1': (1.0, 0.2),
     'L2_xattn_lambda_2': (0.9916666746139526, 0.2),
     'L2_ffn_bg': (0.0, 0.1),
     'L2_ffn_b1': (0.0, 0.1),
     'L2_ffn_b2': (0.0, 0.1),
     'L3_xattn_b_out': (0.0, 0.1),
     'L3_xattn_b_gate': (0.0, 0.364),
     'L3_xattn_gamma': (1.0, 0.6),
     'L3_xattn_beta': (0.0, 0.8),
     'L3_ffn_rms_weight': (1.0, 0.2)}
    factors = {'L2_xattn_q1_w': 2.77,
     'L2_xattn_q2_w': 6.087,
     'L2_xattn_kv2_w': 5.328,
     'L3_xattn_Wqkv': 4.487,
     'L3_xattn_Wout': 4.219,
     'L3_xattn_Wgate': 6.705}
    for name, (base, spread) in spreads.items():
        noise = np.random.default_rng([zlib.crc32(name.encode()), seed]).standard_normal(out[name].shape)
        drawn = base * np.exp(spread * noise) if base else spread * noise
        out[name] = jnp.asarray(drawn.astype(out[name].dtype))
    for name, factor in factors.items():
        out[name] = (out[name] * factor).astype(out[name].dtype)
    return out
```

```python
from contextlib import ExitStack

import numpy as np

import concourse.bass as bass
from concourse import mybir

F32 = mybir.dt.float32
I32 = mybir.dt.int32
ALU = mybir.AluOpType
ACT = mybir.ActivationFunctionType
AX = mybir.AxisListType

P = 128
B, S, K, D = 4, 512, 77, 128
NT = B * S // P
TG = S // P
NG = NT // TG
H, HD = 16, D // 16
RG, HR = 4, 4
E = 8
LN_EPS = 1e-5
RMS_EPS = 1e-6
CAPACITY = 615
NEG = -1.0e20

PARAMS = [
    ("ident", 128), ("blocks", RG), ("ctxT", B * K), ("ctx", B * D), ("L0x_wo", D), ("L0x_bo", D),
    ("iota", E), ("L0f_wr", E), ("L0f_br", E), ("L0f_b1", 32), ("L0f_b2", D),
    ("L1x_wq", D), ("L1x_wk", D), ("L1x_wv", D), ("L1x_bq", 1), ("L1x_bk", 1), ("L1x_bv", D),
    ("L1f_wr", E), ("L1f_br", E), ("L1f_b1", 18), ("L1f_b2", D),
    ("L2x_q1", D), ("L2x_q2", D), ("L2x_k1", D), ("L2x_v1", D), ("L2x_k2", D), ("L2x_wo", D),
    ("L2x_bo", D), ("L2x_norm", 1), ("L2x_lam1", H), ("L2x_lam2", H),
    ("L2f_wr", E), ("L2f_br", E), ("L2f_b1", 32), ("L2f_b2", D), ("before", P), ("ones", P),
    ("L3x_q", D), ("L3x_qr", D), ("L3x_k", D), ("L3x_kr", D), ("L3x_v", D), ("L3x_wo", D),
    ("L3x_bo", D), ("L3x_boc", 1), ("L3x_wg", D), ("L3x_bg", D), ("L3x_gamma", 1), ("L3x_beta", 1),
    ("cos", S), ("sin", S), ("tbias", TG * K), ("L3f_rms", 1), ("L3f_wr", E),
]
COLUMN = {}
_at = 0
for _name, _n in PARAMS:
    COLUMN[_name] = (_at, _n)
    _at += _n
NPAR = _at
NPAR_FIRST = COLUMN["iota"][0]

FFNS = {
    "L0f": dict(experts=8, chunks=4, rows=128, gated=False, act=ACT.Gelu),
    "L1f": dict(experts=9, chunks=2, rows=128, gated=False, act=ACT.Gelu),
    "L2f": dict(experts=8, chunks=4, rows=128, gated=False, act=ACT.Gelu_apprx_tanh),
    "L3f": dict(experts=8, chunks=4, rows=112, gated=True, act=ACT.Silu),
}


def build(nc, x_in, par_in, mask_in, w_in, out):
    ctx = ExitStack()

    def sb(name, shape, dt=F32):
        return ctx.enter_context(nc.sbuf_tensor(name, shape, dt))

    def plain_sem(name):
        return ctx.enter_context(nc.semaphore(name))

    roles = {}

    class Signal:
        def __init__(self, role, total):
            sm, base = roles.get(role) or (ctx.enter_context(nc.semaphore(role)), 0)
            self.sem, self.base, self.total = sm, base, total
            roles[role] = (sm, base + total)

        def at(self, n):
            return self.base + n

    def sem(name, total=1):
        return Signal(name, total)


    with ctx:
        X = sb("X", [P, NT, D])
        xn = sb("xn", [P, NT, D])
        xnT = sb("xnT", [P, NT * P])
        qa = sb("qa", [P, NT * P])
        qb = sb("qb", [P, NT * P])
        par = sb("par", [P, NPAR])
        score = sb("score", [P, 2, H, K])
        hT = sb("hT", [P, 2, 4, 512])
        gact = sb("gact", [P, 2, 512])
        regA = sb("regA", [P, 8192])
        regB = sb("regB", [P, 11264])
        kbd = [sb(f"kbd{i}", [P, B, HR, K]) for i in range(3)]
        vaug = [sb(f"vaug{i}", [K, B, H, HD + 1]) for i in range(3)]
        k1T = sb("k1T", [P, B * K])
        v1 = sb("v1", [K, B, D])
        bound = sb("bound", [P, NT, K])
        stats = sb("stats", [P, NT, 6])
        mv = sb("mv", [P, NT, 2])
        rstd = sb("rstd", [P, NT])
        vare = sb("vare", [P, NT])
        mhalf = sb("mhalf", [P, NT])
        mx = sb("mx", [P, 2, H])
        rec = sb("rec", [P, 2, H])
        lam = sb("lam", [P, H])
        oc = sb("oc", [P, 2, D])
        oc2 = sb("oc2", [P, 2, D])
        oss = sb("oss", [P, 2])
        osr = sb("osr", [P, 2])
        ocT = sb("ocT", [P, 2, P])
        attT = sb("attT", [P, 2, P])
        fin = sb("fin", [P, 5, D])
        hflat = hT[:, 0, :, :].rearrange("p c n -> p (c n)")
        rt = hflat[:, 0:8 * NT * E].rearrange("p (a t e) -> p a t e", a=8, t=NT)
        rc = hflat[:, 8 * NT * E:12 * NT * E].rearrange("p (a t e) -> p a t e", a=2, t=2 * NT)
        rs = sb("rs", [P, 6, 2 * NT])
        wts = sb("wts", [P, NT, 9])
        ctxn = score[0:K, 0, :, :].rearrange("p h k -> p (h k)")[:, 0:B * D].rearrange("p (b d) -> p b d", b=B)
        PS = ctx.enter_context(nc.psum_tensor("PS", [P, 8, 512], F32))

        def pc(name, rows=P):
            at, n = COLUMN[name]
            return par[0:rows, at:at + n]

        ident = pc("ident")
        qbw = qb[0:9, :]

        par_in_1 = plain_sem("par_first_loaded")
        par_in_2 = plain_sem("par_rest_loaded")
        x_loaded = [plain_sem(f"x_loaded{g}") for g in range(NG)]
        mask_loaded = plain_sem("mask_loaded")
        w_loaded = {f: [plain_sem(f"{f}_w_loaded{i}") for i in range(3)] for f in FFNS}
        w_done = {f: plain_sem(f"{f}_experts_done") for f in ("L0f", "L1f")}
        stored = plain_sem("stored")
        v_step = plain_sem("vector_step")
        p_step = plain_sem("pool_step")
        a_step = plain_sem("scalar_step")
        const_ready = plain_sem("const_ready")

        class Steps:
            def __init__(self):
                self.n = 0

            def one(self):
                self.n += 1
                return 1

        def w_third(f, e):
            return min(2, e * 3 // FFNS[f]["experts"])

        def third(f, i):
            n = FFNS[f]["experts"]
            es = [e for e in range(n) if w_third(f, e) == i]
            return es[0], es[-1] + 1

        def views(f):
            c = FFNS[f]
            reg = {"L0f": regA, "L1f": regB, "L2f": regA, "L3f": regB}[f]
            n, hid = c["experts"], c["chunks"] * c["rows"]
            a = n * hid
            w1 = reg[:, 0:a].rearrange("p (e h) -> p e h", e=n)
            w3 = reg[:, a:2 * a].rearrange("p (e h) -> p e h", e=n) if c["gated"] else None
            o = 2 * a if c["gated"] else a
            w2 = reg[:, o:o + n * c["chunks"] * D].rearrange("p (e c d) -> p e c d", e=n, c=c["chunks"])
            return w1, w3, w2

        def sync_program(sp, last_x_done):
            sp.dma_start(par[:, 0:NPAR_FIRST], par_in[:, 0:NPAR_FIRST]).then_inc(par_in_1, 16)
            for g in range(NG):
                sp.dma_start(X[:, TG * g:TG * g + TG, :], x_in[:, TG * g:TG * g + TG, :]).then_inc(x_loaded[g], 16)
            sp.dma_start(qb[:, 0:NT * K].bitcast(I32), mask_in).then_inc(mask_loaded, 16)
            sp.dma_start(par[:, NPAR_FIRST:NPAR], par_in[:, NPAR_FIRST:NPAR]).then_inc(par_in_2, 16)
            for f in ("L0f", "L1f", "L2f", "L3f"):
                if f == "L2f":
                    sp.wait_ge(w_done["L0f"], 1)
                if f == "L3f":
                    sp.wait_ge(w_done["L1f"], 1)
                w1, w3, w2 = views(f)
                rows = FFNS[f]["rows"]
                for i in range(3):
                    e0, e1 = third(f, i)
                    sp.dma_start(w1[:, e0:e1, :], w_in[f][0][:, e0:e1, :]).then_inc(w_loaded[f][i], 16)
                    if w3 is not None:
                        sp.dma_start(w3[:, e0:e1, :], w_in[f][2][:, e0:e1, :]).then_inc(w_loaded[f][i], 16)
                    sp.dma_start(w2[0:rows, e0:e1, :, :], w_in[f][1][:, e0:e1, :, :]).then_inc(w_loaded[f][i], 16)
            for g in range(NG):
                sp.wait_ge(last_x_done.sem, last_x_done.at(TG * (g + 1)))
                sp.dma_start(out[:, TG * g:TG * g + TG, :], X[:, TG * g:TG * g + TG, :]).then_inc(stored, 16)
            sp.wait_ge(stored, 16 * NG)

        def kv_stage(tag):
            s_psum = sem("kv_psum", {"L0x": 0, "L1x": 2, "L2x": 3, "L3x": 4}[tag])
            s_used = sem("kv_used", {"L0x": 0, "L1x": 2, "L2x": 3 * B, "L3x": 3 + 2 * B}[tag])
            ready = sem("kv_ready", {"L0x": 2 * B, "L3x": 1}.get(tag, 0))
            blocks = pc("blocks").unsqueeze(2).to_broadcast([P, HR, K])

            def spread(nc_v, st, dst, srcT, b):
                return nc_v.tensor_tensor(dst[:, b, :, :],
                                          srcT[:, b * K:b * K + K].unsqueeze(1).to_broadcast([P, HR, K]),
                                          blocks, ALU.mult)

            if tag == "L0x":
                def vector(v, st):
                    v.wait_ge(par_in_1, 16)
                    v.wait_ge(const_ready, 1)
                    for b in range(B):
                        spread(nc.vector, st, kbd[0], pc("ctxT"), b).then_inc(ready.sem, 1)
                        nc.vector.tensor_copy(vaug[0][:, b, :, 0:HD],
                                              pc("ctx", K)[:, b * D:b * D + D].rearrange("k (h d) -> k h d", h=H))\
                            .then_inc(ready.sem, 1)
                return dict(vector=vector, tensor=None, ready=ready, total=2 * B)

            if tag == "L1x":
                def tensor(pe):
                    pe.wait_ge(par_in_2, 16)
                    nc.tensor.matmul(PS[:, 7, 0:B * K], pc("L1x_wk"), pc("ctxT"), start=True, stop=True).then_inc(s_psum.sem, 1)
                    pe.wait_ge(s_used.sem, s_used.at(1))
                    for b in range(B):
                        last = nc.tensor.matmul(PS[0:K, 7, b * D:b * D + D], pc("ctxT")[:, b * K:b * K + K],
                                                pc("L1x_wv"), start=True, stop=True)
                    last.then_inc(s_psum.sem, 1)

                def vector(v, st):
                    v.wait_ge(s_psum.sem, s_psum.at(1))
                    nc.vector.tensor_scalar(k1T[:, :], PS[:, 7, 0:B * K], pc("L1x_bk"), None, ALU.add).then_inc(s_used.sem, 1)
                    v.wait_ge(s_psum.sem, s_psum.at(2))
                    nc.vector.tensor_tensor(v1[:, :, :], PS[0:K, 7, :].rearrange("k (b d) -> k b d", b=B),
                                            pc("L1x_bv", K).unsqueeze(1).to_broadcast([K, B, D]), ALU.add)\
                        .then_inc(s_used.sem, 1)
                return dict(vector=vector, tensor=tensor, ready=s_used, total=2)

            if tag == "L2x":
                def tensor(pe):
                    for i, w in enumerate(("L2x_k1", "L2x_k2")):
                        if i:
                            pe.wait_ge(s_used.sem, s_used.at(B * i))
                        nc.tensor.matmul(PS[:, 7, 0:B * K], pc(w), pc("ctxT"), start=True, stop=True).then_inc(s_psum.sem, 1)
                    pe.wait_ge(s_used.sem, s_used.at(2 * B))
                    for b in range(B):
                        last = nc.tensor.matmul(PS[0:K, 7, b * D:b * D + D], pc("ctxT")[:, b * K:b * K + K],
                                                pc("L2x_v1"), start=True, stop=True)
                    last.then_inc(s_psum.sem, 1)

                def vector(v, st):
                    for i in range(2):
                        v.wait_ge(s_psum.sem, s_psum.at(i + 1))
                        for b in range(B):
                            spread(nc.vector, st, kbd[1 + i], PS[:, 7, 0:B * K], b).then_inc(s_used.sem, 1)
                    v.wait_ge(s_psum.sem, s_psum.at(3))
                    for b in range(B):
                        nc.vector.tensor_copy(vaug[1][:, b, :, 0:HD],
                                              PS[0:K, 7, b * D:b * D + D].rearrange("k (h d) -> k h d", h=H))\
                            .then_inc(s_used.sem, 1)
                return dict(vector=vector, tensor=tensor, ready=s_used, total=3 * B)

            def tensor(pe):
                pe.wait_ge(ready.sem, ready.at(1))
                for b in range(B):
                    last = nc.tensor.transpose(PS[:, 7, b * K:b * K + K], ctxn[:, b, :], ident[0:K, 0:K])
                last.then_inc(s_psum.sem, 1)
                pe.wait_ge(s_used.sem, s_used.at(1))
                cT = k1T[:, :]
                nc.tensor.matmul(PS[:, 7, 0:B * K], pc("L3x_k"), cT, start=True, stop=True).then_inc(s_psum.sem, 1)
                pe.wait_ge(s_used.sem, s_used.at(2))
                nc.tensor.matmul(PS[:, 7, 0:B * K], pc("L3x_kr"), cT, start=True, stop=True).then_inc(s_psum.sem, 1)
                pe.wait_ge(s_used.sem, s_used.at(3))
                for b in range(B):
                    last = nc.tensor.matmul(PS[0:K, 7, b * D:b * D + D], cT[:, b * K:b * K + K], pc("L3x_v"),
                                            start=True, stop=True)
                last.then_inc(s_psum.sem, 1)

            def vector(v, st):
                for b in range(B):
                    nc.vector.bn_stats(stats[0:K, b, :], pc("ctx", K)[:, b * D:b * D + D]).then_inc(v_step, st.one())
                v.wait_ge(v_step, st.n)
                for b in range(B):
                    nc.vector.bn_aggr(mv[0:K, b, :], stats[0:K, b, :]).then_inc(v_step, st.one())
                v.wait_ge(v_step, st.n)
                nc.vector.tensor_copy(rs[0:K, 0, 0:B], mv[0:K, 0:B, 1]).then_inc(s_var.sem, 1)
                v.wait_ge(s_rstd.sem, s_rstd.at(1))
                for b in range(B):
                    nc.vector.tensor_scalar(ctxn[:, b, :], pc("ctx", K)[:, b * D:b * D + D],
                                                  mv[0:K, b, 0:1], rs[0:K, 1, b:b + 1], ALU.subtract, ALU.mult).then_inc(v_step, st.one())
                v.wait_ge(v_step, st.n)
                v.sem_inc(ready.sem, 1)
                v.wait_ge(s_psum.sem, s_psum.at(1))
                nc.vector.tensor_scalar(k1T[:, :], PS[:, 7, 0:B * K], pc("L3x_gamma"), pc("L3x_beta"),
                                        ALU.mult, ALU.add).then_inc(s_used.sem, 1)
                kw = fin[:, 0:3, :].rearrange("p a d -> p (a d)")[:, 0:B * K].rearrange("p (b k) -> p b k", b=B)
                kr = qb[:, 0:B * K].rearrange("p (b k) -> p b k", b=B)
                for i, (dst, tab) in enumerate(((kw, "cos"), (kr, "sin"))):
                    v.wait_ge(s_psum.sem, s_psum.at(2 + i))
                    nc.vector.tensor_tensor(dst, PS[:, 7, 0:B * K].rearrange("p (b k) -> p b k", b=B),
                                            pc(tab)[:, 0:K].unsqueeze(1).to_broadcast([P, B, K]), ALU.mult)\
                        .then_inc(s_used.sem, 1)
                v.wait_ge(s_used.sem, s_used.at(3))
                nc.vector.tensor_tensor(kw, kw, kr, ALU.add).then_inc(v_step, st.one())
                v.wait_ge(v_step, st.n)
                for b in range(B):
                    nc.vector.tensor_tensor(kbd[0][:, b, :, :], kw[:, b, :].unsqueeze(1).to_broadcast([P, HR, K]),
                                            blocks, ALU.mult).then_inc(s_used.sem, 1)
                v.wait_ge(s_psum.sem, s_psum.at(4))
                for b in range(B):
                    nc.vector.tensor_copy(vaug[2][:, b, :, 0:HD],
                                          PS[0:K, 7, b * D:b * D + D].rearrange("k (h d) -> k h d", h=H))\
                        .then_inc(s_used.sem, 1)

            s_var = sem("L3x_kv_variance")
            s_rstd = sem("L3x_kv_rstd")

            def pool(g, st):
                g.wait_ge(s_var.sem, s_var.at(1))
                nc.gpsimd.tensor_scalar(rs[0:K, 2, 0:B], rs[0:K, 0, 0:B], LN_EPS, None, ALU.add).then_inc(p_step, st.one())
                g.wait_ge(p_step, st.n)
                nc.gpsimd.tensor_tensor(rs[0:K, 1, 0:B], rs[0:K, 2, 0:B], mhalf[0:K, 0:B], ALU.pow).then_inc(s_rstd.sem, 1)
            return dict(vector=vector, tensor=tensor, pool=pool, ready=s_used, total=3 + 2 * B)

        def norm_stage(tag, x_ready, second=None, post=None):
            levels = 2 if second else 1
            var_ready = sem("var", levels * NG)
            rstd_ready = sem("rstd", levels * NG)
            xn_ready = sem("xn", NT)
            xT_psum = sem("xT_psum", NG)
            xT_ready = sem("xT", NG)

            def vector(v, st):
                def statistics(level, g):
                    for t in range(TG * g, TG * g + TG):
                        if level == 0:
                            x_ready(v, t)
                            src = X[:, t, :]
                        else:
                            src = xn[:, t, :]
                        if level and second == "rms":
                            nc.vector.scalar_tensor_tensor(fin[:, t % 4, :], src, 1.0, src, ALU.mult, ALU.mult,
                                                                 accum_out=mv[:, t, 1:2]).then_inc(v_step, st.one())
                        else:
                            nc.vector.bn_stats(stats[:, t, :], src).then_inc(v_step, st.one())
                    v.wait_ge(v_step, st.n)
                    if level and second == "rms":
                        nc.vector.tensor_scalar(vare[:, TG * g:TG * g + TG], mv[:, TG * g:TG * g + TG, 1], 1.0 / D,
                                                RMS_EPS, ALU.mult, ALU.add).then_inc(var_ready.sem, 1)
                        return
                    for t in range(TG * g, TG * g + TG):
                        nc.vector.bn_aggr(mv[:, t, :], stats[:, t, :]).then_inc(v_step, st.one())
                    v.wait_ge(v_step, st.n)
                    nc.vector.tensor_scalar(vare[:, TG * g:TG * g + TG], mv[:, TG * g:TG * g + TG, 1], LN_EPS, None,
                                            ALU.add).then_inc(var_ready.sem, 1)

                def apply(level, g):
                    v.wait_ge(rstd_ready.sem, rstd_ready.at(NG * level + g + 1))
                    for t in range(TG * g, TG * g + TG):
                        src = X[:, t, :] if level == 0 else xn[:, t, :]
                        dst = xn[:, t, :] if level == 0 else qa[:, t * D:t * D + D]
                        if level and second == "rms":
                            ins = nc.vector.tensor_scalar(dst, src, rstd[:, t:t + 1], None, ALU.mult)
                        else:
                            ins = nc.vector.tensor_scalar(dst, src, mv[:, t, 0:1], rstd[:, t:t + 1],
                                                          ALU.subtract, ALU.mult)
                        if level == levels - 1:
                            ins.then_inc(xn_ready.sem, 1)
                        else:
                            ins.then_inc(v_step, st.one())

                for level in range(levels):
                    if level:
                        v.wait_ge(v_step, st.n)
                    for g in range(NG + 1):
                        if g < NG:
                            statistics(level, g)
                        if g:
                            apply(level, g - 1)

            def pool(p, st):
                for n in range(levels * NG):
                    c = slice(TG * (n % NG), TG * (n % NG) + TG)
                    p.wait_ge(var_ready.sem, var_ready.at(n + 1))
                    nc.gpsimd.tensor_tensor(rstd[:, c], vare[:, c], mhalf[:, c], ALU.pow).then_inc(rstd_ready.sem, 1)

            def tensor(pe):
                for g in range(NG):
                    pe.wait_ge(xn_ready.sem, xn_ready.at(TG * (g + 1)))
                    if g >= 2:
                        pe.wait_ge(xT_ready.sem, xT_ready.at(g - 1))
                    for j in range(TG):
                        t = TG * g + j
                        src = xn[:, t, :] if levels == 1 else qa[:, t * D:t * D + D]
                        last = nc.tensor.transpose(PS[:, 4 + g % 2, j * P:j * P + P], src, ident)
                    last.then_inc(xT_psum.sem, 1)

            def scalar(a, st):
                for g in range(NG):
                    a.wait_ge(xT_psum.sem, xT_psum.at(g + 1))
                    dst = xnT[:, g * 512:g * 512 + 512]
                    if post is None:
                        ins = nc.scalar.activation(dst, PS[:, 4 + g % 2, :], ACT.Copy)
                    else:
                        ins = nc.scalar.activation(dst, PS[:, 4 + g % 2, :], ACT.Identity, scale=post[0], bias=post[1])
                    ins.then_inc(xT_ready.sem, 1)
            return dict(vector=vector, pool=pool, tensor=tensor, scalar=scalar, ready=xT_ready)

        def proj_stage(tag, xT_ready):
            ws = {"L1x": ["L1x_wq"], "L2x": ["L2x_q1", "L2x_q2"], "L3x": ["L3x_q", "L3x_qr"]}[tag]
            n = len(ws)
            q_psum = sem("q_psum", n * NG)
            q_used = sem("q_rotated" if tag == "L3x" else "q_copied", n * NG)
            q_ready = sem("q_ready", NG if tag == "L3x" else 0)

            def tensor(pe):
                for g in range(NG):
                    pe.wait_ge(xT_ready.sem, xT_ready.at(g + 1))
                    for s in range(n):
                        i = n * g + s
                        if i >= 2:
                            pe.wait_ge(q_used.sem, q_used.at(i - 1))
                        nc.tensor.matmul(PS[:, 6 + i % 2, :], pc(ws[s]), xnT[:, g * 512:g * 512 + 512],
                                         start=True, stop=True).then_inc(q_psum.sem, 1)

            if tag != "L3x":
                def scalar(a, st):
                    for i in range(n * NG):
                        g, s = i // n, i % n
                        a.wait_ge(q_psum.sem, q_psum.at(i + 1))
                        dst = (qa, qb)[s][:, g * 512:g * 512 + 512]
                        if tag == "L1x":
                            ins = nc.scalar.activation(dst, PS[:, 6 + i % 2, :], ACT.Identity, bias=pc("L1x_bq"))
                        else:
                            ins = nc.scalar.activation(dst, PS[:, 6 + i % 2, :], ACT.Copy)
                        ins.then_inc(q_used.sem, 1)
                return dict(tensor=tensor, scalar=scalar, ready=q_used, per=n)

            def vector(v, st):
                for g in range(NG):
                    c = slice(g * 512, g * 512 + 512)
                    v.wait_ge(q_psum.sem, q_psum.at(2 * g + 1))
                    nc.vector.tensor_tensor(qa[:, c], PS[:, 6, :], pc("cos"), ALU.mult).then_inc(q_used.sem, 1)
                    v.wait_ge(q_psum.sem, q_psum.at(2 * g + 2))
                    nc.vector.tensor_tensor(qb[:, c], PS[:, 7, :], pc("sin"), ALU.mult).then_inc(q_used.sem, 1)
                    v.wait_ge(q_used.sem, q_used.at(2 * g + 2))
                    nc.vector.tensor_tensor(qa[:, c], qa[:, c], qb[:, c], ALU.add).then_inc(q_ready.sem, 1)
            return dict(tensor=tensor, vector=vector, ready=q_ready, per=1)

        def attention_stage(tag, q_ready, q_per, kv, first):
            sets = 2 if tag == "L2x" else 1
            units = NT * sets
            q = [xnT] if tag == "L0x" else [qa, qb]
            keys = {"L0x": [kbd[0]], "L2x": [kbd[1], kbd[2]], "L3x": [kbd[0]]}[tag]
            vals = vaug[{"L0x": 0, "L2x": 1, "L3x": 2}[tag]]
            scale = {"L0x": float(D) ** -0.5, "L2x": float(HD) ** -0.5, "L3x": 1.0}[tag]
            scores_ready = sem("scores", units)
            scores_used = sem("scores_used", units)
            shifted = sem("shifted", units)
            exp_ready = sem("exp", units)
            pT_psum = sem("pT_psum", RG * units)
            pT_ready = sem("pT", RG * units)
            o_psum = sem("o_psum", units)
            o_used = sem("o_used", units)
            o_ready = sem("o", NT)
            oT_psum = sem("oT_psum", NT)
            oT_ready = sem("oT", NT)
            y_psum = sem("y_psum", NT)
            x_done = sem("x_done", NT)
            if tag == "L3x":
                aT_ready = sem("attT", NT)
                g_psum = sem("gate_psum", NT)
                g_in = sem("gate_in", NT)
                g_exp = sem("gate_exp", NT)
            if tag == "L2x":
                ss_ready = sem("square_sum", NT)
                rms_ready = sem("rms", NT)

            def tile_of(u):
                return u // sets

            def tensor(pe):
                def scores(u):
                    t, s = tile_of(u), u % sets
                    pe.wait_ge(q_ready.sem, q_ready.at(q_per * (t // TG + 1)))
                    if u:
                        pe.wait_ge(scores_used.sem, scores_used.at(u))
                    for r in range(RG):
                        rows = slice(32 * r, 32 * r + 32)
                        last = nc.tensor.matmul(PS[:, r, 0:HR * K], q[s][rows, t * P:t * P + P],
                                                keys[s][rows, t // TG, :, :], start=True, stop=True)
                    last.then_inc(scores_ready.sem, 1)

                def transposes(u):
                    pe.wait_ge(exp_ready.sem, exp_ready.at(u + 1))
                    for i in range(RG):
                        n = RG * u + i
                        if n >= 2:
                            pe.wait_ge(pT_ready.sem, pT_ready.at(n - 1))
                        for j in range(HR):
                            last = nc.tensor.transpose(PS[0:K, 4 + n % 2, j * P:j * P + P],
                                                       score[:, u % 2, HR * i + j, :], ident)
                        last.then_inc(pT_psum.sem, 1)

                def weighted(u):
                    t = tile_of(u)
                    if u:
                        pe.wait_ge(o_used.sem, o_used.at(u))
                    for h in range(H):
                        if h % HR == 0:
                            pe.wait_ge(pT_ready.sem, pT_ready.at(RG * u + h // HR + 1))
                        last = nc.tensor.matmul(PS[:, 6, h * (HD + 1):(h + 1) * (HD + 1)],
                                                hT[0:K, u % 2, h // HR, (h % HR) * P:(h % HR) * P + P],
                                                vals[:, t // TG, h, :], start=True, stop=True)
                    last.then_inc(o_psum.sem, 1)

                def out_transpose(t):
                    pe.wait_ge(o_ready.sem, o_ready.at(t + 1))
                    if t:
                        pe.wait_ge(x_done.sem, x_done.at(t))
                    nc.tensor.transpose(PS[:, 7, 0:P], (oc2 if tag == "L2x" else oc)[:, t % 2, :], ident)\
                        .then_inc(oT_psum.sem, 1)

                def out_project(t):
                    pe.wait_ge(oT_ready.sem, oT_ready.at(t + 1))
                    last = nc.tensor.matmul(PS[:, 7, P:2 * P], ocT[:, t % 2, :], pc(f"{tag}_wo"), start=True, stop=True)
                    if tag == "L3x":
                        last = nc.tensor.matmul(PS[:, 7, 2 * P:3 * P], pc("L3x_wo"), ocT[:, t % 2, :],
                                                start=True, stop=True)
                    last.then_inc(y_psum.sem, 1)

                def gate(t):
                    if tag == "L3x":
                        pe.wait_ge(aT_ready.sem, aT_ready.at(t + 1))
                        nc.tensor.matmul(PS[:, 7, 3 * P:4 * P], attT[:, t % 2, :], pc("L3x_wg"), start=True, stop=True)\
                            .then_inc(g_psum.sem, 1)

                pe.wait_ge(kv["ready"].sem, kv["ready"].at(kv["total"]))
                scores(0)
                for u in range(units + sets):
                    if u + 1 < units:
                        scores(u + 1)
                    late = tile_of(u - sets) if u >= sets and u % sets == 0 else None
                    if late is not None:
                        out_transpose(late)
                    if u < units:
                        transposes(u)
                    if late is not None:
                        out_project(late)
                    if u < units:
                        weighted(u)
                    if late is not None:
                        gate(late)

            def vector(v, st):
                def softmax_shift(u):
                    t = tile_of(u)
                    v.wait_ge(scores_ready.sem, scores_ready.at(u + 1))
                    dst = score[:, u % 2, :, :]
                    ps = PS[:, 0:RG, 0:HR * K].rearrange("p r (h k) -> p r h k", h=HR)
                    dst4 = dst.rearrange("p (r h) k -> p r h k", r=RG)
                    m = mx[:, u % 2, :]
                    if tag == "L2x":
                        nc.vector.tensor_reduce(m, ps, AX.X, ALU.max).then_inc(v_step, st.one())
                        v.wait_ge(v_step, st.n)
                        nc.vector.tensor_tensor(dst4, ps, m.rearrange("p (r h) -> p r h", r=RG).unsqueeze(3)
                                                .to_broadcast([P, RG, HR, K]), ALU.subtract).then_inc(scores_used.sem, 1)
                        v.wait_ge(scores_used.sem, scores_used.at(u + 1))
                        v.sem_inc(shifted.sem, 1)
                        return
                    for r in range(RG):
                        src = PS[:, r, 0:HR * K].rearrange("p (h k) -> p h k", h=HR)
                        d = dst[:, HR * r:HR * r + HR, :]
                        if tag == "L0x":
                            ins = nc.vector.tensor_tensor(d, src, bound[:, t, :].unsqueeze(1).to_broadcast([P, HR, K]),
                                                          ALU.min)
                        else:
                            tb = pc("tbias")[:, (t % TG) * K:(t % TG) * K + K].unsqueeze(1).to_broadcast([P, HR, K])
                            ins = nc.vector.scalar_tensor_tensor(d, src, float(HD) ** -0.5, tb, ALU.mult, ALU.add)
                        if r < RG - 1:
                            ins.then_inc(v_step, st.one())
                        else:
                            ins.then_inc(scores_used.sem, 1)
                    v.wait_ge(scores_used.sem, scores_used.at(u + 1))
                    nc.vector.tensor_reduce(m, dst, AX.X, ALU.max).then_inc(v_step, st.one())
                    v.wait_ge(v_step, st.n)
                    nc.vector.tensor_tensor(dst, dst, m.unsqueeze(2).to_broadcast([P, H, K]), ALU.subtract)\
                        .then_inc(shifted.sem, 1)

                def normalise(u):
                    t, s = tile_of(u), u % sets
                    v.wait_ge(o_psum.sem, o_psum.at(u + 1))
                    o = PS[:, 6, 0:H * (HD + 1)].rearrange("p (h d) -> p h d", h=H)
                    r = rec[:, u % 2, :]
                    nc.vector.reciprocal(r, o[:, :, HD]).then_inc(v_step, st.one())
                    v.wait_ge(v_step, st.n)
                    if tag == "L2x" and s:
                        nc.vector.tensor_tensor(r, r, lam[:, :], ALU.mult).then_inc(v_step, st.one())
                        v.wait_ge(v_step, st.n)
                    rb = r.unsqueeze(2).to_broadcast([P, H, HD])
                    heads = oc[:, t % 2, :].rearrange("p (h d) -> p h d", h=H)
                    if tag != "L2x":
                        nc.vector.tensor_tensor(heads, o[:, :, 0:HD], rb, ALU.mult).then_inc(o_used.sem, 1)
                        v.wait_ge(o_used.sem, o_used.at(u + 1))
                        v.sem_inc(o_ready.sem, 1)
                        return
                    if s == 0:
                        nc.vector.tensor_tensor(heads, o[:, :, 0:HD], rb, ALU.mult).then_inc(o_used.sem, 1)
                        return
                    second = fin[:, 0, :].rearrange("p (h d) -> p h d", h=H)
                    nc.vector.tensor_tensor(second, o[:, :, 0:HD], rb, ALU.mult).then_inc(o_used.sem, 1)
                    v.wait_ge(o_used.sem, o_used.at(u + 1))
                    nc.vector.tensor_tensor(oc[:, t % 2, :], oc[:, t % 2, :], fin[:, 0, :], ALU.subtract).then_inc(v_step, st.one())
                    v.wait_ge(v_step, st.n)
                    nc.vector.scalar_tensor_tensor(fin[:, 1, :], oc[:, t % 2, :], 1.0, oc[:, t % 2, :],
                                                           ALU.mult, ALU.mult, accum_out=oss[:, t % 2:t % 2 + 1]).then_inc(v_step, st.one())
                    v.wait_ge(v_step, st.n)
                    v.sem_inc(ss_ready.sem, 1)
                    v.wait_ge(rms_ready.sem, rms_ready.at(t + 1))
                    nc.vector.tensor_scalar(oc2[:, t % 2, :], oc[:, t % 2, :], osr[:, t % 2:t % 2 + 1], None, ALU.mult)\
                        .then_inc(o_ready.sem, 1)

                def evacuate_oT(t):
                    v.wait_ge(oT_psum.sem, oT_psum.at(t + 1))
                    if tag == "L2x":
                        ins = nc.vector.tensor_scalar(ocT[:, t % 2, :], PS[:, 7, 0:P], pc("L2x_norm"), None, ALU.mult)
                    else:
                        ins = nc.vector.tensor_copy(ocT[:, t % 2, :], PS[:, 7, 0:P])
                    ins.then_inc(oT_ready.sem, 1)

                def finish(t):
                    v.wait_ge(y_psum.sem, y_psum.at(t + 1))
                    y, att, xt = PS[:, 7, P:2 * P], fin[:, 2, :], X[:, t, :]
                    if tag != "L3x":
                        nc.vector.tensor_tensor(att, y, pc(f"{tag}_bo"), ALU.add).then_inc(v_step, st.one())
                        v.wait_ge(v_step, st.n)
                        nc.vector.tensor_tensor(xt, xt, att, ALU.add).then_inc(x_done.sem, 1)
                        return
                    nc.vector.tensor_tensor(att, y, pc("L3x_bo"), ALU.add).then_inc(v_step, st.one())
                    nc.vector.tensor_scalar(attT[:, t % 2, :], PS[:, 7, 2 * P:3 * P], pc("L3x_boc"), None, ALU.add)\
                        .then_inc(aT_ready.sem, 1)
                    v.wait_ge(v_step, st.n)
                    nc.vector.tensor_tensor(fin[:, 3, :], att, xn[:, t, :], ALU.subtract).then_inc(v_step, st.one())
                    nc.vector.tensor_tensor(xt, xt, xn[:, t, :], ALU.add).then_inc(v_step, st.one())
                    v.wait_ge(v_step, st.n)
                    v.wait_ge(g_psum.sem, g_psum.at(t + 1))
                    nc.vector.tensor_tensor(fin[:, 4, :], PS[:, 7, 3 * P:4 * P], pc("L3x_bg"), ALU.add)\
                        .then_inc(g_in.sem, 1)
                    v.wait_ge(g_exp.sem, g_exp.at(t + 1))
                    nc.vector.tensor_scalar(fin[:, 4, :], fin[:, 4, :], 1.0, None, ALU.add).then_inc(v_step, st.one())
                    v.wait_ge(v_step, st.n)
                    nc.vector.reciprocal(fin[:, 4, :], fin[:, 4, :]).then_inc(v_step, st.one())
                    v.wait_ge(v_step, st.n)
                    nc.vector.tensor_tensor(fin[:, 3, :], fin[:, 3, :], fin[:, 4, :], ALU.mult).then_inc(v_step, st.one())
                    v.wait_ge(v_step, st.n)
                    nc.vector.tensor_tensor(xt, xt, fin[:, 3, :], ALU.add).then_inc(x_done.sem, 1)

                if tag == "L2x":
                    nc.vector.tensor_tensor(lam[:, :], pc("L2x_lam1"), pc("L2x_lam2"), ALU.subtract).then_inc(v_step, st.one())
                    v.wait_ge(v_step, st.n)
                    nc.vector.tensor_scalar(lam[:, :], lam[:, :], 0.1, None, ALU.add).then_inc(v_step, st.one())
                    v.wait_ge(v_step, st.n)
                softmax_shift(0)
                for u in range(units + sets):
                    late = tile_of(u - sets) if u >= sets and u % sets == 0 else None
                    if late is not None:
                        evacuate_oT(late)
                    if u + 1 < units:
                        softmax_shift(u + 1)
                    if late is not None:
                        finish(late)
                    if u < units:
                        normalise(u)

            def scalar(a, st):
                def exps(u):
                    a.wait_ge(shifted.sem, shifted.at(u + 1))
                    nc.scalar.activation(score[:, u % 2, :, :], score[:, u % 2, :, :], ACT.Exp, scale=scale)\
                        .then_inc(exp_ready.sem, 1)

                exps(0)
                for u in range(units + sets):
                    if u < units:
                        for i in range(RG):
                            n = RG * u + i
                            a.wait_ge(pT_psum.sem, pT_psum.at(n + 1))
                            if i == 0 and u >= 2:
                                a.wait_ge(o_psum.sem, o_psum.at(u - 1))
                            nc.scalar.activation(hT[0:K, u % 2, i, :], PS[0:K, 4 + n % 2, :], ACT.Copy)\
                                .then_inc(pT_ready.sem, 1)
                    if u + 1 < units:
                        exps(u + 1)
                    if tag == "L3x" and u >= sets:
                        a.wait_ge(g_in.sem, g_in.at(u - sets + 1))
                        nc.scalar.activation(fin[:, 4, :], fin[:, 4, :], ACT.Exp, scale=-1.0).then_inc(g_exp.sem, 1)

            def pool(p, st):
                if tag == "L2x":
                    for t in range(NT):
                        p.wait_ge(ss_ready.sem, ss_ready.at(t + 1))
                        nc.gpsimd.tensor_scalar(oss[:, t % 2:t % 2 + 1], oss[:, t % 2:t % 2 + 1], 1.0 / D,
                                                        RMS_EPS, ALU.mult, ALU.add).then_inc(p_step, st.one())
                        p.wait_ge(p_step, st.n)
                        nc.gpsimd.tensor_tensor(osr[:, t % 2:t % 2 + 1], oss[:, t % 2:t % 2 + 1], mhalf[:, 0:1],
                                                ALU.pow).then_inc(rms_ready.sem, 1)
            return dict(tensor=tensor, vector=vector, scalar=scalar, pool=pool, x_done=x_done)

        def single_stage(tag, q_ready, kv):
            scores_ready = sem("scores", B)
            shifted = sem("shifted", B)
            exp_ready = sem("exp", B)
            pT_psum = sem("pT_psum", B)
            pT_ready = sem("pT", B)
            o_psum = sem("o_psum", B)
            x_done = sem("x_done", NT)

            def tensor(pe):
                pe.wait_ge(kv["ready"].sem, kv["ready"].at(kv["total"]))

                def scores(b):
                    pe.wait_ge(q_ready.sem, q_ready.at(b + 1))
                    if b >= 2:
                        pe.wait_ge(shifted.sem, shifted.at(b - 1))
                    for j in range(TG):
                        t = TG * b + j
                        last = nc.tensor.matmul(PS[:, b % 2, j * K:j * K + K], qa[:, t * P:t * P + P],
                                                k1T[:, b * K:b * K + K], start=True, stop=True)
                    last.then_inc(scores_ready.sem, 1)

                scores(0)
                for b in range(B):
                    if b + 1 < B:
                        scores(b + 1)
                    pe.wait_ge(exp_ready.sem, exp_ready.at(b + 1))
                    for j in range(TG):
                        last = nc.tensor.transpose(PS[0:K, 2 + b % 2, j * P:j * P + P], score[:, b % 2, j, :], ident)
                    last.then_inc(pT_psum.sem, 1)
                    pe.wait_ge(pT_ready.sem, pT_ready.at(b + 1))
                    if b >= 2:
                        pe.wait_ge(x_done.sem, x_done.at(TG * (b - 1)))
                    for j in range(TG):
                        last = nc.tensor.matmul(PS[:, 4 + b % 2, j * P:j * P + P], hT[0:K, b % 2, 0, j * P:j * P + P],
                                                v1[:, b, :], start=True, stop=True)
                    last.then_inc(o_psum.sem, 1)

            def vector(v, st):
                def shift(b):
                    v.wait_ge(scores_ready.sem, scores_ready.at(b + 1))
                    ps = PS[:, b % 2, 0:TG * K].rearrange("p (j k) -> p j k", j=TG)
                    m = mx[:, b % 2, 0:TG]
                    nc.vector.tensor_reduce(m, ps, AX.X, ALU.max).then_inc(v_step, st.one())
                    v.wait_ge(v_step, st.n)
                    nc.vector.tensor_tensor(score[:, b % 2, 0:TG, :], ps, m.unsqueeze(2).to_broadcast([P, TG, K]),
                                            ALU.subtract).then_inc(shifted.sem, 1)

                shift(0)
                for b in range(B):
                    if b + 1 < B:
                        shift(b + 1)
                    v.wait_ge(exp_ready.sem, exp_ready.at(b + 1))
                    r = rec[:, b % 2, 0:TG]
                    nc.vector.tensor_reduce(r, score[:, b % 2, 0:TG, :], AX.X, ALU.add).then_inc(v_step, st.one())
                    v.wait_ge(v_step, st.n)
                    nc.vector.reciprocal(r, r).then_inc(v_step, st.one())
                    v.wait_ge(v_step, st.n)
                    v.wait_ge(o_psum.sem, o_psum.at(b + 1))
                    for j in range(TG):
                        t = TG * b + j
                        nc.vector.scalar_tensor_tensor(X[:, t, :], PS[:, 4 + b % 2, j * P:j * P + P], r[:, j:j + 1],
                                                       X[:, t, :], ALU.mult, ALU.add).then_inc(x_done.sem, 1)

            def scalar(a, st):
                def exps(b):
                    a.wait_ge(shifted.sem, shifted.at(b + 1))
                    nc.scalar.activation(score[:, b % 2, 0:TG, :], score[:, b % 2, 0:TG, :], ACT.Exp,
                                         scale=float(D) ** -0.5).then_inc(exp_ready.sem, 1)
                exps(0)
                for b in range(B):
                    a.wait_ge(pT_psum.sem, pT_psum.at(b + 1))
                    nc.scalar.activation(hT[0:K, b % 2, 0, :], PS[0:K, 2 + b % 2, :], ACT.Copy).then_inc(pT_ready.sem, 1)
                    if b + 1 < B:
                        exps(b + 1)
            return dict(tensor=tensor, vector=vector, scalar=scalar, x_done=x_done)

        def route_stage(tag, xT_ready):
            logits_psum = sem("logits", 1)
            e_in = sem("route_in", 1)
            e_out = sem("route_exp", 1)
            w_ready = sem("w", 1)
            wT_psum = sem("wT_psum", 0 if tag == "L3f" else NG)
            wT_ready = sem("wT", 0 if tag == "L3f" else NG)
            b2_psum = sem("b2_psum", 0 if tag == "L3f" else NG)
            x_first = sem("x_first", NG)
            n_e = FFNS[tag]["experts"]
            if tag == "L2f":
                oh_ready = sem("L2f_onehots")
                count_psum = sem("L2f_counts")

            def tensor(pe):
                for t in range(NT):
                    if t % TG == 0:
                        pe.wait_ge(xT_ready.sem, xT_ready.at(t // TG + 1))
                    last = nc.tensor.matmul(PS[:, 6, t * E:t * E + E], xnT[:, t * P:t * P + P], pc(f"{tag}_wr"),
                                            start=True, stop=True)
                last.then_inc(logits_psum.sem, 1)
                if tag == "L2f":
                    pe.wait_ge(oh_ready.sem, oh_ready.at(2))
                    for i in range(2):
                        oh = rt[:, 4 + i, :, :]
                        nc.tensor.matmul(PS[:, 7, i * P:i * P + P], pc("before"), oh, start=True, stop=True)
                        last = nc.tensor.matmul(PS[:, 7, (2 + i) * P:(3 + i) * P], pc("ones"), oh, start=True, stop=True)
                    last.then_inc(count_psum.sem, 1)
                if tag == "L3f":
                    return
                pe.wait_ge(w_ready.sem, w_ready.at(1))
                for g in range(NG):
                    if g >= 2:
                        pe.wait_ge(wT_ready.sem, wT_ready.at(g - 1))
                    for j in range(TG):
                        last = nc.tensor.transpose(PS[0:n_e, 4 + g % 2, j * P:j * P + P], wts[:, TG * g + j, 0:n_e], ident)
                    last.then_inc(wT_psum.sem, 1)
                for g in range(NG):
                    pe.wait_ge(wT_ready.sem, wT_ready.at(g + 1))
                    if g >= 2:
                        pe.wait_ge(x_first.sem, x_first.at(g - 1))
                    for j in range(TG):
                        t = TG * g + j
                        last = nc.tensor.matmul(PS[:, 6 + g % 2, j * P:j * P + P], qb[0:n_e, t * P:t * P + P],
                                                pc(f"{tag}_b2", n_e), start=True, stop=True)
                    last.then_inc(b2_psum.sem, 1)

            def scalar(a, st):
                a.wait_ge(e_in.sem, e_in.at(1))
                nc.scalar.activation(rt[:, 1, :, :], rt[:, 1, :, :], ACT.Exp).then_inc(e_out.sem, 1)
                if tag == "L3f":
                    return
                for g in range(NG):
                    a.wait_ge(wT_psum.sem, wT_psum.at(g + 1))
                    nc.scalar.activation(qb[0:n_e, g * 512:g * 512 + 512], PS[0:n_e, 4 + g % 2, :], ACT.Copy)\
                        .then_inc(wT_ready.sem, 1)

            def vector(v, st):
                def over_e(a):
                    return a.unsqueeze(2).to_broadcast([P, NT, E])

                iota = pc("iota").unsqueeze(1).to_broadcast([P, NT, E])
                lg, pr, eq, key, oh1, oh2, rest, w = (rt[:, i, :, :] for i in range(8))
                m1, m2, ssum, kmin, keep, g12 = (rs[:, i, 0:NT] for i in range(6))
                v.wait_ge(logits_psum.sem, logits_psum.at(1))
                logits = PS[:, 6, 0:NT * E].rearrange("p (t e) -> p t e", e=E)
                if tag == "L3f":
                    nc.vector.tensor_copy(lg, logits).then_inc(v_step, st.one())
                    v.wait_ge(v_step, st.n)
                else:
                    nc.vector.tensor_tensor(lg, logits, pc(f"{tag}_br").unsqueeze(1).to_broadcast([P, NT, E]),
                                                    ALU.add).then_inc(v_step, st.one())
                    v.wait_ge(v_step, st.n)
                nc.vector.tensor_reduce(m1, lg, AX.X, ALU.max).then_inc(v_step, st.one())
                v.wait_ge(v_step, st.n)
                nc.vector.tensor_tensor(pr, lg, over_e(m1), ALU.subtract).then_inc(e_in.sem, 1)
                v.wait_ge(e_out.sem, e_out.at(1))

                def first_of_max(src, m, oh):
                    nc.vector.tensor_tensor(eq, src, over_e(m), ALU.is_equal).then_inc(v_step, st.one())
                    v.wait_ge(v_step, st.n)
                    nc.vector.scalar_tensor_tensor(key, eq, -1000.0, iota, ALU.mult, ALU.add).then_inc(v_step, st.one())
                    v.wait_ge(v_step, st.n)
                    nc.vector.tensor_reduce(kmin, key, AX.X, ALU.min).then_inc(v_step, st.one())
                    v.wait_ge(v_step, st.n)
                    return nc.vector.tensor_tensor(oh, key, over_e(kmin), ALU.is_equal)

                wv = wts[:, :, 0:E]
                if tag == "L0f":
                    first_of_max(lg, m1, oh1).then_inc(v_step, st.one())
                    v.wait_ge(v_step, st.n)
                    nc.vector.scalar_tensor_tensor(rest, oh1, -3.0e38, lg, ALU.mult, ALU.add).then_inc(v_step, st.one())
                    v.wait_ge(v_step, st.n)
                    nc.vector.tensor_reduce(m2, rest, AX.X, ALU.max).then_inc(v_step, st.one())
                    v.wait_ge(v_step, st.n)
                    nc.vector.tensor_tensor(eq, lg, over_e(m2), ALU.is_ge).then_inc(v_step, st.one())
                    v.wait_ge(v_step, st.n)
                    nc.vector.tensor_tensor(w, pr, eq, ALU.mult).then_inc(v_step, st.one())
                    v.wait_ge(v_step, st.n)
                    nc.vector.tensor_reduce(ssum, w, AX.X, ALU.add).then_inc(v_step, st.one())
                    v.wait_ge(v_step, st.n)
                    nc.vector.reciprocal(ssum, ssum).then_inc(v_step, st.one())
                    v.wait_ge(v_step, st.n)
                    nc.vector.tensor_tensor(wv, w, over_e(ssum), ALU.mult).then_inc(w_ready.sem, 1)
                else:
                    nc.vector.tensor_reduce(ssum, pr, AX.X, ALU.add).then_inc(v_step, st.one())
                    v.wait_ge(v_step, st.n)
                    nc.vector.reciprocal(ssum, ssum).then_inc(v_step, st.one())
                    v.wait_ge(v_step, st.n)
                    nc.vector.tensor_tensor(pr, pr, over_e(ssum), ALU.mult).then_inc(v_step, st.one())
                    v.wait_ge(v_step, st.n)
                    nc.vector.tensor_reduce(m1, pr, AX.X, ALU.max).then_inc(v_step, st.one())
                    v.wait_ge(v_step, st.n)
                    if tag == "L2f":
                        first_of_max(pr, m1, oh1).then_inc(oh_ready.sem, 1)
                        v.wait_ge(oh_ready.sem, oh_ready.at(1))
                    else:
                        first_of_max(pr, m1, oh1).then_inc(v_step, st.one())
                        v.wait_ge(v_step, st.n)
                    nc.vector.scalar_tensor_tensor(rest, oh1, -3.0, pr, ALU.mult, ALU.add).then_inc(v_step, st.one())
                    v.wait_ge(v_step, st.n)
                    nc.vector.tensor_reduce(m2, rest, AX.X, ALU.max).then_inc(v_step, st.one())
                    v.wait_ge(v_step, st.n)
                    if tag == "L2f":
                        first_of_max(rest, m2, oh2).then_inc(oh_ready.sem, 1)
                        v.wait_ge(oh_ready.sem, oh_ready.at(2))
                    else:
                        first_of_max(rest, m2, oh2).then_inc(v_step, st.one())
                        v.wait_ge(v_step, st.n)
                    if tag != "L1f":
                        nc.vector.tensor_tensor(g12, m1, m2, ALU.add).then_inc(v_step, st.one())
                        v.wait_ge(v_step, st.n)
                        nc.vector.reciprocal(g12, g12).then_inc(v_step, st.one())
                        v.wait_ge(v_step, st.n)
                    if tag == "L2f":
                        v.wait_ge(count_psum.sem, count_psum.at(1))
                        before = PS[:, 7, 0:2 * P].rearrange("p (t e) -> p t e", e=E)
                        nc.vector.memset(rc[:, 0, 0, :], 0.0).then_inc(v_step, st.one())
                        nc.vector.tensor_copy(rc[:, 0, 1:2 * NT, :],
                                                      PS[:, 7, 2 * P:4 * P].rearrange("p (t e) -> p t e", e=E)[:, 0:2 * NT - 1, :]).then_inc(v_step, st.one())
                        v.wait_ge(v_step, st.n)
                        side, step = 0, 1
                        while step < 2 * NT:
                            a, b = rc[:, side, :, :], rc[:, 1 - side, :, :]
                            nc.vector.tensor_copy(b[:, 0:step, :], a[:, 0:step, :]).then_inc(v_step, st.one())
                            nc.vector.tensor_tensor(b[:, step:, :], a[:, step:, :], a[:, 0:2 * NT - step, :], ALU.add).then_inc(v_step, st.one())
                            v.wait_ge(v_step, st.n)
                            side, step = 1 - side, 2 * step
                        pos, work = rc[:, side, :, :], rc[:, 1 - side, :, :]
                        nc.vector.tensor_tensor(work, pos, before, ALU.add).then_inc(v_step, st.one())
                        v.wait_ge(v_step, st.n)
                        oh12 = rt[:, 4:6, :, :].rearrange("p a t e -> p (a t) e")
                        nc.vector.tensor_tensor(pos, work, oh12, ALU.mult).then_inc(v_step, st.one())
                        v.wait_ge(v_step, st.n)
                        both = rs[:, 4, :]
                        nc.vector.tensor_reduce(both, pos, AX.X, ALU.add).then_inc(v_step, st.one())
                        v.wait_ge(v_step, st.n)
                        nc.vector.tensor_scalar(both, both, float(CAPACITY), None, ALU.is_lt).then_inc(v_step, st.one())
                        v.wait_ge(v_step, st.n)
                        nc.vector.tensor_tensor(work, oh12, both.unsqueeze(2).to_broadcast([P, 2 * NT, E]), ALU.mult).then_inc(v_step, st.one())
                        v.wait_ge(v_step, st.n)
                        nc.vector.tensor_tensor(eq, work[:, 0:NT, :], work[:, NT:2 * NT, :], ALU.add).then_inc(v_step, st.one())
                        v.wait_ge(v_step, st.n)
                    else:
                        nc.vector.tensor_tensor(eq, oh1, oh2, ALU.add).then_inc(v_step, st.one())
                        v.wait_ge(v_step, st.n)
                    if tag == "L1f":
                        nc.vector.memset(wts[:, :, E:E + 1], 1.0).then_inc(v_step, st.one())
                        nc.vector.tensor_tensor(wv, pr, eq, ALU.mult).then_inc(w_ready.sem, 1)
                    else:
                        nc.vector.tensor_tensor(w, pr, eq, ALU.mult).then_inc(v_step, st.one())
                        v.wait_ge(v_step, st.n)
                        nc.vector.tensor_tensor(wv, w, over_e(g12), ALU.mult).then_inc(w_ready.sem, 1)
                for g in range(NG):
                    xs = X[:, TG * g:TG * g + TG, :]
                    if tag == "L3f":
                        other = xn[:, TG * g:TG * g + TG, :]
                    else:
                        v.wait_ge(b2_psum.sem, b2_psum.at(g + 1))
                        other = PS[:, 6 + g % 2, :].rearrange("p (t d) -> p t d", d=D)
                    nc.vector.tensor_tensor(xs, xs, other, ALU.add).then_inc(x_first.sem, 1)
            return dict(tensor=tensor, vector=vector, scalar=scalar, w_ready=w_ready, x_first=x_first)

        def ffn_stage(tag, x_first, w_ready):
            c = FFNS[tag]
            n_e, chunks, rows, gated = c["experts"], c["chunks"], c["rows"], c["gated"]
            w1, w3, w2 = views(tag)
            steps = n_e * NG
            h_psum = sem("h_psum", steps * chunks)
            h_ready = sem("h_gated" if gated else "h", steps * chunks)
            y_psum = sem("y_psum", steps)
            y_used = sem("y_used", TG * steps)
            if gated:
                s_ready = sem("silu", steps * chunks)

            def tensor(pe):
                def hidden(n):
                    e, g = n // NG, n % NG
                    if g == 0:
                        pe.wait_ge(w_loaded[tag][w_third(tag, e)], 48 if gated else 32)
                    for k in range(chunks):
                        i = n * chunks + k
                        moving = xnT[:, g * 512:g * 512 + 512]
                        if gated:
                            if i >= 2:
                                pe.wait_ge(h_ready.sem, h_ready.at(i - 1))
                            nc.tensor.matmul(PS[0:rows, i % 2, :], w1[:, e, k * rows:(k + 1) * rows], moving,
                                             start=True, stop=True)
                            nc.tensor.matmul(PS[0:rows, 2 + i % 2, :], w3[:, e, k * rows:(k + 1) * rows], moving,
                                             start=True, stop=True).then_inc(h_psum.sem, 1)
                        else:
                            if i >= 4:
                                pe.wait_ge(h_ready.sem, h_ready.at(i - 3))
                            nc.tensor.matmul(PS[0:rows, i % 4, :], w1[:, e, k * rows:(k + 1) * rows], moving,
                                             start=True, stop=True).then_inc(h_psum.sem, 1)

                def output(n):
                    e = n // NG
                    if n >= 2:
                        pe.wait_ge(y_used.sem, y_used.at(TG * (n - 1)))
                    pe.wait_ge(h_ready.sem, h_ready.at(chunks * (n + 1)))
                    for j in range(TG):
                        for k in range(chunks):
                            last = nc.tensor.matmul(PS[:, 6 + n % 2, j * P:j * P + P],
                                                    hT[0:rows, n % 2, k, j * P:j * P + P], w2[0:rows, e, k, :],
                                                    start=k == 0, stop=k == chunks - 1)
                    last.then_inc(y_psum.sem, 1)

                pe.wait_ge(x_first.sem, x_first.at(NG))
                hidden(0)
                for n in range(steps):
                    if n + 1 < steps:
                        hidden(n + 1)
                    output(n)
                if tag in w_done:
                    pe.wait_ge(y_used.sem, y_used.at(TG * steps))
                    pe.sem_inc(w_done[tag], 1)

            def scalar(a, st):
                for i in range(steps * chunks):
                    n, k = i // chunks, i % chunks
                    a.wait_ge(h_psum.sem, h_psum.at(i + 1))
                    if gated:
                        if i >= 2:
                            a.wait_ge(h_ready.sem, h_ready.at(i - 1))
                        nc.scalar.activation(gact[0:rows, i % 2, :], PS[0:rows, i % 2, :], c["act"]).then_inc(s_ready.sem, 1)
                    else:
                        if k == 0 and n >= 2:
                            a.wait_ge(y_psum.sem, y_psum.at(n - 1))
                        col = (n // NG) * chunks + k
                        nc.scalar.activation(hT[:, n % 2, k, :], PS[:, i % 4, :], c["act"],
                                             bias=pc(f"{tag}_b1")[:, col:col + 1]).then_inc(h_ready.sem, 1)

            def vector(v, st):
                def gate(n):
                    for k in range(chunks):
                        i = n * chunks + k
                        v.wait_ge(s_ready.sem, s_ready.at(i + 1))
                        if k == 0 and n >= 2:
                            v.wait_ge(y_psum.sem, y_psum.at(n - 1))
                        nc.vector.tensor_tensor(hT[0:rows, n % 2, k, :], gact[0:rows, i % 2, :], PS[0:rows, 2 + i % 2, :],
                                                ALU.mult).then_inc(h_ready.sem, 1)

                v.wait_ge(x_first.sem, x_first.at(NG))
                v.wait_ge(w_ready.sem, w_ready.at(1))
                if gated:
                    gate(0)
                for n in range(steps):
                    e, g = n // NG, n % NG
                    if gated and n + 1 < steps:
                        gate(n + 1)
                    v.wait_ge(y_psum.sem, y_psum.at(n + 1))
                    for j in range(TG):
                        t = TG * g + j
                        if n >= NG:
                            v.wait_ge(y_used.sem, y_used.at(TG * (n - NG) + j + 1))
                        nc.vector.scalar_tensor_tensor(X[:, t, :], PS[:, 6 + n % 2, j * P:j * P + P],
                                                       wts[:, t, e:e + 1], X[:, t, :], ALU.mult, ALU.add)\
                            .then_inc(y_used.sem, 1)
            return dict(tensor=tensor, vector=vector, scalar=scalar, x_done=y_used, base=TG * NG * (n_e - 1))

        stages = []

        def constants_vector(v, st):
            for i in range(3):
                nc.vector.memset(vaug[i][:, :, :, HD:HD + 1], 1.0).then_inc(v_step, st.one())
            nc.vector.memset(mhalf[:, :], -0.5).then_inc(v_step, st.one())
            v.wait_ge(v_step, st.n)
            v.sem_inc(const_ready, 1)
            v.wait_ge(mask_loaded, 16)
            m = qb[:, 0:NT * K].bitcast(I32).rearrange("p (t k) -> p t k", t=NT)
            nc.vector.tensor_scalar(bound[:, :, :], m, 0, 3.0e38, ALU.not_equal, ALU.mult).then_inc(v_step, st.one())
            v.wait_ge(v_step, st.n)
            nc.vector.tensor_scalar(bound[:, :, :], bound[:, :, :], NEG, None, ALU.add).then_inc(v_step, st.one())
            v.wait_ge(v_step, st.n)

        def constants_pool(p, st):
            p.wait_ge(const_ready, 1)

        stages.append(dict(vector=constants_vector, pool=constants_pool))
        def loaded(v, t):
            if t % TG == 0:
                v.wait_ge(x_loaded[t // TG], 16)

        def tensor_start(pe):
            pe.wait_ge(par_in_1, 16)
        stages.append(dict(tensor=tensor_start))

        def after(sm, base=0):
            def x_is_ready(v, t):
                v.wait_ge(sm.sem, sm.at(base + t + 1))
            return x_is_ready

        def add(st):
            stages.append({k: st.get(k) for k in ("tensor", "vector", "scalar", "pool")})
            return st

        x_ready = loaded
        for layer in range(4):
            tag = f"L{layer}x"
            kv = add(kv_stage(tag))
            post = (pc("L3x_gamma"), pc("L3x_beta")) if layer == 3 else None
            if layer == 3:
                nm = add(norm_stage(tag, x_ready, "ln", post))
            else:
                nm = add(norm_stage(tag, x_ready))
            if layer == 0:
                at = add(attention_stage(tag, nm["ready"], 1, kv, True))
            else:
                pj = add(proj_stage(tag, nm["ready"]))
                at = add(single_stage(tag, pj["ready"], kv) if layer == 1 else
                         attention_stage(tag, pj["ready"], pj["per"], kv, False))
            x_ready = after(at["x_done"])
            tag = f"L{layer}f"
            if layer == 3:
                nm = add(norm_stage(tag, x_ready, "rms", (pc("L3f_rms"), 0.0)))
            else:
                nm = add(norm_stage(tag, x_ready))
            ro = add(route_stage(tag, nm["ready"]))
            ff = add(ffn_stage(tag, ro["x_first"], ro["w_ready"]))
            x_ready = after(ff["x_done"], ff["base"])
        final = sem("x_final", NT)

        block = ctx.enter_context(nc.Block())

        @block.sync
        def _(sp):
            sync_program(sp, final)

        @block.tensor
        def _(pe):
            for s in stages:
                if s.get("tensor"):
                    s["tensor"](pe)

        @block.vector
        def _(v):
            st = Steps()
            for s in stages:
                if s.get("vector"):
                    s["vector"](v, st)
            for t in range(NT):
                x_ready(v, t)
                v.sem_inc(final.sem, 1)

        @block.scalar
        def _(a):
            st = Steps()
            a.wait_ge(par_in_2, 16)
            for s in stages:
                if s.get("scalar"):
                    s["scalar"](a, st)

        @block.gpsimd
        def _(p):
            st = Steps()
            for s in stages:
                if s.get("pool"):
                    s["pool"](p, st)


def bilinear(n_in, n_out):
    scale = n_out / n_in
    inv = 1.0 / scale
    kernel_scale = max(inv, 1.0)
    at = (np.arange(n_out, dtype=np.float64) + 0.5) * inv - 0.5
    x = np.abs(at[None, :] - np.arange(n_in, dtype=np.float64)[:, None]) / kernel_scale
    w = np.maximum(0.0, 1.0 - x)
    total = w.sum(axis=0, keepdims=True)
    w = np.where(np.abs(total) > 1000.0 * np.finfo(np.float32).eps, w / np.where(total != 0, total, 1), 0)
    inside = (at >= -0.5) & (at <= n_in - 0.5)
    return np.where(inside[None, :], w, 0.0)


def tables():
    pos = np.arange(128, dtype=np.float64)
    dist = np.abs(pos[None, :] - pos[:, None])
    bias = np.exp(-dist * 0.1) - dist * 0.05
    tb = bilinear(128, S).T @ bias @ bilinear(128, K)
    tb = tb.reshape(TG, P, K).transpose(1, 0, 2).reshape(P, TG * K).astype(np.float32)
    half = HD // 2
    inv = (1.0 / np.float32(10000.0) ** (np.arange(0, HD, 2, dtype=np.float32) / np.float32(HD))).astype(np.float32)
    ang = (np.arange(S, dtype=np.float32)[:, None] * inv[None, :]).astype(np.float32).astype(np.float64)
    d = np.arange(P) % HD
    cos = np.cos(ang)[:, d % half].T
    sin = np.sin(ang)[:, d % half].T * np.where(d < half, -1.0, 1.0)[:, None]
    blocks = ((np.arange(P)[:, None] % 32) // HD == np.arange(HR)[None, :])
    before = np.arange(P)[:, None] < np.arange(P)[None, :]
    return dict(ident=np.eye(P), blocks=blocks, before=before, ones=np.ones((P, P)), cos=cos, sin=sin, tbias=tb,
                iota=np.tile(np.arange(E), (P, 1)))


def rotated_rows(w):
    return np.concatenate([w.reshape(H, 2, HD // 2, D)[:, 1:2], w.reshape(H, 2, HD // 2, D)[:, 0:1]], axis=1).reshape(D, D)


def kernel(**inp):
    import concourse.bacc as bacc
    from concourse.bass_utils import run_bass_kernel_spmd

    a = {k: np.asarray(v) for k, v in inp.items()}

    def row(v):
        return np.broadcast_to(v.reshape(1, -1), (P, v.size))

    def col(v):
        return v.reshape(-1, 1)

    def chunks(b, n):
        return b.reshape(b.shape[0], n, P).transpose(2, 0, 1).reshape(P, -1)

    ctx = a["ctx_1024"]
    kv1, kv2, qkv = a["L2_xattn_kv1_w"], a["L2_xattn_kv2_w"], a["L3_xattn_Wqkv"]
    L1b1 = np.concatenate([a["L1_ffn_rb1"], a["L1_ffn_sb1"][None]], 0)
    L1b2 = np.concatenate([a["L1_ffn_rb2"], a["L1_ffn_sb2"][None]], 0)
    p = dict(tables())
    p.update(
        ctxT=ctx.transpose(2, 0, 1).reshape(D, B * K), ctx=ctx.transpose(1, 0, 2).reshape(K, B * D),
        L0x_wo=a["L0_xattn_W_out"].T, L0x_bo=row(a["L0_xattn_b_out"]),
        L0f_wr=a["L0_ffn_Wr"], L0f_br=row(a["L0_ffn_br"]), L0f_b1=chunks(a["L0_ffn_b1"], 4), L0f_b2=a["L0_ffn_b2"],
        L1x_wq=a["L1_xattn_W_q"], L1x_wk=a["L1_xattn_W_k"], L1x_wv=a["L1_xattn_W_v"],
        L1x_bq=col(a["L1_xattn_b_q"]), L1x_bk=col(a["L1_xattn_b_k"]), L1x_bv=row(a["L1_xattn_b_v"]),
        L1f_wr=a["L1_ffn_router_w"], L1f_br=row(a["L1_ffn_router_b"]), L1f_b1=chunks(L1b1, 2), L1f_b2=L1b2,
        L2x_q1=a["L2_xattn_q1_w"].T, L2x_q2=a["L2_xattn_q2_w"].T, L2x_k1=kv1[:D].T, L2x_v1=kv1[D:].T,
        L2x_k2=kv2[:D].T, L2x_wo=a["L2_xattn_proj_w"].T, L2x_bo=row(a["L2_xattn_proj_b"]),
        L2x_norm=col(a["L2_xattn_norm_w"]), L2x_lam1=row(a["L2_xattn_lambda_1"]), L2x_lam2=row(a["L2_xattn_lambda_2"]),
        L2f_wr=a["L2_ffn_Wg"], L2f_br=row(a["L2_ffn_bg"]), L2f_b1=chunks(a["L2_ffn_b1"], 4), L2f_b2=a["L2_ffn_b2"],
        L3x_q=qkv[:D].T, L3x_qr=rotated_rows(qkv[:D]).T, L3x_k=qkv[D:2 * D].T, L3x_kr=rotated_rows(qkv[D:2 * D]).T,
        L3x_v=qkv[2 * D:].T, L3x_wo=a["L3_xattn_Wout"].T, L3x_bo=row(a["L3_xattn_b_out"]),
        L3x_boc=col(a["L3_xattn_b_out"]), L3x_wg=a["L3_xattn_Wgate"].T, L3x_bg=row(a["L3_xattn_b_gate"]),
        L3x_gamma=col(a["L3_xattn_gamma"]), L3x_beta=col(a["L3_xattn_beta"]),
        L3f_rms=col(a["L3_ffn_rms_weight"]), L3f_wr=a["L3_ffn_gate_w"].T,
    )
    pack = np.zeros((P, NPAR), np.float32)
    for name, (at, n) in COLUMN.items():
        v = np.asarray(p[name], np.float32)
        pack[:v.shape[0], at:at + n] = v

    def first(w):
        return np.ascontiguousarray(w.transpose(1, 0, 2))

    def second(w, n):
        e, h, d = w.shape
        return np.ascontiguousarray(w.reshape(e, n, h // n, d).transpose(2, 0, 1, 3))

    w = {
        "L0f": [first(a["L0_ffn_W1"]), second(a["L0_ffn_W2"], 4)],
        "L1f": [first(np.concatenate([a["L1_ffn_rw1"], a["L1_ffn_sw1"][None]], 0)),
                second(np.concatenate([a["L1_ffn_rw2"], a["L1_ffn_sw2"][None]], 0), 2)],
        "L2f": [first(a["L2_ffn_W1"]), second(a["L2_ffn_W2"], 4)],
        "L3f": [first(a["L3_ffn_w1"].transpose(0, 2, 1)), second(a["L3_ffn_w2"].transpose(0, 2, 1), 4),
                first(a["L3_ffn_w3"].transpose(0, 2, 1))],
    }
    arrays = {
        "x_tiles": np.ascontiguousarray(a["x"].reshape(NT, P, D).transpose(1, 0, 2)),
        "params": pack,
        "mask": np.ascontiguousarray(a["mask_Bx1xSxS2_if1"].reshape(NT, P, K).transpose(1, 0, 2).reshape(P, NT * K)),
    }
    for f, ws in w.items():
        for i, m in enumerate(ws):
            arrays[f"{f}_w{i}"] = m

    nc = bacc.Bacc("TRN2", target_bir_lowering=False, num_devices=1)
    aps = {k: nc.dram_tensor(k, v.shape, mybir.dt.from_np(v.dtype), kind="ExternalInput").ap() for k, v in arrays.items()}
    out = nc.dram_tensor("x_out", (P, NT, D), F32, kind="ExternalOutput").ap()
    build(nc, aps["x_tiles"], aps["params"], aps["mask"],
          {f: [aps[f"{f}_w{i}"] for i in range(len(ws))] for f, ws in w.items()}, out)
    r = run_bass_kernel_spmd(nc, [arrays], core_ids=[0])
    got = r.results[0]["x_out"]
    return np.ascontiguousarray(got.reshape(P, NT, D).transpose(1, 0, 2)).reshape(B, S, D)
```

```python
from contextlib import ExitStack

import numpy as np

import concourse.bass as bass
from concourse import mybir

F32 = mybir.dt.float32
F32R = mybir.dt.float32r
I32 = mybir.dt.int32
ALU = mybir.AluOpType
ACT = mybir.ActivationFunctionType
AX = mybir.AxisListType

P = 128
B, S, K, D = 4, 512, 77, 128
NT = B * S // P
TG = S // P
NG = NT // TG
H, HD = 16, D // 16
RG, HR = 4, 4
E = 8
LN_EPS = 1e-5
RMS_EPS = 1e-6
CAPACITY = 615
NEG = -1.0e20

NBLK = -(-H * K // P)
BLOCKS = []
for _j in range(NBLK):
    _n = min(P, H * K - _j * P)
    _h = _j * P // K
    BLOCKS.append((_h, (_j * P + _n - 1) // K - _h + 1, _n))
VW = HD + 1
NHM = 3 * (NBLK - 1) + BLOCKS[-1][1]

PARAMS = [
    ("ident", 128), ("heads", H), ("hmask", NHM), ("wrap", K + P), ("ctxT", B * K), ("ctx", B * D), ("L0x_wo", D), ("L0x_bo", D),
    ("iota", E), ("L0f_wr", E), ("L0f_br", E), ("L0f_b1", 32), ("L0f_b2", D),
    ("L1x_wq", D), ("L1x_wk", D), ("L1x_wv", D), ("L1x_bq", 1), ("L1x_bk", 1), ("L1x_bv", D),
    ("L1f_wr", E), ("L1f_br", E), ("L1f_b1", 18), ("L1f_b2", D),
    ("L2x_q1", D), ("L2x_q2", D), ("L2x_k1", D), ("L2x_v1", D), ("L2x_k2", D), ("L2x_wo", D),
    ("L2x_bo", D), ("L2x_norm", 1), ("L2x_lam1", H), ("L2x_lam2", H),
    ("L2f_wr", E), ("L2f_br", E), ("L2f_b1", 32), ("L2f_b2", D), ("before", P), ("ones", P),
    ("L3x_q", D), ("L3x_qr", D), ("L3x_k", D), ("L3x_kr", D), ("L3x_v", D), ("L3x_wo", D),
    ("L3x_bo", D), ("L3x_boc", 1), ("L3x_wg", D), ("L3x_bg", D), ("L3x_gamma", 1), ("L3x_beta", 1),
    ("headsc", H), ("cos", S), ("sin", S), ("tbias", TG * K), ("L3f_rms", 1), ("L3f_wr", E),
]
COLUMN = {}
_at = 0
for _name, _n in PARAMS:
    COLUMN[_name] = (_at, _n)
    _at += _n
NPAR = _at
NPAR_FIRST = COLUMN["iota"][0]

FFNS = {
    "L0f": dict(experts=8, chunks=4, rows=128, gated=False, act=ACT.Gelu),
    "L1f": dict(experts=9, chunks=2, rows=128, gated=False, act=ACT.Gelu),
    "L2f": dict(experts=8, chunks=4, rows=128, gated=False, act=ACT.Gelu_apprx_tanh),
    "L3f": dict(experts=8, chunks=4, rows=112, gated=True, act=ACT.Silu),
}


def build(nc, x_in, par_in, mask_in, w_in, out):
    ctx = ExitStack()

    def sb(name, shape, dt=F32):
        return ctx.enter_context(nc.sbuf_tensor(name, shape, dt))

    def under(name, widths, skip=()):
        with ExitStack() as freed:
            tensors = []
            for i, n in enumerate(widths):
                if i < len(skip) and skip[i]:
                    freed.enter_context(nc.sbuf_tensor(f"{name}_skip{i}", [P, skip[i]], F32))
                tensors.append(freed.enter_context(nc.sbuf_tensor(f"{name}{i}", [P, n], F32R)))
            return tensors

    def plain_sem(name):
        return ctx.enter_context(nc.semaphore(name))

    roles = {}

    class Signal:
        def __init__(self, role, total):
            sm, base = roles.get(role) or (ctx.enter_context(nc.semaphore(role)), 0)
            self.sem, self.base, self.total = sm, base, total
            roles[role] = (sm, base + total)

        def at(self, n):
            return self.base + n

    def sem(name, total=1):
        return Signal(name, total)


    with ctx:
        X = sb("X", [P, NT, D])
        xn = sb("xn", [P, NT, D])
        x_low = under("x_low", [NT * P])[0]
        xnT = sb("xnT", [P, NT * P])
        x_up = under("x_up", [NT * P])[0]
        qa = sb("qa", [P, NT * P])
        qb = sb("qb", [P, NT * P])
        par = sb("par", [P, NPAR])
        score = sb("score", [P, 3, H, K])
        hT = sb("hT", [P, 2, 4, 512])
        gact = score[:, 0, :, :].rearrange("p h k -> p (h k)")[:, 0:1024].rearrange("p (a n) -> p a n", a=2)
        w_halves_3, x_up_3 = under("gated", [8 * 4 * 112, NT * P], skip=[0, 4 * H * K - 8 * 4 * 112])
        regA = sb("regA", [P, 8192])
        w_halves = under("w_halves", [4 * 512], skip=[4096 + 4 * H * K])[0]
        regB = sb("regB", [P, 11264])
        kb_of = {f"L{i}x": reg[:, at:at + 4 * H * K].rearrange("p (s b h k) -> p s b h k", s=2, b=2, h=H)
                 for i, reg, at in ((0, regB, 4096), (2, regB, 4096), (3, regA, 0))}
        vaug = sb("vaug", [K, B, H + 1, VW])
        vblk = sb("vblk", [P, B, NHM * VW])
        vfull = sb("vfull", [P, B, H * VW])
        k1T = sb("k1T", [P, B * K])
        k2T = sb("k2T", [P, B * K])
        v1 = sb("v1", [K, B, D])
        bound = regB[:, 0:NT * K].rearrange("p (t k) -> p t k", t=NT)
        stats = sb("stats", [P, NT, 6])
        mv = sb("mv", [P, NT, 2])
        rstd = sb("rstd", [P, NT])
        vare = sb("vare", [P, NT])
        mhalf = sb("mhalf", [P, NT])
        mx = sb("mx", [P, 3, H])
        rec = sb("rec", [P, 2, H])
        lam = sb("lam", [P, H])
        oc = sb("oc", [P, 2, D])
        oc2 = sb("oc2", [P, 2, D])
        oss = sb("oss", [P, 2])
        osr = sb("osr", [P, 2])
        ocT = sb("ocT", [P, 2, P])
        attT = sb("attT", [P, 2, P])
        fin = sb("fin", [P, 5, D])
        gin = sb("gin", [P, 2, D])
        gdiff = sb("gdiff", [P, 2, D])
        hflat = hT[:, 0, :, :].rearrange("p c n -> p (c n)")
        rt = hflat[:, 0:8 * NT * E].rearrange("p (a t e) -> p a t e", a=8, t=NT)
        rc = hflat[:, 8 * NT * E:12 * NT * E].rearrange("p (a t e) -> p a t e", a=2, t=2 * NT)
        rs = sb("rs", [P, 6, 2 * NT])
        wts = sb("wts", [P, NT, 9])
        ctxn = score[0:K, 0, :, :].rearrange("p h k -> p (h k)")[:, 0:B * D].rearrange("p (b d) -> p b d", b=B)
        PS = ctx.enter_context(nc.psum_tensor("PS", [P, 8, 512], F32))

        def pc(name, rows=P):
            at, n = COLUMN[name]
            return par[0:rows, at:at + n]

        ident = pc("ident")

        par_in_1 = plain_sem("par_first_loaded")
        par_in_2 = plain_sem("par_rest_loaded")
        x_loaded = [plain_sem(f"x_loaded{g}") for g in range(NG)]
        mask_loaded = plain_sem("mask_loaded")
        w_loaded = {f: [plain_sem(f"{f}_w_loaded{i}") for i in range(3)] for f in FFNS}
        w_done = {f: plain_sem(f"{f}_experts_done") for f in ("L0f", "L2f")}
        stored = plain_sem("stored")
        v_step = plain_sem("vector_step")
        p_step = plain_sem("pool_step")
        a_step = plain_sem("scalar_step")
        const_ready = plain_sem("const_ready")

        class Steps:
            def __init__(self):
                self.n = 0

            def one(self):
                self.n += 1
                return 1

        def w_third(f, e):
            return min(2, e * 3 // FFNS[f]["experts"])

        def third(f, i):
            n = FFNS[f]["experts"]
            es = [e for e in range(n) if w_third(f, e) == i]
            return es[0], es[-1] + 1

        def views(f):
            c = FFNS[f]
            reg = {"L0f": regA, "L1f": regB, "L2f": regA, "L3f": regB}[f]
            n, hid = c["experts"], c["chunks"] * c["rows"]
            a = n * hid
            w1 = reg[:, 0:a].rearrange("p (e h) -> p e h", e=n)
            w3 = reg[:, a:2 * a].rearrange("p (e h) -> p e h", e=n) if c["gated"] else None
            o = 2 * a if c["gated"] else a
            w2 = reg[:, o:o + n * c["chunks"] * D].rearrange("p (e c d) -> p e c d", e=n, c=c["chunks"])
            return w1, w3, w2

        def split_space(f):
            hid = FFNS[f]["chunks"] * FFNS[f]["rows"]
            if f == "L3f":
                return x_up_3, w_halves_3[:, :].rearrange("p (b m u h) -> p b m u h", b=2, m=2, u=2)
            return x_up, w_halves[:, 0:4 * hid].rearrange("p (b m u h) -> p b m u h", b=2, m=1, u=2)

        def sync_program(sp, last_x_done, x_dones):
            sp.dma_start(par[:, 0:NPAR_FIRST], par_in[:, 0:NPAR_FIRST]).then_inc(par_in_1, 16)
            for g in range(NG):
                sp.dma_start(X[:, TG * g:TG * g + TG, :], x_in[:, TG * g:TG * g + TG, :]).then_inc(x_loaded[g], 16)
            sp.dma_start(qb[:, 0:NT * K].bitcast(I32), mask_in).then_inc(mask_loaded, 16)
            sp.dma_start(par[:, NPAR_FIRST:NPAR], par_in[:, NPAR_FIRST:NPAR]).then_inc(par_in_2, 16)
            for f in ("L0f", "L1f", "L2f", "L3f"):
                if f == "L1f":
                    sp.wait_ge(x_dones[0].sem, x_dones[0].at(NT))
                if f == "L2f":
                    sp.wait_ge(w_done["L0f"], 1)
                if f == "L3f":
                    sp.wait_ge(w_done["L2f"], 1)
                w1, w3, w2 = views(f)
                rows = FFNS[f]["rows"]
                for i in range(3):
                    e0, e1 = third(f, i)
                    sp.dma_start(w1[:, e0:e1, :], w_in[f][0][:, e0:e1, :]).then_inc(w_loaded[f][i], 16)
                    if w3 is not None:
                        sp.dma_start(w3[:, e0:e1, :], w_in[f][2][:, e0:e1, :]).then_inc(w_loaded[f][i], 16)
                    sp.dma_start(w2[0:rows, e0:e1, :, :], w_in[f][1][:, e0:e1, :, :]).then_inc(w_loaded[f][i], 16)
            for g in range(NG):
                sp.wait_ge(last_x_done.sem, last_x_done.at(TG * (g + 1)))
                sp.dma_start(out[:, TG * g:TG * g + TG, :], X[:, TG * g:TG * g + TG, :]).then_inc(stored, 16)
            sp.wait_ge(stored, 16 * NG)

        def kv_stages(tag):
            multi = tag != "L1x"
            psum_n = {"L0x": 0, "L1x": 2, "L2x": 3, "L3x": 4}[tag]
            s_psum = sem("kv_psum", psum_n)
            kT_ready = sem("kT_ready", 1)
            v_ready = sem("v_ready", 1)
            vb_psum = sem("vb_psum", B if multi else 0)
            vb_ready = sem("vb_ready", B if multi else 0)
            c_ready = sem("ctx_normalised", 1 if tag == "L3x" else 0)
            cT_ready = sem("ctx_transposed", 1 if tag == "L3x" else 0)
            s_var = sem("ctx_variance", 1 if tag == "L3x" else 0)
            s_rstd = sem("ctx_rstd", 1 if tag == "L3x" else 0)
            keysT = {"L0x": [pc("ctxT")], "L1x": [k1T[:, :]], "L2x": [k1T[:, :], k2T[:, :]], "L3x": [k2T[:, :]]}[tag]

            banks_read = []

            def values(pe, bank, ctxT, w):
                for b in range(B):
                    last = nc.tensor.matmul(PS[0:K, bank, b * D:b * D + D], ctxT[:, b * K:b * K + K], pc(w),
                                            start=True, stop=True)
                last.then_inc(s_psum.sem, 1)

            def tensor_early(pe):
                if tag == "L0x":
                    return
                if tag == "L1x":
                    pe.wait_ge(par_in_2, 16)
                cT, ws = pc("ctxT"), {"L1x": ["L1x_wk"], "L2x": ["L2x_k1", "L2x_k2"], "L3x": ["L3x_k", "L3x_kr"]}[tag]
                if tag == "L3x":
                    pe.wait_ge(c_ready.sem, c_ready.at(1))
                    for b in range(B):
                        last = nc.tensor.transpose(PS[:, 3, b * K:b * K + K], ctxn[:, b, :], ident[0:K, 0:K])
                    last.then_inc(s_psum.sem, 1)
                    pe.wait_ge(cT_ready.sem, cT_ready.at(1))
                    cT = k1T[:, :]
                for i, w in enumerate(ws):
                    nc.tensor.matmul(PS[:, i, 0:B * K], pc(w), cT, start=True, stop=True).then_inc(s_psum.sem, 1)
                values(pe, 2, cT, {"L1x": "L1x_wv", "L2x": "L2x_v1", "L3x": "L3x_v"}[tag])

            def scalar_early(a, st):
                if tag == "L3x":
                    a.wait_ge(s_psum.sem, s_psum.at(1))
                    nc.scalar.activation(k1T[:, :], PS[:, 3, 0:B * K], ACT.Identity, scale=pc("L3x_gamma"),
                                         bias=pc("L3x_beta")).then_inc(cT_ready.sem, 1)

            def pool_early(p, st):
                if tag == "L3x":
                    p.wait_ge(s_var.sem, s_var.at(1))
                    nc.gpsimd.tensor_scalar(rs[0:K, 2, 0:B], rs[0:K, 0, 0:B], LN_EPS, None, ALU.add).then_inc(p_step, st.one())
                    p.wait_ge(p_step, st.n)
                    nc.gpsimd.tensor_tensor(rs[0:K, 1, 0:B], rs[0:K, 2, 0:B], mhalf[0:K, 0:B], ALU.pow)\
                        .then_inc(s_rstd.sem, 1)

            def vector_early(v, st):
                if tag != "L3x":
                    return
                for b in range(B):
                    nc.vector.bn_stats(stats[0:K, b, :], pc("ctx", K)[:, b * D:b * D + D]).then_inc(v_step, st.one())
                v.wait_ge(v_step, st.n)
                for b in range(B):
                    nc.vector.bn_aggr(mv[0:K, b, :], stats[0:K, b, :]).then_inc(v_step, st.one())
                v.wait_ge(v_step, st.n)
                nc.vector.tensor_copy(rs[0:K, 0, 0:B], mv[0:K, 0:B, 1]).then_inc(s_var.sem, 1)
                v.wait_ge(s_rstd.sem, s_rstd.at(1))
                for b in range(B):
                    nc.vector.tensor_scalar(ctxn[:, b, :], pc("ctx", K)[:, b * D:b * D + D], mv[0:K, b, 0:1],
                                            rs[0:K, 1, b:b + 1], ALU.subtract, ALU.mult).then_inc(v_step, st.one())
                v.wait_ge(v_step, st.n)
                v.sem_inc(c_ready.sem, 1)

            def vector(v, st):
                if tag == "L1x":
                    v.wait_ge(s_psum.sem, s_psum.at(1))
                    nc.vector.tensor_scalar(k1T[:, :], PS[:, 0, 0:B * K], pc("L1x_bk"), None, ALU.add)\
                        .then_inc(kT_ready.sem, 1)
                    v.wait_ge(s_psum.sem, s_psum.at(2))
                    nc.vector.tensor_tensor(v1[:, :, :], PS[0:K, 2, :].rearrange("k (b d) -> k b d", b=B),
                                            pc("L1x_bv", K).unsqueeze(1).to_broadcast([K, B, D]), ALU.add)\
                        .then_inc(v_ready.sem, 1)
                    return
                if tag == "L0x":
                    v.wait_ge(par_in_1, 16)
                    v.sem_inc(kT_ready.sem, 1)
                if tag == "L2x":
                    for i, dst in enumerate((k1T, k2T)):
                        v.wait_ge(s_psum.sem, s_psum.at(i + 1))
                        nc.vector.tensor_copy(dst[:, :], PS[:, i, 0:B * K]).then_inc(v_step, st.one())
                    v.wait_ge(v_step, st.n)
                    v.sem_inc(kT_ready.sem, 1)
                if tag == "L3x":
                    for i, (dst, tab) in enumerate(((k2T, "cos"), (k1T, "sin"))):
                        v.wait_ge(s_psum.sem, s_psum.at(4))
                        nc.vector.tensor_tensor(dst[:, :].rearrange("p (b k) -> p b k", b=B),
                                                PS[:, i, 0:B * K].rearrange("p (b k) -> p b k", b=B),
                                                pc(tab)[:, 0:K].unsqueeze(1).to_broadcast([P, B, K]), ALU.mult)\
                            .then_inc(v_step, st.one())
                    v.wait_ge(v_step, st.n)
                    nc.vector.tensor_tensor(k2T[:, :], k2T[:, :], k1T[:, :], ALU.add).then_inc(kT_ready.sem, 1)
                for b in range(B):
                    if tag == "L0x":
                        src = pc("ctx", K)[:, b * D:b * D + D]
                    else:
                        v.wait_ge(s_psum.sem, s_psum.at(psum_n))
                        src = PS[0:K, 2, b * D:b * D + D]
                    nc.vector.tensor_copy(vaug[:, b, 0:H, 0:HD], src.rearrange("k (h d) -> k h d", h=H))\
                        .then_inc(v_step, st.one())
                v.wait_ge(v_step, st.n)
                v.sem_inc(v_ready.sem, 1)
                mask = pc("hmask").unsqueeze(2).to_broadcast([P, NHM, VW])
                for b in range(B):
                    v.wait_ge(vb_psum.sem, vb_psum.at(b + 1))
                    by_block = PS[:, 6 + b % 2, 0:NHM * VW].rearrange("p (n w) -> p n w", w=VW)
                    nc.vector.tensor_tensor(vfull[:, b, 0:3 * VW].rearrange("p (n w) -> p n w", w=VW),
                                            by_block[:, 0:3, :], mask[:, 0:3, :], ALU.mult).then_inc(v_step, st.one())
                    nc.vector.tensor_tensor(vblk[:, b, :].rearrange("p (n w) -> p n w", w=VW), by_block, mask, ALU.mult)\
                        .then_inc(vb_ready.sem, 1)
                v.wait_ge(v_step, st.n)

            def tensor(pe):
                pe.wait_ge(v_ready.sem, v_ready.at(1))
                if tag == "L1x":
                    return
                if banks_read:
                    pe.wait_ge(banks_read[0].sem, banks_read[0].at(banks_read[1]))
                for b in range(B):
                    if b >= 2:
                        pe.wait_ge(vb_ready.sem, vb_ready.at(b - 1))
                    for j in range(NBLK):
                        h0, at = BLOCKS[j][0], j * P % K
                        n = min(3, NHM - 3 * j)
                        last = nc.tensor.matmul(PS[:, 6 + b % 2, 3 * j * VW:(3 * j + n) * VW],
                                                pc("wrap", K)[:, at:at + P], vaug[:, b, h0:h0 + n, :],
                                                start=True, stop=True)
                    last.then_inc(vb_psum.sem, 1)
            early = dict(tensor=tensor_early, vector=vector_early, scalar=scalar_early, pool=pool_early)
            return early, dict(vector=vector, tensor=tensor), dict(keysT=keysT, kT_ready=kT_ready, vb_ready=vb_ready,
                                                                  banks_read=banks_read)

        def norm_stage(tag, x_ready, second=None, post=None):
            levels = 2 if second else 1
            var_ready = sem("var", levels * NG)
            rstd_ready = sem("rstd", levels * NG)
            xn_ready = sem("xn", NT)
            xT_psum = sem("xT_psum", NG)
            xT_ready = sem("xT", NG)
            upper = split_space(tag)[0] if tag in FFNS else None
            upper_ready = sem("x_upper", NG) if tag in FFNS else None

            def vector(v, st):
                def statistics(level, g):
                    for t in range(TG * g, TG * g + TG):
                        if level == 0:
                            x_ready(v, t)
                            src = X[:, t, :]
                        else:
                            src = xn[:, t, :]
                        if level and second == "rms":
                            nc.vector.scalar_tensor_tensor(fin[:, t % 4, :], src, 1.0, src, ALU.mult, ALU.mult,
                                                                 accum_out=mv[:, t, 1:2]).then_inc(v_step, st.one())
                        else:
                            nc.vector.bn_stats(stats[:, t, :], src).then_inc(v_step, st.one())
                    v.wait_ge(v_step, st.n)
                    if level and second == "rms":
                        nc.vector.tensor_scalar(vare[:, TG * g:TG * g + TG], mv[:, TG * g:TG * g + TG, 1], 1.0 / D,
                                                RMS_EPS, ALU.mult, ALU.add).then_inc(var_ready.sem, 1)
                        return
                    for t in range(TG * g, TG * g + TG):
                        nc.vector.bn_aggr(mv[:, t, :], stats[:, t, :]).then_inc(v_step, st.one())
                    v.wait_ge(v_step, st.n)
                    nc.vector.tensor_scalar(vare[:, TG * g:TG * g + TG], mv[:, TG * g:TG * g + TG, 1], LN_EPS, None,
                                            ALU.add).then_inc(var_ready.sem, 1)

                def apply(level, g):
                    v.wait_ge(rstd_ready.sem, rstd_ready.at(NG * level + g + 1))
                    for t in range(TG * g, TG * g + TG):
                        src = X[:, t, :] if level == 0 else xn[:, t, :]
                        dst = xn[:, t, :] if level == 0 else qa[:, t * D:t * D + D]
                        if level and second == "rms":
                            ins = nc.vector.tensor_scalar(dst, src, rstd[:, t:t + 1], None, ALU.mult)
                        else:
                            ins = nc.vector.tensor_scalar(dst, src, mv[:, t, 0:1], rstd[:, t:t + 1],
                                                          ALU.subtract, ALU.mult)
                        if level == levels - 1:
                            ins.then_inc(xn_ready.sem, 1)
                        else:
                            ins.then_inc(v_step, st.one())

                for level in range(levels):
                    if level:
                        v.wait_ge(v_step, st.n)
                    for g in range(NG + 1):
                        if g < NG:
                            statistics(level, g)
                        if g:
                            apply(level, g - 1)

            def pool(p, st):
                for n in range(levels * NG):
                    c = slice(TG * (n % NG), TG * (n % NG) + TG)
                    p.wait_ge(var_ready.sem, var_ready.at(n + 1))
                    nc.gpsimd.tensor_tensor(rstd[:, c], vare[:, c], mhalf[:, c], ALU.pow).then_inc(rstd_ready.sem, 1)

            def tensor(pe):
                for g in range(NG):
                    pe.wait_ge(xn_ready.sem, xn_ready.at(TG * (g + 1)))
                    if g >= 2:
                        read = upper_ready or xT_ready
                        pe.wait_ge(read.sem, read.at(g - 1))
                    for j in range(TG):
                        t = TG * g + j
                        src = xn[:, t, :] if levels == 1 else qa[:, t * D:t * D + D]
                        last = nc.tensor.transpose(PS[:, 4 + g % 2, j * P:j * P + P], src, ident)
                    last.then_inc(xT_psum.sem, 1)

            def scalar(a, st):
                for g in range(NG):
                    a.wait_ge(xT_psum.sem, xT_psum.at(g + 1))
                    cols = slice(g * 512, g * 512 + 512)
                    scale, bias = post or (1.0, 0.0)
                    nc.scalar.activation(xnT[:, cols], PS[:, 4 + g % 2, :], ACT.Identity, scale=scale,
                                         bias=bias).then_inc(xT_ready.sem, 1)
                    if upper is not None:
                        nc.scalar.activation(upper[:, cols], PS[:, 4 + g % 2, :], ACT.Identity,
                                             scale=scale, bias=bias).then_inc(upper_ready.sem, 1)
            return dict(vector=vector, pool=pool, tensor=tensor, scalar=scalar, ready=xT_ready, upper_ready=upper_ready)

        def proj_stage(tag, xT_ready):
            ws = {"L1x": ["L1x_wq"], "L2x": ["L2x_q1", "L2x_q2"], "L3x": ["L3x_q", "L3x_qr"]}[tag]
            n = len(ws)
            q_psum = sem("q_psum", n * NG)
            q_used = sem("q_rotated" if tag == "L3x" else "q_copied", n * NG)
            q_ready = sem("q_ready", NG if tag == "L3x" else 0)

            def tensor(pe):
                for g in range(NG):
                    pe.wait_ge(xT_ready.sem, xT_ready.at(g + 1))
                    for s in range(n):
                        i = n * g + s
                        if i >= 2:
                            pe.wait_ge(q_used.sem, q_used.at(i - 1))
                        nc.tensor.matmul(PS[:, 6 + i % 2, :], pc(ws[s]), xnT[:, g * 512:g * 512 + 512],
                                         start=True, stop=True).then_inc(q_psum.sem, 1)

            if tag != "L3x":
                def scalar(a, st):
                    for i in range(n * NG):
                        g, s = i // n, i % n
                        a.wait_ge(q_psum.sem, q_psum.at(i + 1))
                        dst = (qa, qb)[s][:, g * 512:g * 512 + 512]
                        if tag == "L1x":
                            ins = nc.scalar.activation(dst, PS[:, 6 + i % 2, :], ACT.Identity, bias=pc("L1x_bq"))
                        else:
                            ins = nc.scalar.activation(dst, PS[:, 6 + i % 2, :], ACT.Copy)
                        ins.then_inc(q_used.sem, 1)
                return dict(tensor=tensor, scalar=scalar, ready=q_used, per=n, used=q_used, projections=n)

            def vector(v, st):
                for g in range(NG):
                    c = slice(g * 512, g * 512 + 512)
                    v.wait_ge(q_psum.sem, q_psum.at(2 * g + 1))
                    nc.vector.tensor_tensor(qa[:, c], PS[:, 6, :], pc("cos"), ALU.mult).then_inc(q_used.sem, 1)
                    v.wait_ge(q_psum.sem, q_psum.at(2 * g + 2))
                    nc.vector.tensor_tensor(qb[:, c], PS[:, 7, :], pc("sin"), ALU.mult).then_inc(q_used.sem, 1)
                    v.wait_ge(q_used.sem, q_used.at(2 * g + 2))
                    nc.vector.tensor_tensor(qa[:, c], qa[:, c], qb[:, c], ALU.add).then_inc(q_ready.sem, 1)
            return dict(tensor=tensor, vector=vector, ready=q_ready, per=1, used=q_used, projections=n)

        def attention_stage(tag, q_ready, q_per, kv):
            kb = kb_of[tag]
            sets = 2 if tag == "L2x" else 1
            units = NT * sets
            q = [xnT] if tag == "L0x" else [qa, qb]
            scale = {"L0x": float(D) ** -0.5, "L2x": float(HD) ** -0.5, "L3x": 1.0}[tag]
            spread = pc("headsc" if tag == "L3x" else "heads")
            kb_ready = sem("kb_ready", sets * B)
            scores_ready = sem("scores", units)
            scores_used = sem("scores_used", units)
            to_shift = sem("to_shift", 0 if sets == 2 else units)
            shifted = sem("shifted_2" if sets == 2 else "shifted", units)
            exp_ready = sem("exp", units)
            pT_psum = sem("pT_psum", 3 * units)
            pT_ready = sem("pT", 3 * units)
            o_psum = sem("o_psum", units)
            o_used = sem("o_used", units)
            o_ready = sem("o", NT)
            oT_psum = sem("oT_psum", NT)
            oT_ready = sem("oT", NT)
            y_psum = sem("y_psum", NT)
            x_done = sem("x_done", NT)
            if tag == "L3x":
                aT_ready = sem("attT", NT)
                g_psum = sem("gate_psum", NT)
                g_in = sem("gate_in", NT)
                g_exp = sem("gate_exp", NT)
            if tag == "L2x":
                ss_ready = sem("square_sum", NT)
                rms_ready = sem("rms", NT)
            groups = [range(i, min(i + 4, NBLK)) for i in range(0, NBLK, 4)]

            def tile_of(u):
                return u // sets

            def exps_of(u):
                return score[:, u % 3, :, :].rearrange("p h k -> p (h k)")

            def after_unit(u):
                return tile_of(u - sets) if u >= sets and u % sets == 0 else None

            def tensor(pe):
                def scores(u):
                    t, s = tile_of(u), u % sets
                    b = t // TG
                    pe.wait_ge(q_ready.sem, q_ready.at(q_per * (b + 1)))
                    pe.wait_ge(kb_ready.sem, kb_ready.at(sets * b + s + 1))
                    if u:
                        pe.wait_ge(scores_used.sem, scores_used.at(u))
                    for r in range(RG):
                        last = nc.tensor.matmul(PS[:, r, 0:HR * K], q[s][:, t * P:t * P + P],
                                                kb[:, s, b % 2, HR * r:HR * r + HR, :], start=True, stop=True)
                    last.then_inc(scores_ready.sem, 1)

                def transposes(u):
                    pe.wait_ge(exp_ready.sem, exp_ready.at(u + 1))
                    for i, blocks in enumerate(groups):
                        n = 3 * u + i
                        if n >= 2:
                            pe.wait_ge(pT_ready.sem, pT_ready.at(n - 1))
                        for j in blocks:
                            w = BLOCKS[j][2]
                            last = nc.tensor.transpose(PS[0:w, 4 + n % 2, (j % 4) * P:(j % 4) * P + P],
                                                       exps_of(u)[:, j * P:j * P + w], ident)
                        last.then_inc(pT_psum.sem, 1)

                def weighted(u):
                    b = tile_of(u) // TG
                    if u:
                        pe.wait_ge(o_used.sem, o_used.at(u))
                    for j, (h0, nh, w) in enumerate(BLOCKS):
                        if j % 4 == 0:
                            pe.wait_ge(pT_ready.sem, pT_ready.at(3 * u + j // 4 + 1))
                        pT = hT[0:w, u % 2, j // 4, (j % 4) * P:(j % 4) * P + P]
                        if j == 0:
                            nc.tensor.matmul(PS[:, 6, 0:H * VW], pT, vfull[:, b, :], start=True, stop=False)
                        else:
                            last = nc.tensor.matmul(PS[:, 6, h0 * VW:(h0 + nh) * VW], pT,
                                                    vblk[0:w, b, 3 * j * VW:(3 * j + nh) * VW],
                                                    start=False, stop=j == NBLK - 1)
                    last.then_inc(o_psum.sem, 1)

                def out_transpose(t):
                    pe.wait_ge(o_ready.sem, o_ready.at(t + 1))
                    if t:
                        free = g_in if tag == "L3x" else x_done
                        pe.wait_ge(free.sem, free.at(t))
                    nc.tensor.transpose(PS[:, 7, 0:P], (oc2 if tag == "L2x" else oc)[:, t % 2, :], ident)\
                        .then_inc(oT_psum.sem, 1)

                def out_project(t):
                    pe.wait_ge(oT_ready.sem, oT_ready.at(t + 1))
                    last = nc.tensor.matmul(PS[:, 7, P:2 * P], ocT[:, t % 2, :], pc(f"{tag}_wo"), start=True, stop=True)
                    if tag == "L3x":
                        last = nc.tensor.matmul(PS[:, 7, 2 * P:3 * P], pc("L3x_wo"), ocT[:, t % 2, :],
                                                start=True, stop=True)
                    last.then_inc(y_psum.sem, 1)

                def gate(t):
                    pe.wait_ge(aT_ready.sem, aT_ready.at(t + 1))
                    nc.tensor.matmul(PS[:, 7, 3 * P:4 * P], attT[:, t % 2, :], pc("L3x_wg"), start=True, stop=True)\
                        .then_inc(g_psum.sem, 1)

                scores(0)
                scores(1)
                pe.wait_ge(kv["vb_ready"].sem, kv["vb_ready"].at(B))
                for u in range(units + sets):
                    if u + 2 < units:
                        scores(u + 2)
                    done = after_unit(u)
                    if done is not None:
                        out_transpose(done)
                    if u < units:
                        transposes(u)
                    if done is not None:
                        out_project(done)
                    if u < units:
                        weighted(u)
                    if done is not None and tag == "L3x":
                        gate(done)

            def vector(v, st):
                def maxima(u):
                    t = tile_of(u)
                    v.wait_ge(scores_ready.sem, scores_ready.at(u + 1))
                    ps = PS[:, 0:RG, 0:HR * K].rearrange("p r (h k) -> p r h k", h=HR)
                    dst = score[:, u % 3, :, :]
                    dst4 = dst.rearrange("p (r h) k -> p r h k", r=RG)
                    m = mx[:, u % 3, :]
                    if tag == "L2x":
                        nc.vector.tensor_reduce(m, ps, AX.X, ALU.max).then_inc(v_step, st.one())
                        v.wait_ge(v_step, st.n)
                        nc.vector.tensor_tensor(dst4, ps, m.rearrange("p (r h) -> p r h", r=RG).unsqueeze(3)
                                                .to_broadcast([P, RG, HR, K]), ALU.subtract).then_inc(scores_used.sem, 1)
                        return
                    if tag == "L0x":
                        other, op = bound[:, t, :], ALU.min
                    else:
                        other, op = pc("tbias")[:, (t % TG) * K:(t % TG) * K + K], ALU.add
                    nc.vector.tensor_tensor(dst4, ps, other.unsqueeze(1).unsqueeze(1).to_broadcast([P, RG, HR, K]), op)\
                        .then_inc(scores_used.sem, 1)
                    v.wait_ge(scores_used.sem, scores_used.at(u + 1))
                    nc.vector.tensor_reduce(m, dst, AX.X, ALU.max).then_inc(to_shift.sem, 1)

                def normalise(u):
                    t, s = tile_of(u), u % sets
                    v.wait_ge(o_psum.sem, o_psum.at(u + 1))
                    o = PS[:, 6, 0:H * VW].rearrange("p (h d) -> p h d", h=H)
                    r = rec[:, u % 2, :]
                    nc.vector.reciprocal(r, o[:, :, HD]).then_inc(v_step, st.one())
                    v.wait_ge(v_step, st.n)
                    if tag == "L2x" and s:
                        nc.vector.tensor_tensor(r, r, lam[:, :], ALU.mult).then_inc(v_step, st.one())
                        v.wait_ge(v_step, st.n)
                    rb = r.unsqueeze(2).to_broadcast([P, H, HD])
                    heads = oc[:, t % 2, :].rearrange("p (h d) -> p h d", h=H)
                    if tag != "L2x":
                        nc.vector.tensor_tensor(heads, o[:, :, 0:HD], rb, ALU.mult).then_inc(o_used.sem, 1)
                        v.wait_ge(o_used.sem, o_used.at(u + 1))
                        v.sem_inc(o_ready.sem, 1)
                        return
                    if s == 0:
                        nc.vector.tensor_tensor(heads, o[:, :, 0:HD], rb, ALU.mult).then_inc(o_used.sem, 1)
                        return
                    second = fin[:, 0, :].rearrange("p (h d) -> p h d", h=H)
                    nc.vector.tensor_tensor(second, o[:, :, 0:HD], rb, ALU.mult).then_inc(o_used.sem, 1)
                    v.wait_ge(o_used.sem, o_used.at(u + 1))
                    nc.vector.tensor_tensor(oc[:, t % 2, :], oc[:, t % 2, :], fin[:, 0, :], ALU.subtract)\
                        .then_inc(v_step, st.one())
                    v.wait_ge(v_step, st.n)
                    nc.vector.scalar_tensor_tensor(fin[:, 1, :], oc[:, t % 2, :], 1.0, oc[:, t % 2, :], ALU.mult,
                                                   ALU.mult, accum_out=oss[:, t % 2:t % 2 + 1]).then_inc(ss_ready.sem, 1)

                def root_mean_square(t):
                    v.wait_ge(rms_ready.sem, rms_ready.at(t + 1))
                    nc.vector.tensor_scalar(oc2[:, t % 2, :], oc[:, t % 2, :], osr[:, t % 2:t % 2 + 1], None, ALU.mult)\
                        .then_inc(o_ready.sem, 1)

                def evacuate_oT(t):
                    v.wait_ge(oT_psum.sem, oT_psum.at(t + 1))
                    if tag == "L2x":
                        nc.vector.tensor_scalar(ocT[:, t % 2, :], PS[:, 7, 0:P], pc("L2x_norm"), None, ALU.mult)\
                            .then_inc(oT_ready.sem, 1)
                    else:
                        nc.vector.tensor_copy(ocT[:, t % 2, :], PS[:, 7, 0:P]).then_inc(oT_ready.sem, 1)

                def finish(t):
                    v.wait_ge(y_psum.sem, y_psum.at(t + 1))
                    y, att, xt = PS[:, 7, P:2 * P], fin[:, 2, :], X[:, t, :]
                    nc.vector.tensor_tensor(att, y, pc(f"{tag}_bo"), ALU.add).then_inc(v_step, st.one())
                    if tag != "L3x":
                        v.wait_ge(v_step, st.n)
                        nc.vector.tensor_tensor(xt, xt, att, ALU.add).then_inc(x_done.sem, 1)
                        return
                    nc.vector.tensor_scalar(attT[:, t % 2, :], PS[:, 7, 2 * P:3 * P], pc("L3x_boc"), None, ALU.add)\
                        .then_inc(aT_ready.sem, 1)
                    v.wait_ge(v_step, st.n)
                    nc.vector.tensor_tensor(gdiff[:, t % 2, :], att, xn[:, t, :], ALU.subtract).then_inc(v_step, st.one())
                    nc.vector.tensor_tensor(xt, xt, xn[:, t, :], ALU.add).then_inc(v_step, st.one())

                def gate_in(t):
                    v.wait_ge(g_psum.sem, g_psum.at(t + 1))
                    nc.vector.tensor_tensor(gin[:, t % 2, :], PS[:, 7, 3 * P:4 * P], pc("L3x_bg"), ALU.add)\
                        .then_inc(g_in.sem, 1)

                def gate_out(t):
                    g, d = gin[:, t % 2, :], gdiff[:, t % 2, :]
                    v.wait_ge(g_exp.sem, g_exp.at(t + 1))
                    nc.vector.tensor_scalar(g, g, 1.0, None, ALU.add).then_inc(v_step, st.one())
                    v.wait_ge(v_step, st.n)
                    nc.vector.reciprocal(g, g).then_inc(v_step, st.one())
                    v.wait_ge(v_step, st.n)
                    nc.vector.tensor_tensor(d, d, g, ALU.mult).then_inc(v_step, st.one())
                    v.wait_ge(v_step, st.n)
                    nc.vector.tensor_tensor(X[:, t, :], X[:, t, :], d, ALU.add).then_inc(x_done.sem, 1)

                if tag == "L2x":
                    nc.vector.tensor_tensor(lam[:, :], pc("L2x_lam1"), pc("L2x_lam2"), ALU.subtract).then_inc(v_step, st.one())
                    v.wait_ge(v_step, st.n)
                    nc.vector.tensor_scalar(lam[:, :], lam[:, :], 0.1, None, ALU.add).then_inc(v_step, st.one())
                    v.wait_ge(v_step, st.n)
                maxima(0)
                maxima(1)
                for u in range(units + sets + (tag == "L3x")):
                    done = after_unit(u) if u < units + sets else None
                    if tag == "L3x" and u >= 2:
                        gate_in(u - 2)
                    if done is not None:
                        if tag == "L2x":
                            root_mean_square(done)
                        evacuate_oT(done)
                    if u + 2 < units:
                        maxima(u + 2)
                    if tag == "L3x" and u >= 2:
                        gate_out(u - 2)
                    if done is not None:
                        finish(done)
                    if u < units:
                        normalise(u)

            def scalar(a, st):
                def exps(u):
                    ready = scores_used if sets == 2 else shifted
                    a.wait_ge(ready.sem, ready.at(u + 1))
                    nc.scalar.activation(score[:, u % 3, :, :], score[:, u % 3, :, :], ACT.Exp, scale=scale)\
                        .then_inc(exp_ready.sem, 1)

                exps(0)
                for u in range(units + sets + (tag == "L3x")):
                    if tag == "L3x" and u >= 2:
                        t = u - 2
                        a.wait_ge(g_in.sem, g_in.at(t + 1))
                        nc.scalar.activation(gin[:, t % 2, :], gin[:, t % 2, :], ACT.Exp, scale=-1.0).then_inc(g_exp.sem, 1)
                    if u < units:
                        for i, blocks in enumerate(groups):
                            n, width = 3 * u + i, len(blocks) * P
                            a.wait_ge(pT_psum.sem, pT_psum.at(n + 1))
                            if i == 0 and u >= 2:
                                a.wait_ge(o_psum.sem, o_psum.at(u - 1))
                            full = width if blocks[-1] < NBLK - 1 else width - P
                            nc.scalar.activation(hT[:, u % 2, i, 0:full], PS[:, 4 + n % 2, 0:full], ACT.Copy)\
                                .then_inc(*((pT_ready.sem, 1) if full == width else (a_step, st.one())))
                            if full < width:
                                rows = BLOCKS[-1][2]
                                nc.scalar.activation(hT[0:rows, u % 2, i, full:width], PS[0:rows, 4 + n % 2, full:width],
                                                     ACT.Copy).then_inc(pT_ready.sem, 1)
                    if u + 1 < units:
                        exps(u + 1)

            def pool(p, st):
                def spread_keys(b):
                    for s in range(sets):
                        if b >= 2:
                            p.wait_ge(scores_ready.sem, scores_ready.at(sets * TG * (b - 1)))
                        keys = kv["keysT"][s][:, b * K:b * K + K].unsqueeze(1).to_broadcast([P, H, K])
                        nc.gpsimd.tensor_tensor(kb[:, s, b % 2, :, :], keys, spread.unsqueeze(2).to_broadcast([P, H, K]),
                                                ALU.mult).then_inc(kb_ready.sem, 1)

                def shift(u):
                    p.wait_ge(to_shift.sem, to_shift.at(u + 1))
                    nc.gpsimd.tensor_tensor(score[:, u % 3, :, :], score[:, u % 3, :, :],
                                            mx[:, u % 3, :].unsqueeze(2).to_broadcast([P, H, K]), ALU.subtract)\
                        .then_inc(shifted.sem, 1)

                p.wait_ge(kv["kT_ready"].sem, kv["kT_ready"].at(1))
                spread_keys(0)
                for t in range(NT):
                    if t % TG == 0 and t // TG + 1 < B:
                        if sets == 2 or t > 0:
                            spread_keys(t // TG + 1)
                    if sets == 1:
                        shift(t)
                        if t == 0:
                            spread_keys(1)
                    if tag == "L2x":
                        p.wait_ge(ss_ready.sem, ss_ready.at(t + 1))
                        nc.gpsimd.tensor_scalar(oss[:, t % 2:t % 2 + 1], oss[:, t % 2:t % 2 + 1], 1.0 / D,
                                                RMS_EPS, ALU.mult, ALU.add).then_inc(p_step, st.one())
                        p.wait_ge(p_step, st.n)
                        nc.gpsimd.tensor_tensor(osr[:, t % 2:t % 2 + 1], oss[:, t % 2:t % 2 + 1], mhalf[:, 0:1],
                                                ALU.pow).then_inc(rms_ready.sem, 1)
            return dict(tensor=tensor, vector=vector, scalar=scalar, pool=pool, x_done=x_done)

        def single_stage(tag, q_ready, kv):
            scores_ready = sem("scores", B)
            shifted = sem("shifted", B)
            exp_ready = sem("exp", B)
            pT_psum = sem("pT_psum", B)
            pT_ready = sem("pT", B)
            o_psum = sem("o_psum", B)
            x_done = sem("x_done", NT)

            def tensor(pe):
                def scores(b):
                    pe.wait_ge(q_ready.sem, q_ready.at(b + 1))
                    if b >= 2:
                        pe.wait_ge(shifted.sem, shifted.at(b - 1))
                    for j in range(TG):
                        t = TG * b + j
                        last = nc.tensor.matmul(PS[:, b % 2, j * K:j * K + K], qa[:, t * P:t * P + P],
                                                k1T[:, b * K:b * K + K], start=True, stop=True)
                    last.then_inc(scores_ready.sem, 1)

                scores(0)
                for b in range(B):
                    if b + 1 < B:
                        scores(b + 1)
                    pe.wait_ge(exp_ready.sem, exp_ready.at(b + 1))
                    for j in range(TG):
                        last = nc.tensor.transpose(PS[0:K, 2 + b % 2, j * P:j * P + P], score[:, b % 2, j, :], ident)
                    last.then_inc(pT_psum.sem, 1)
                    pe.wait_ge(pT_ready.sem, pT_ready.at(b + 1))
                    if b >= 2:
                        pe.wait_ge(x_done.sem, x_done.at(TG * (b - 1)))
                    for j in range(TG):
                        last = nc.tensor.matmul(PS[:, 4 + b % 2, j * P:j * P + P], hT[0:K, b % 2, 0, j * P:j * P + P],
                                                v1[:, b, :], start=True, stop=True)
                    last.then_inc(o_psum.sem, 1)

            def vector(v, st):
                def shift(b):
                    v.wait_ge(scores_ready.sem, scores_ready.at(b + 1))
                    ps = PS[:, b % 2, 0:TG * K].rearrange("p (j k) -> p j k", j=TG)
                    m = mx[:, b % 2, 0:TG]
                    nc.vector.tensor_reduce(m, ps, AX.X, ALU.max).then_inc(v_step, st.one())
                    v.wait_ge(v_step, st.n)
                    nc.vector.tensor_tensor(score[:, b % 2, 0:TG, :], ps, m.unsqueeze(2).to_broadcast([P, TG, K]),
                                            ALU.subtract).then_inc(shifted.sem, 1)

                shift(0)
                for b in range(B):
                    if b + 1 < B:
                        shift(b + 1)
                    v.wait_ge(exp_ready.sem, exp_ready.at(b + 1))
                    r = rec[:, b % 2, 0:TG]
                    nc.vector.tensor_reduce(r, score[:, b % 2, 0:TG, :], AX.X, ALU.add).then_inc(v_step, st.one())
                    v.wait_ge(v_step, st.n)
                    nc.vector.reciprocal(r, r).then_inc(v_step, st.one())
                    v.wait_ge(v_step, st.n)
                    v.wait_ge(o_psum.sem, o_psum.at(b + 1))
                    for j in range(TG):
                        t = TG * b + j
                        nc.vector.scalar_tensor_tensor(X[:, t, :], PS[:, 4 + b % 2, j * P:j * P + P], r[:, j:j + 1],
                                                       X[:, t, :], ALU.mult, ALU.add).then_inc(x_done.sem, 1)

            def scalar(a, st):
                def exps(b):
                    a.wait_ge(shifted.sem, shifted.at(b + 1))
                    nc.scalar.activation(score[:, b % 2, 0:TG, :], score[:, b % 2, 0:TG, :], ACT.Exp,
                                         scale=float(D) ** -0.5).then_inc(exp_ready.sem, 1)
                exps(0)
                for b in range(B):
                    a.wait_ge(pT_psum.sem, pT_psum.at(b + 1))
                    nc.scalar.activation(hT[0:K, b % 2, 0, :], PS[0:K, 2 + b % 2, :], ACT.Copy).then_inc(pT_ready.sem, 1)
                    if b + 1 < B:
                        exps(b + 1)
            return dict(tensor=tensor, vector=vector, scalar=scalar, x_done=x_done)

        def route_stage(tag, xT_ready):
            logits_psum = sem("logits", 1)
            e_in = sem("route_in", 1)
            e_out = sem("route_exp", 1)
            w_ready = sem("w", 1)
            wT_psum = sem("wT_psum", 0 if tag == "L3f" else NG)
            wT_ready = sem("wT", 0 if tag == "L3f" else NG)
            b2_psum = sem("b2_psum", 0 if tag == "L3f" else NG)
            x_first = sem("x_first", NG)
            n_e = FFNS[tag]["experts"]
            if tag == "L2f":
                oh_ready = sem("L2f_onehots")
                count_psum = sem("L2f_counts")

            def tensor(pe):
                for t in range(NT):
                    if t % TG == 0:
                        pe.wait_ge(xT_ready.sem, xT_ready.at(t // TG + 1))
                    last = nc.tensor.matmul(PS[:, 6, t * E:t * E + E], xnT[:, t * P:t * P + P], pc(f"{tag}_wr"),
                                            start=True, stop=True)
                last.then_inc(logits_psum.sem, 1)
                if tag == "L2f":
                    pe.wait_ge(oh_ready.sem, oh_ready.at(2))
                    for i in range(2):
                        oh = rt[:, 4 + i, :, :]
                        nc.tensor.matmul(PS[:, 7, i * P:i * P + P], pc("before"), oh, start=True, stop=True)
                        last = nc.tensor.matmul(PS[:, 7, (2 + i) * P:(3 + i) * P], pc("ones"), oh, start=True, stop=True)
                    last.then_inc(count_psum.sem, 1)
                if tag == "L3f":
                    return
                pe.wait_ge(w_ready.sem, w_ready.at(1))
                for g in range(NG):
                    if g >= 2:
                        pe.wait_ge(wT_ready.sem, wT_ready.at(g - 1))
                    for j in range(TG):
                        last = nc.tensor.transpose(PS[0:n_e, 4 + g % 2, j * P:j * P + P], wts[:, TG * g + j, 0:n_e], ident)
                    last.then_inc(wT_psum.sem, 1)
                for g in range(NG):
                    pe.wait_ge(wT_ready.sem, wT_ready.at(g + 1))
                    if g >= 2:
                        pe.wait_ge(x_first.sem, x_first.at(g - 1))
                    for j in range(TG):
                        t = TG * g + j
                        last = nc.tensor.matmul(PS[:, 6 + g % 2, j * P:j * P + P], qb[0:n_e, t * P:t * P + P],
                                                pc(f"{tag}_b2", n_e), start=True, stop=True)
                    last.then_inc(b2_psum.sem, 1)

            def scalar(a, st):
                a.wait_ge(e_in.sem, e_in.at(1))
                nc.scalar.activation(rt[:, 1, :, :], rt[:, 1, :, :], ACT.Exp).then_inc(e_out.sem, 1)
                if tag == "L3f":
                    return
                for g in range(NG):
                    a.wait_ge(wT_psum.sem, wT_psum.at(g + 1))
                    nc.scalar.activation(qb[0:n_e, g * 512:g * 512 + 512], PS[0:n_e, 4 + g % 2, :], ACT.Copy)\
                        .then_inc(wT_ready.sem, 1)

            def vector(v, st):
                def over_e(a):
                    return a.unsqueeze(2).to_broadcast([P, NT, E])

                iota = pc("iota").unsqueeze(1).to_broadcast([P, NT, E])
                lg, pr, eq, key, oh1, oh2, rest, w = (rt[:, i, :, :] for i in range(8))
                m1, m2, ssum, kmin, keep, g12 = (rs[:, i, 0:NT] for i in range(6))
                v.wait_ge(logits_psum.sem, logits_psum.at(1))
                logits = PS[:, 6, 0:NT * E].rearrange("p (t e) -> p t e", e=E)
                if tag == "L3f":
                    nc.vector.tensor_copy(lg, logits).then_inc(v_step, st.one())
                    v.wait_ge(v_step, st.n)
                else:
                    nc.vector.tensor_tensor(lg, logits, pc(f"{tag}_br").unsqueeze(1).to_broadcast([P, NT, E]),
                                                    ALU.add).then_inc(v_step, st.one())
                    v.wait_ge(v_step, st.n)
                nc.vector.tensor_reduce(m1, lg, AX.X, ALU.max).then_inc(v_step, st.one())
                v.wait_ge(v_step, st.n)
                nc.vector.tensor_tensor(pr, lg, over_e(m1), ALU.subtract).then_inc(e_in.sem, 1)
                v.wait_ge(e_out.sem, e_out.at(1))

                def first_of_max(src, m, oh):
                    nc.vector.tensor_tensor(eq, src, over_e(m), ALU.is_equal).then_inc(v_step, st.one())
                    v.wait_ge(v_step, st.n)
                    nc.vector.scalar_tensor_tensor(key, eq, -1000.0, iota, ALU.mult, ALU.add).then_inc(v_step, st.one())
                    v.wait_ge(v_step, st.n)
                    nc.vector.tensor_reduce(kmin, key, AX.X, ALU.min).then_inc(v_step, st.one())
                    v.wait_ge(v_step, st.n)
                    return nc.vector.tensor_tensor(oh, key, over_e(kmin), ALU.is_equal)

                wv = wts[:, :, 0:E]
                if tag == "L0f":
                    first_of_max(lg, m1, oh1).then_inc(v_step, st.one())
                    v.wait_ge(v_step, st.n)
                    nc.vector.scalar_tensor_tensor(rest, oh1, -3.0e38, lg, ALU.mult, ALU.add).then_inc(v_step, st.one())
                    v.wait_ge(v_step, st.n)
                    nc.vector.tensor_reduce(m2, rest, AX.X, ALU.max).then_inc(v_step, st.one())
                    v.wait_ge(v_step, st.n)
                    nc.vector.tensor_tensor(eq, lg, over_e(m2), ALU.is_ge).then_inc(v_step, st.one())
                    v.wait_ge(v_step, st.n)
                    nc.vector.tensor_tensor(w, pr, eq, ALU.mult).then_inc(v_step, st.one())
                    v.wait_ge(v_step, st.n)
                    nc.vector.tensor_reduce(ssum, w, AX.X, ALU.add).then_inc(v_step, st.one())
                    v.wait_ge(v_step, st.n)
                    nc.vector.reciprocal(ssum, ssum).then_inc(v_step, st.one())
                    v.wait_ge(v_step, st.n)
                    nc.vector.tensor_tensor(wv, w, over_e(ssum), ALU.mult).then_inc(w_ready.sem, 1)
                else:
                    nc.vector.tensor_reduce(ssum, pr, AX.X, ALU.add).then_inc(v_step, st.one())
                    v.wait_ge(v_step, st.n)
                    nc.vector.reciprocal(ssum, ssum).then_inc(v_step, st.one())
                    v.wait_ge(v_step, st.n)
                    nc.vector.tensor_tensor(pr, pr, over_e(ssum), ALU.mult).then_inc(v_step, st.one())
                    v.wait_ge(v_step, st.n)
                    nc.vector.tensor_reduce(m1, pr, AX.X, ALU.max).then_inc(v_step, st.one())
                    v.wait_ge(v_step, st.n)
                    if tag == "L2f":
                        first_of_max(pr, m1, oh1).then_inc(oh_ready.sem, 1)
                        v.wait_ge(oh_ready.sem, oh_ready.at(1))
                    else:
                        first_of_max(pr, m1, oh1).then_inc(v_step, st.one())
                        v.wait_ge(v_step, st.n)
                    nc.vector.scalar_tensor_tensor(rest, oh1, -3.0, pr, ALU.mult, ALU.add).then_inc(v_step, st.one())
                    v.wait_ge(v_step, st.n)
                    nc.vector.tensor_reduce(m2, rest, AX.X, ALU.max).then_inc(v_step, st.one())
                    v.wait_ge(v_step, st.n)
                    if tag == "L2f":
                        first_of_max(rest, m2, oh2).then_inc(oh_ready.sem, 1)
                        v.wait_ge(oh_ready.sem, oh_ready.at(2))
                    else:
                        first_of_max(rest, m2, oh2).then_inc(v_step, st.one())
                        v.wait_ge(v_step, st.n)
                    if tag != "L1f":
                        nc.vector.tensor_tensor(g12, m1, m2, ALU.add).then_inc(v_step, st.one())
                        v.wait_ge(v_step, st.n)
                        nc.vector.reciprocal(g12, g12).then_inc(v_step, st.one())
                        v.wait_ge(v_step, st.n)
                    if tag == "L2f":
                        v.wait_ge(count_psum.sem, count_psum.at(1))
                        before = PS[:, 7, 0:2 * P].rearrange("p (t e) -> p t e", e=E)
                        nc.vector.memset(rc[:, 0, 0, :], 0.0).then_inc(v_step, st.one())
                        nc.vector.tensor_copy(rc[:, 0, 1:2 * NT, :],
                                                      PS[:, 7, 2 * P:4 * P].rearrange("p (t e) -> p t e", e=E)[:, 0:2 * NT - 1, :]).then_inc(v_step, st.one())
                        v.wait_ge(v_step, st.n)
                        side, step = 0, 1
                        while step < 2 * NT:
                            a, b = rc[:, side, :, :], rc[:, 1 - side, :, :]
                            nc.vector.tensor_copy(b[:, 0:step, :], a[:, 0:step, :]).then_inc(v_step, st.one())
                            nc.vector.tensor_tensor(b[:, step:, :], a[:, step:, :], a[:, 0:2 * NT - step, :], ALU.add).then_inc(v_step, st.one())
                            v.wait_ge(v_step, st.n)
                            side, step = 1 - side, 2 * step
                        pos, work = rc[:, side, :, :], rc[:, 1 - side, :, :]
                        nc.vector.tensor_tensor(work, pos, before, ALU.add).then_inc(v_step, st.one())
                        v.wait_ge(v_step, st.n)
                        oh12 = rt[:, 4:6, :, :].rearrange("p a t e -> p (a t) e")
                        nc.vector.tensor_tensor(pos, work, oh12, ALU.mult).then_inc(v_step, st.one())
                        v.wait_ge(v_step, st.n)
                        both = rs[:, 4, :]
                        nc.vector.tensor_reduce(both, pos, AX.X, ALU.add).then_inc(v_step, st.one())
                        v.wait_ge(v_step, st.n)
                        nc.vector.tensor_scalar(both, both, float(CAPACITY), None, ALU.is_lt).then_inc(v_step, st.one())
                        v.wait_ge(v_step, st.n)
                        nc.vector.tensor_tensor(work, oh12, both.unsqueeze(2).to_broadcast([P, 2 * NT, E]), ALU.mult).then_inc(v_step, st.one())
                        v.wait_ge(v_step, st.n)
                        nc.vector.tensor_tensor(eq, work[:, 0:NT, :], work[:, NT:2 * NT, :], ALU.add).then_inc(v_step, st.one())
                        v.wait_ge(v_step, st.n)
                    else:
                        nc.vector.tensor_tensor(eq, oh1, oh2, ALU.add).then_inc(v_step, st.one())
                        v.wait_ge(v_step, st.n)
                    if tag == "L1f":
                        nc.vector.memset(wts[:, :, E:E + 1], 1.0).then_inc(v_step, st.one())
                        nc.vector.tensor_tensor(wv, pr, eq, ALU.mult).then_inc(w_ready.sem, 1)
                    else:
                        nc.vector.tensor_tensor(w, pr, eq, ALU.mult).then_inc(v_step, st.one())
                        v.wait_ge(v_step, st.n)
                        nc.vector.tensor_tensor(wv, w, over_e(g12), ALU.mult).then_inc(w_ready.sem, 1)
                for g in range(NG):
                    xs = X[:, TG * g:TG * g + TG, :]
                    if tag == "L3f":
                        other = xn[:, TG * g:TG * g + TG, :]
                    else:
                        v.wait_ge(b2_psum.sem, b2_psum.at(g + 1))
                        other = PS[:, 6 + g % 2, :].rearrange("p (t d) -> p t d", d=D)
                    nc.vector.tensor_tensor(xs, xs, other, ALU.add).then_inc(x_first.sem, 1)
            return dict(tensor=tensor, vector=vector, scalar=scalar, w_ready=w_ready, x_first=x_first,
                        logits=logits_psum)

        def ffn_stage(tag, x_first, w_ready, upper_ready, logits_read):
            c = FFNS[tag]
            n_e, chunks, rows, gated = c["experts"], c["chunks"], c["rows"], c["gated"]
            w1, w3, w2 = views(tag)
            steps = n_e * NG
            h_psum = sem("h_psum", steps * chunks)
            h_ready = sem("h_gated" if gated else "h", steps * chunks)
            x_split = sem("x_lower", NG)
            w_split = sem("w_halves", n_e)
            upper, halves = split_space(tag)
            y_psum = sem("y_psum", steps)
            y_used = sem("y_used", TG * steps)
            if gated:
                s_ready = sem("silu", steps * chunks)

            def tensor(pe):
                def hidden(n):
                    e, g = n // NG, n % NG
                    if g == 0:
                        pe.wait_ge(w_split.sem, w_split.at(e + 1))
                    if e == 0:
                        pe.wait_ge(x_split.sem, x_split.at(g + 1))
                    cols = slice(g * 512, g * 512 + 512)
                    banks = 2 if gated else 4
                    for k in range(chunks):
                        i = n * chunks + k
                        if i >= banks:
                            pe.wait_ge(h_ready.sem, h_ready.at(i - banks + 1))
                        for m in range(2 if gated else 1):
                            w_up, w_low = (halves[:, e % 2, m, u, k * rows:(k + 1) * rows] for u in range(2))
                            dst = PS[0:rows, 2 * m + i % banks, :]
                            nc.tensor.matmul(dst, w_up, upper[:, cols], start=True, stop=False)
                            nc.tensor.matmul(dst, w_up, x_low[:, cols], start=False, stop=False)
                            last = nc.tensor.matmul(dst, w_low, upper[:, cols], start=False, stop=True)
                        last.then_inc(h_psum.sem, 1)

                def output(n):
                    e = n // NG
                    if n % NG == 0:
                        pe.wait_ge(w_loaded[tag][w_third(tag, e)], 48 if gated else 32)
                    if n >= 2:
                        pe.wait_ge(y_used.sem, y_used.at(TG * (n - 1)))
                    pe.wait_ge(h_ready.sem, h_ready.at(chunks * (n + 1)))
                    for j in range(TG):
                        for k in range(chunks):
                            last = nc.tensor.matmul(PS[:, 6 + n % 2, j * P:j * P + P],
                                                    hT[0:rows, n % 2, k, j * P:j * P + P], w2[0:rows, e, k, :],
                                                    start=k == 0, stop=k == chunks - 1)
                    last.then_inc(y_psum.sem, 1)

                pe.wait_ge(x_first.sem, x_first.at(NG))
                hidden(0)
                for n in range(steps):
                    if n + 1 < steps:
                        hidden(n + 1)
                    output(n)
                if tag in w_done:
                    pe.wait_ge(y_used.sem, y_used.at(TG * steps))
                    pe.sem_inc(w_done[tag], 1)

            def scalar(a, st):
                for i in range(steps * chunks):
                    n, k = i // chunks, i % chunks
                    a.wait_ge(h_psum.sem, h_psum.at(i + 1))
                    if gated:
                        if i >= 2:
                            a.wait_ge(h_ready.sem, h_ready.at(i - 1))
                        nc.scalar.activation(gact[0:rows, i % 2, :], PS[0:rows, i % 2, :], c["act"]).then_inc(s_ready.sem, 1)
                    else:
                        if k == 0 and n >= 2:
                            a.wait_ge(y_psum.sem, y_psum.at(n - 1))
                        col = (n // NG) * chunks + k
                        nc.scalar.activation(hT[:, n % 2, k, :], PS[:, i % 4, :], c["act"],
                                             bias=pc(f"{tag}_b1")[:, col:col + 1]).then_inc(h_ready.sem, 1)

            def vector(v, st):
                def gate(n):
                    for k in range(chunks):
                        i = n * chunks + k
                        v.wait_ge(s_ready.sem, s_ready.at(i + 1))
                        if k == 0 and n >= 2:
                            v.wait_ge(y_psum.sem, y_psum.at(n - 1))
                        nc.vector.tensor_tensor(hT[0:rows, n % 2, k, :], gact[0:rows, i % 2, :], PS[0:rows, 2 + i % 2, :],
                                                ALU.mult).then_inc(h_ready.sem, 1)

                v.wait_ge(x_first.sem, x_first.at(NG))
                v.wait_ge(w_ready.sem, w_ready.at(1))
                if gated:
                    gate(0)
                for n in range(steps):
                    e, g = n // NG, n % NG
                    if gated and n + 1 < steps:
                        gate(n + 1)
                    v.wait_ge(y_psum.sem, y_psum.at(n + 1))
                    for j in range(TG):
                        t = TG * g + j
                        if n >= NG:
                            v.wait_ge(y_used.sem, y_used.at(TG * (n - NG) + j + 1))
                        nc.vector.scalar_tensor_tensor(X[:, t, :], PS[:, 6 + n % 2, j * P:j * P + P],
                                                       wts[:, t, e:e + 1], X[:, t, :], ALU.mult, ALU.add)\
                            .then_inc(y_used.sem, 1)
            def pool(p, st):
                def split_weights(e):
                    p.wait_ge(w_loaded[tag][w_third(tag, e)], 48 if gated else 32)
                    if e >= 2:
                        p.wait_ge(h_psum.sem, h_psum.at(chunks * NG * (e - 1)))
                    ws = [w1, w3] if gated else [w1]
                    for m, w in enumerate(ws):
                        nc.gpsimd.tensor_copy(halves[:, e % 2, m, 0, :], w[:, e, :]).then_inc(p_step, st.one())
                    p.wait_ge(p_step, st.n)
                    for m, w in enumerate(ws):
                        ins = nc.gpsimd.tensor_tensor(halves[:, e % 2, m, 1, :], w[:, e, :],
                                                      halves[:, e % 2, m, 0, :].bitcast(F32), ALU.subtract)
                        ins.then_inc(*((w_split.sem, 1) if w is ws[-1] else (p_step, st.one())))
                    p.wait_ge(p_step, st.n)

                split_weights(0)
                p.wait_ge(upper_ready.sem, upper_ready.at(NG))
                p.wait_ge(logits_read.sem, logits_read.at(1))
                for g in range(NG):
                    cols = slice(g * 512, g * 512 + 512)
                    nc.gpsimd.tensor_tensor(x_low[:, cols], xnT[:, cols], upper[:, cols].bitcast(F32), ALU.subtract)\
                        .then_inc(x_split.sem, 1)
                for e in range(1, n_e):
                    split_weights(e)
            return dict(tensor=tensor, vector=vector, scalar=scalar, pool=pool, x_done=y_used, base=TG * NG * (n_e - 1))

        stages = []

        def constants_vector(v, st):
            nc.vector.memset(vaug[:, :, :, HD:VW], 1.0).then_inc(v_step, st.one())
            nc.vector.memset(vaug[:, :, H:H + 1, 0:HD], 0.0).then_inc(v_step, st.one())
            nc.vector.memset(vfull[:, :, 3 * VW:], 0.0).then_inc(v_step, st.one())
            nc.vector.memset(mhalf[:, :], -0.5).then_inc(v_step, st.one())
            v.wait_ge(v_step, st.n)
            v.sem_inc(const_ready, 1)
            v.wait_ge(mask_loaded, 16)
            m = qb[:, 0:NT * K].bitcast(I32).rearrange("p (t k) -> p t k", t=NT)
            nc.vector.tensor_scalar(bound[:, :, :], m, 0, 3.0e38, ALU.not_equal, ALU.mult).then_inc(v_step, st.one())
            v.wait_ge(v_step, st.n)
            nc.vector.tensor_scalar(bound[:, :, :], bound[:, :, :], NEG, None, ALU.add).then_inc(v_step, st.one())
            v.wait_ge(v_step, st.n)

        def constants_pool(p, st):
            p.wait_ge(const_ready, 1)

        stages.append(dict(vector=constants_vector, pool=constants_pool))
        def loaded(v, t):
            if t % TG == 0:
                v.wait_ge(x_loaded[t // TG], 16)

        def tensor_start(pe):
            pe.wait_ge(par_in_1, 16)
        stages.append(dict(tensor=tensor_start))

        def after(sm, base=0):
            def x_is_ready(v, t):
                v.wait_ge(sm.sem, sm.at(base + t + 1))
            return x_is_ready

        def add(st):
            stages.append({k: st.get(k) for k in ("tensor", "vector", "scalar", "pool")})
            return st

        x_ready = loaded
        x_dones = []
        for layer in range(4):
            tag = f"L{layer}x"
            early, late, kv = kv_stages(tag)
            add(early)
            post = (pc("L3x_gamma"), pc("L3x_beta")) if layer == 3 else None
            if layer == 3:
                nm = add(norm_stage(tag, x_ready, "ln", post))
            else:
                nm = add(norm_stage(tag, x_ready))
            if layer == 0:
                add(late)
                at = add(attention_stage(tag, nm["ready"], 1, kv))
            else:
                pj = add(proj_stage(tag, nm["ready"]))
                kv["banks_read"] += [pj["used"], pj["projections"] * NG]
                add(late)
                at = add(single_stage(tag, pj["ready"], kv) if layer == 1 else
                         attention_stage(tag, pj["ready"], pj["per"], kv))
            x_dones.append(at["x_done"])
            x_ready = after(at["x_done"])
            tag = f"L{layer}f"
            if layer == 3:
                nm = add(norm_stage(tag, x_ready, "rms", (pc("L3f_rms"), 0.0)))
            else:
                nm = add(norm_stage(tag, x_ready))
            ro = add(route_stage(tag, nm["ready"]))
            ff = add(ffn_stage(tag, ro["x_first"], ro["w_ready"], nm["upper_ready"], ro["logits"]))
            x_ready = after(ff["x_done"], ff["base"])
        final = sem("x_final", NT)

        block = ctx.enter_context(nc.Block())

        @block.sync
        def _(sp):
            sync_program(sp, final, x_dones)

        @block.tensor
        def _(pe):
            for s in stages:
                if s.get("tensor"):
                    s["tensor"](pe)

        @block.vector
        def _(v):
            st = Steps()
            for s in stages:
                if s.get("vector"):
                    s["vector"](v, st)
            for t in range(NT):
                x_ready(v, t)
                v.sem_inc(final.sem, 1)

        @block.scalar
        def _(a):
            st = Steps()
            a.wait_ge(par_in_2, 16)
            for s in stages:
                if s.get("scalar"):
                    s["scalar"](a, st)

        @block.gpsimd
        def _(p):
            st = Steps()
            for s in stages:
                if s.get("pool"):
                    s["pool"](p, st)


def bilinear(n_in, n_out):
    scale = n_out / n_in
    inv = 1.0 / scale
    kernel_scale = max(inv, 1.0)
    at = (np.arange(n_out, dtype=np.float64) + 0.5) * inv - 0.5
    x = np.abs(at[None, :] - np.arange(n_in, dtype=np.float64)[:, None]) / kernel_scale
    w = np.maximum(0.0, 1.0 - x)
    total = w.sum(axis=0, keepdims=True)
    w = np.where(np.abs(total) > 1000.0 * np.finfo(np.float32).eps, w / np.where(total != 0, total, 1), 0)
    inside = (at >= -0.5) & (at <= n_in - 0.5)
    return np.where(inside[None, :], w, 0.0)


def tables():
    pos = np.arange(128, dtype=np.float64)
    dist = np.abs(pos[None, :] - pos[:, None])
    bias = np.exp(-dist * 0.1) - dist * 0.05
    tb = bilinear(128, S).T @ bias @ bilinear(128, K)
    tb = tb.reshape(TG, P, K).transpose(1, 0, 2).reshape(P, TG * K).astype(np.float32)
    half = HD // 2
    inv = (1.0 / np.float32(10000.0) ** (np.arange(0, HD, 2, dtype=np.float32) / np.float32(HD))).astype(np.float32)
    ang = (np.arange(S, dtype=np.float32)[:, None] * inv[None, :]).astype(np.float32).astype(np.float64)
    d = np.arange(P) % HD
    cos = np.cos(ang)[:, d % half].T
    sin = np.sin(ang)[:, d % half].T * np.where(d < half, -1.0, 1.0)[:, None]
    heads = np.arange(P)[:, None] // HD == np.arange(H)[None, :]
    hmask = np.concatenate([(np.arange(P)[:, None] + j * P) // K == h0 + np.arange(min(3, NHM - 3 * j))[None, :]
                            for j, (h0, _, _) in enumerate(BLOCKS)], axis=1)
    wrap = np.arange(K + P)[None, :] % K == np.arange(K)[:, None]
    before = np.arange(P)[:, None] < np.arange(P)[None, :]
    return dict(ident=np.eye(P), heads=heads, headsc=heads * float(HD) ** -0.5, hmask=hmask, wrap=wrap, before=before, ones=np.ones((P, P)), cos=cos, sin=sin, tbias=tb,
                iota=np.tile(np.arange(E), (P, 1)))


def rotated_rows(w):
    return np.concatenate([w.reshape(H, 2, HD // 2, D)[:, 1:2], w.reshape(H, 2, HD // 2, D)[:, 0:1]], axis=1).reshape(D, D)


def kernel(**inp):
    import concourse.bacc as bacc
    from concourse.bass_utils import run_bass_kernel_spmd

    a = {k: np.asarray(v) for k, v in inp.items()}

    def row(v):
        return np.broadcast_to(v.reshape(1, -1), (P, v.size))

    def col(v):
        return v.reshape(-1, 1)

    def chunks(b, n):
        return b.reshape(b.shape[0], n, P).transpose(2, 0, 1).reshape(P, -1)

    ctx = a["ctx_1024"]
    kv1, kv2, qkv = a["L2_xattn_kv1_w"], a["L2_xattn_kv2_w"], a["L3_xattn_Wqkv"]
    L1b1 = np.concatenate([a["L1_ffn_rb1"], a["L1_ffn_sb1"][None]], 0)
    L1b2 = np.concatenate([a["L1_ffn_rb2"], a["L1_ffn_sb2"][None]], 0)
    p = dict(tables())
    p.update(
        ctxT=ctx.transpose(2, 0, 1).reshape(D, B * K), ctx=ctx.transpose(1, 0, 2).reshape(K, B * D),
        L0x_wo=a["L0_xattn_W_out"].T, L0x_bo=row(a["L0_xattn_b_out"]),
        L0f_wr=a["L0_ffn_Wr"], L0f_br=row(a["L0_ffn_br"]), L0f_b1=chunks(a["L0_ffn_b1"], 4), L0f_b2=a["L0_ffn_b2"],
        L1x_wq=a["L1_xattn_W_q"], L1x_wk=a["L1_xattn_W_k"], L1x_wv=a["L1_xattn_W_v"],
        L1x_bq=col(a["L1_xattn_b_q"]), L1x_bk=col(a["L1_xattn_b_k"]), L1x_bv=row(a["L1_xattn_b_v"]),
        L1f_wr=a["L1_ffn_router_w"], L1f_br=row(a["L1_ffn_router_b"]), L1f_b1=chunks(L1b1, 2), L1f_b2=L1b2,
        L2x_q1=a["L2_xattn_q1_w"].T, L2x_q2=a["L2_xattn_q2_w"].T, L2x_k1=kv1[:D].T, L2x_v1=kv1[D:].T,
        L2x_k2=kv2[:D].T, L2x_wo=a["L2_xattn_proj_w"].T, L2x_bo=row(a["L2_xattn_proj_b"]),
        L2x_norm=col(a["L2_xattn_norm_w"]), L2x_lam1=row(a["L2_xattn_lambda_1"]), L2x_lam2=row(a["L2_xattn_lambda_2"]),
        L2f_wr=a["L2_ffn_Wg"], L2f_br=row(a["L2_ffn_bg"]), L2f_b1=chunks(a["L2_ffn_b1"], 4), L2f_b2=a["L2_ffn_b2"],
        L3x_q=qkv[:D].T, L3x_qr=rotated_rows(qkv[:D]).T, L3x_k=qkv[D:2 * D].T, L3x_kr=rotated_rows(qkv[D:2 * D]).T,
        L3x_v=qkv[2 * D:].T, L3x_wo=a["L3_xattn_Wout"].T, L3x_bo=row(a["L3_xattn_b_out"]),
        L3x_boc=col(a["L3_xattn_b_out"]), L3x_wg=a["L3_xattn_Wgate"].T, L3x_bg=row(a["L3_xattn_b_gate"]),
        L3x_gamma=col(a["L3_xattn_gamma"]), L3x_beta=col(a["L3_xattn_beta"]),
        L3f_rms=col(a["L3_ffn_rms_weight"]), L3f_wr=a["L3_ffn_gate_w"].T,
    )
    pack = np.zeros((P, NPAR), np.float32)
    for name, (at, n) in COLUMN.items():
        v = np.asarray(p[name], np.float32)
        pack[:v.shape[0], at:at + n] = v

    def first(w):
        return np.ascontiguousarray(w.transpose(1, 0, 2))

    def second(w, n):
        e, h, d = w.shape
        return np.ascontiguousarray(w.reshape(e, n, h // n, d).transpose(2, 0, 1, 3))

    w = {
        "L0f": [first(a["L0_ffn_W1"]), second(a["L0_ffn_W2"], 4)],
        "L1f": [first(np.concatenate([a["L1_ffn_rw1"], a["L1_ffn_sw1"][None]], 0)),
                second(np.concatenate([a["L1_ffn_rw2"], a["L1_ffn_sw2"][None]], 0), 2)],
        "L2f": [first(a["L2_ffn_W1"]), second(a["L2_ffn_W2"], 4)],
        "L3f": [first(a["L3_ffn_w1"].transpose(0, 2, 1)), second(a["L3_ffn_w2"].transpose(0, 2, 1), 4),
                first(a["L3_ffn_w3"].transpose(0, 2, 1))],
    }
    arrays = {
        "x_tiles": np.ascontiguousarray(a["x"].reshape(NT, P, D).transpose(1, 0, 2)),
        "params": pack,
        "mask": np.ascontiguousarray(a["mask_Bx1xSxS2_if1"].reshape(NT, P, K).transpose(1, 0, 2).reshape(P, NT * K)),
    }
    for f, ws in w.items():
        for i, m in enumerate(ws):
            arrays[f"{f}_w{i}"] = m

    nc = bacc.Bacc("TRN2", target_bir_lowering=False, num_devices=1)
    aps = {k: nc.dram_tensor(k, v.shape, mybir.dt.from_np(v.dtype), kind="ExternalInput").ap() for k, v in arrays.items()}
    out = nc.dram_tensor("x_out", (P, NT, D), F32, kind="ExternalOutput").ap()
    build(nc, aps["x_tiles"], aps["params"], aps["mask"],
          {f: [aps[f"{f}_w{i}"] for i in range(len(ws))] for f, ws in w.items()}, out)
    r = run_bass_kernel_spmd(nc, [arrays], core_ids=[0])
    got = r.results[0]["x_out"]
    return np.ascontiguousarray(got.reshape(P, NT, D).transpose(1, 0, 2)).reshape(B, S, D)
```

```python
from contextlib import ExitStack

import numpy as np

import concourse.bass as bass
from concourse import mybir

F32 = mybir.dt.float32
F32R = mybir.dt.float32r
I32 = mybir.dt.int32
ALU = mybir.AluOpType
ACT = mybir.ActivationFunctionType
AX = mybir.AxisListType

P = 128
B, S, K, D = 4, 512, 77, 128
NT = B * S // P
TG = S // P
NG = NT // TG
H, HD = 16, D // 16
RG, HR = 4, 4
E = 8
LN_EPS = 1e-5
RMS_EPS = 1e-6
CAPACITY = 615
NEG = -1.0e20

NBLK = -(-H * K // P)
BLOCKS = []
for _j in range(NBLK):
    _n = min(P, H * K - _j * P)
    _h = _j * P // K
    BLOCKS.append((_h, (_j * P + _n - 1) // K - _h + 1, _n))
VW = HD + 1
NHM = 3 * (NBLK - 1) + BLOCKS[-1][1]
VB = 12
VB_COLUMNS = [min(VB, NHM - i) for i in range(0, NHM, VB)]

PARAMS = [
    ("ident", 128), ("heads", H), ("hmask", NHM), ("wrap", K + P), ("ctxT", B * K), ("ctx", B * D), ("L0x_wo", D), ("L0x_bo", D),
    ("iota", E), ("L0f_wr", E), ("L0f_br", E), ("L0f_b1", 32), ("L0f_b2", D),
    ("L1x_wq", D), ("L1x_wk", D), ("L1x_wv", D), ("L1x_bq", 1), ("L1x_bk", 1), ("L1x_bv", D),
    ("L1f_wr", E), ("L1f_br", E), ("L1f_b1", 18), ("L1f_b2", D),
    ("L2x_q1", D), ("L2x_q2", D), ("L2x_k1", D), ("L2x_v1", D), ("L2x_k2", D), ("L2x_wo", D),
    ("L2x_bo", D), ("L2x_norm", 1), ("L2x_lam1", H), ("L2x_lam2", H),
    ("L2f_wr", E), ("L2f_br", E), ("L2f_b1", 32), ("L2f_b2", D), ("before", P), ("ones", P),
    ("L3x_q", D), ("L3x_qr", D), ("L3x_k", D), ("L3x_kr", D), ("L3x_v", D), ("L3x_wo", D),
    ("L3x_bo", D), ("L3x_boc", 1), ("L3x_wg", D), ("L3x_bg", D), ("L3x_gamma", 1), ("L3x_beta", 1),
    ("headsc", H), ("cos", S), ("sin", S), ("tbias", TG * K), ("L3f_rms", 1), ("L3f_wr", E),
]
COLUMN = {}
_at = 0
for _name, _n in PARAMS:
    COLUMN[_name] = (_at, _n)
    _at += _n
NPAR = _at
NPAR_FIRST = COLUMN["iota"][0]

FFNS = {
    "L0f": dict(experts=8, chunks=4, rows=128, gated=False, act=ACT.Gelu),
    "L1f": dict(experts=9, chunks=2, rows=128, gated=False, act=ACT.Gelu),
    "L2f": dict(experts=8, chunks=4, rows=128, gated=False, act=ACT.Gelu_apprx_tanh),
    "L3f": dict(experts=8, chunks=4, rows=112, gated=True, act=ACT.Silu),
}


def build(nc, x_in, par_in, mask_in, w_in, out):
    ctx = ExitStack()

    def sb(name, shape, dt=F32):
        return ctx.enter_context(nc.sbuf_tensor(name, shape, dt))

    def under(name, widths, skip=()):
        with ExitStack() as freed:
            tensors = []
            for i, n in enumerate(widths):
                if i < len(skip) and skip[i]:
                    freed.enter_context(nc.sbuf_tensor(f"{name}_skip{i}", [P, skip[i]], F32))
                tensors.append(freed.enter_context(nc.sbuf_tensor(f"{name}{i}", [P, n], F32R)))
            return tensors

    def plain_sem(name):
        return ctx.enter_context(nc.semaphore(name))

    roles = {}

    class Signal:
        def __init__(self, role, total):
            sm, base = roles.get(role) or (ctx.enter_context(nc.semaphore(role)), 0)
            self.sem, self.base, self.total = sm, base, total
            roles[role] = (sm, base + total)

        def at(self, n):
            return self.base + n

    def sem(name, total=1):
        return Signal(name, total)


    with ctx:
        X = sb("X", [P, NT, D])
        q2_low = under("q2_low", [NT * P])[0]
        xn = sb("xn", [P, NT, D])
        x_low = under("x_low", [NT * P])[0]
        xnT = sb("xnT", [P, NT * P])
        x_up = under("x_up", [NT * P])[0]
        qa = sb("qa", [P, NT * P])
        q2_up = under("q2_up", [NT * P])[0]
        qb = sb("qb", [P, NT * P])
        par = sb("par", [P, NPAR])
        score = sb("score", [P, 3, H, K])
        hT = sb("hT", [P, 2, 4, 512])
        gact = score[:, 0, :, :].rearrange("p h k -> p (h k)")[:, 0:1024].rearrange("p (a n) -> p a n", a=2)
        kb_3 = under("kb_3", [4 * H * K])[0]
        w_halves_3, x_up_3 = under("gated", [8 * 4 * 112, NT * P], skip=[0, 4 * H * K - 8 * 4 * 112])
        regA = sb("regA", [P, 8192])
        kb_0 = under("kb_0", [4 * H * K], skip=[4096])[0]
        kb_2 = under("kb_2", [8 * H * K])[0]
        w_halves = under("w_halves", [4 * 512], skip=[4096 + 4 * H * K])[0]
        regB = sb("regB", [P, 11264])
        kb_of = {tag: kb[:, :].rearrange("p (s b u h k) -> p s b u h k", b=2, u=2, h=H, k=K)
                 for tag, kb in (("L0x", kb_0), ("L2x", kb_2), ("L3x", kb_3))}
        halves_of = {"L0x": regB[:, NT * K:4096], "L2x": regB[:, 8 * H * K:], "L3x": regA[:, 4 * H * K:]}
        vaug = sb("vaug", [K, B, H + 1, VW])
        vblk = sb("vblk", [P, B, NHM * VW])
        vfull = sb("vfull", [P, B, H * VW])
        k1T = sb("k1T", [P, B * K])
        k2T = sb("k2T", [P, B * K])
        k3T = sb("k3T", [P, B * D])
        v1 = k3T[0:K, :].rearrange("k (b d) -> k b d", b=B)
        bound = regB[:, 0:NT * K].rearrange("p (t k) -> p t k", t=NT)
        stats = sb("stats", [P, NT, 6])
        mv = sb("mv", [P, NT, 2])
        rstd = sb("rstd", [P, NT])
        vare = sb("vare", [P, NT])
        mhalf = sb("mhalf", [P, NT])
        mx = sb("mx", [P, 3, H])
        rec = sb("rec", [P, 2, H])
        lam = sb("lam", [P, H])
        oc = sb("oc", [P, 2, D])
        oc2 = sb("oc2", [P, 2, D])
        oss = sb("oss", [P, 2])
        osr = sb("osr", [P, 2])
        ocT = sb("ocT", [P, 2, P])
        attT = sb("attT", [P, 2, P])
        fin = sb("fin", [P, 5, D])
        gin = sb("gin", [P, 2, D])
        gdiff = sb("gdiff", [P, 2, D])
        free = score[:, 1:3, :, :].rearrange("p u h k -> p (u h k)")
        rt = free[:, 0:8 * NT * E].rearrange("p (a t e) -> p a t e", a=8, t=NT)
        rc = free[:, 8 * NT * E:12 * NT * E].rearrange("p (a t e) -> p a t e", a=2, t=2 * NT)
        rs = sb("rs", [P, 6, 2 * NT])
        wts = sb("wts", [P, NT, 9])
        ctxn = score[0:K, 0, :, :].rearrange("p h k -> p (h k)")[:, 0:B * D].rearrange("p (b d) -> p b d", b=B)
        PS = ctx.enter_context(nc.psum_tensor("PS", [P, 8, 512], F32))

        def pc(name, rows=P):
            at, n = COLUMN[name]
            return par[0:rows, at:at + n]

        ident = pc("ident")

        par_in_1 = plain_sem("par_first_loaded")
        par_in_2 = plain_sem("par_rest_loaded")
        x_loaded = [plain_sem(f"x_loaded{g}") for g in range(NG)]
        mask_loaded = plain_sem("mask_loaded")
        w_loaded = {f: [plain_sem(f"{f}_w_loaded{i}") for i in range(3)] for f in FFNS}
        w_done = {f: plain_sem(f"{f}_experts_done") for f in ("L0f", "L2f")}
        stored = plain_sem("stored")
        v_step = plain_sem("vector_step")
        p_step = plain_sem("pool_step")
        a_step = plain_sem("scalar_step")
        const_ready = plain_sem("const_ready")

        class Steps:
            def __init__(self):
                self.n = 0

            def one(self):
                self.n += 1
                return 1

        def w_third(f, e):
            return min(2, e * 3 // FFNS[f]["experts"])

        def third(f, i):
            n = FFNS[f]["experts"]
            es = [e for e in range(n) if w_third(f, e) == i]
            return es[0], es[-1] + 1

        def views(f):
            c = FFNS[f]
            reg = {"L0f": regA, "L1f": regB, "L2f": regA, "L3f": regB}[f]
            n, hid = c["experts"], c["chunks"] * c["rows"]
            a = n * hid
            w1 = reg[:, 0:a].rearrange("p (e h) -> p e h", e=n)
            w3 = reg[:, a:2 * a].rearrange("p (e h) -> p e h", e=n) if c["gated"] else None
            o = 2 * a if c["gated"] else a
            w2 = reg[:, o:o + n * c["chunks"] * D].rearrange("p (e c d) -> p e c d", e=n, c=c["chunks"])
            return w1, w3, w2

        def split_space(f):
            hid = FFNS[f]["chunks"] * FFNS[f]["rows"]
            if f == "L3f":
                return x_up_3, w_halves_3[:, :].rearrange("p (b m u h) -> p b m u h", b=2, m=2, u=2)
            return x_up, w_halves[:, 0:4 * hid].rearrange("p (b m u h) -> p b m u h", b=2, m=1, u=2)

        def sync_program(sp, last_x_done, x_dones):
            for g in range(NG):
                if g == 1:
                    sp.dma_start(par[:, 0:NPAR_FIRST], par_in[:, 0:NPAR_FIRST]).then_inc(par_in_1, 16)
                sp.dma_start(X[:, TG * g:TG * g + TG, :], x_in[:, TG * g:TG * g + TG, :]).then_inc(x_loaded[g], 16)
            sp.dma_start(qb[:, 0:NT * K].bitcast(I32), mask_in).then_inc(mask_loaded, 16)
            sp.dma_start(par[:, NPAR_FIRST:NPAR], par_in[:, NPAR_FIRST:NPAR]).then_inc(par_in_2, 16)
            for f in ("L0f", "L1f", "L2f", "L3f"):
                if f == "L1f":
                    sp.wait_ge(x_dones[0].sem, x_dones[0].at(NT))
                if f == "L2f":
                    sp.wait_ge(w_done["L0f"], 1)
                if f == "L3f":
                    sp.wait_ge(w_done["L2f"], 1)
                w1, w3, w2 = views(f)
                rows = FFNS[f]["rows"]
                for i in range(3):
                    e0, e1 = third(f, i)
                    sp.dma_start(w1[:, e0:e1, :], w_in[f][0][:, e0:e1, :]).then_inc(w_loaded[f][i], 16)
                    if w3 is not None:
                        sp.dma_start(w3[:, e0:e1, :], w_in[f][2][:, e0:e1, :]).then_inc(w_loaded[f][i], 16)
                    sp.dma_start(w2[0:rows, e0:e1, :, :], w_in[f][1][:, e0:e1, :, :]).then_inc(w_loaded[f][i], 16)
            for g in range(NG):
                sp.wait_ge(last_x_done.sem, last_x_done.at(TG * (g + 1)))
                sp.dma_start(out[:, TG * g:TG * g + TG, :], X[:, TG * g:TG * g + TG, :]).then_inc(stored, 16)
            sp.wait_ge(stored, 16 * NG)

        kv_first = {}

        def kv_stage(tag):
            multi = tag != "L1x"
            first_k, n_v, first_vb = {"L0x": (0, 0, 1), "L1x": (0, 1, 2), "L2x": (0, 2, 3), "L3x": (1, 3, 4)}[tag]
            total = first_vb + (len(VB_COLUMNS) if multi else 0)
            in_psum = total - (tag == "L0x")
            kv_psum = sem("kv_psum", in_psum)
            kv_read = sem("kv_read", total)
            if tag == "L3x":
                kT_ready = sem("keys_rotated")
                c_ready = sem("ctx_normalised")
                s_var = sem("ctx_variance")
                s_rstd = sem("ctx_rstd")
            keysT = {"L0x": [pc("ctxT")], "L1x": [k1T[:, :]], "L2x": [k1T[:, :], k2T[:, :]], "L3x": [k2T[:, :]]}[tag]
            keysW = {"L0x": [], "L1x": ["L1x_wk"], "L2x": ["L2x_k1", "L2x_k2"], "L3x": ["L3x_k", "L3x_kr"]}[tag]
            valuesW = {"L0x": None, "L1x": "L1x_wv", "L2x": "L2x_v1", "L3x": "L3x_v"}[tag]
            ctxT = k1T[:, :] if tag == "L3x" else pc("ctxT")

            def bank(i):
                return i - 1 if tag == "L0x" else 6 + i % 2

            def tensor_ctx(pe):
                pe.wait_ge(c_ready.sem, c_ready.at(1))
                for b in range(B):
                    last = nc.tensor.transpose(PS[:, bank(0), b * K:b * K + K], ctxn[:, b, :], ident[0:K, 0:K])
                last.then_inc(kv_psum.sem, 1)

            def tensor_keys(pe):
                if first_k:
                    pe.wait_ge(kv_read.sem, kv_read.at(first_k))
                for i, w in enumerate(keysW):
                    nc.tensor.matmul(PS[:, bank(first_k + i), 0:B * K], pc(w), ctxT, start=True, stop=True)\
                        .then_inc(kv_psum.sem, 1)

            def tensor_values(pe):
                if n_v >= 2:
                    pe.wait_ge(kv_read.sem, kv_read.at(n_v - 1))
                for b in range(B):
                    last = nc.tensor.matmul(PS[0:K, bank(n_v), b * D:b * D + D], ctxT[:, b * K:b * K + K], pc(valuesW),
                                            start=True, stop=True)
                last.then_inc(kv_psum.sem, 1)

            def tensor_blocks(pe, which):
                pe.wait_ge(kv_read.sem, kv_read.at(n_v + 1))
                for i in which:
                    n = first_vb + i
                    if n >= 2 and tag != "L0x":
                        pe.wait_ge(kv_read.sem, kv_read.at(n - 1))
                    dst = PS[:, bank(n), 0:B * VB * VW].rearrange("p (b c) -> p b c", b=B)
                    for j in range(4 * i, min(4 * i + 4, NBLK)):
                        h0, at = BLOCKS[j][0], j * P % K
                        w = min(3, NHM - 3 * j)
                        last = nc.tensor.matmul(dst[:, :, 3 * (j % 4) * VW:(3 * (j % 4) + w) * VW],
                                                pc("wrap", K)[:, at:at + P],
                                                vaug[:, :, h0:h0 + w, :].rearrange("k b n w -> k b (n w)"),
                                                start=True, stop=True)
                    last.then_inc(kv_psum.sem, 1)

            def scalar_ctx(a, st):
                a.wait_ge(kv_psum.sem, kv_psum.at(1))
                nc.scalar.activation(k1T[:, :], PS[:, bank(0), 0:B * K], ACT.Identity, scale=pc("L3x_gamma"),
                                     bias=pc("L3x_beta")).then_inc(kv_read.sem, 1)

            def pool_ctx(p, st):
                p.wait_ge(s_var.sem, s_var.at(1))
                nc.gpsimd.tensor_scalar(rs[0:K, 2, 0:B], rs[0:K, 0, 0:B], LN_EPS, None, ALU.add).then_inc(p_step, st.one())
                p.wait_ge(p_step, st.n)
                nc.gpsimd.tensor_tensor(rs[0:K, 1, 0:B], rs[0:K, 2, 0:B], mhalf[0:K, 0:B], ALU.pow)\
                    .then_inc(s_rstd.sem, 1)

            def vector_ctx(v, st):
                for b in range(B):
                    nc.vector.bn_stats(stats[0:K, b, :], pc("ctx", K)[:, b * D:b * D + D]).then_inc(v_step, st.one())
                v.wait_ge(v_step, st.n)
                for b in range(B):
                    nc.vector.bn_aggr(mv[0:K, b, :], stats[0:K, b, :]).then_inc(v_step, st.one())
                v.wait_ge(v_step, st.n)
                nc.vector.tensor_copy(rs[0:K, 0, 0:B], mv[0:K, 0:B, 1]).then_inc(s_var.sem, 1)
                v.wait_ge(s_rstd.sem, s_rstd.at(1))
                for b in range(B):
                    nc.vector.tensor_scalar(ctxn[:, b, :], pc("ctx", K)[:, b * D:b * D + D], mv[0:K, b, 0:1],
                                            rs[0:K, 1, b:b + 1], ALU.subtract, ALU.mult).then_inc(v_step, st.one())
                v.wait_ge(v_step, st.n)
                v.sem_inc(c_ready.sem, 1)

            def vector_keys(v, st):
                for i, w in enumerate(keysW):
                    n = first_k + i
                    src = PS[:, bank(n), 0:B * K]
                    v.wait_ge(kv_psum.sem, kv_psum.at(n + 1))
                    if tag == "L1x":
                        nc.vector.tensor_scalar(k1T[:, :], src, pc("L1x_bk"), None, ALU.add).then_inc(kv_read.sem, 1)
                    elif tag == "L2x":
                        nc.vector.tensor_copy((k1T, k2T)[i][:, :], src).then_inc(kv_read.sem, 1)
                    else:
                        nc.vector.tensor_tensor((k2T, k3T)[i][:, 0:B * K].rearrange("p (b k) -> p b k", b=B),
                                                src.rearrange("p (b k) -> p b k", b=B),
                                                pc(("cos", "sin")[i])[:, 0:K].unsqueeze(1).to_broadcast([P, B, K]),
                                                ALU.mult).then_inc(kv_read.sem, 1)
                if tag == "L3x":
                    v.wait_ge(kv_read.sem, kv_read.at(first_k + 2))
                    nc.vector.tensor_tensor(k2T[:, :], k2T[:, :], k3T[:, 0:B * K], ALU.add).then_inc(kT_ready.sem, 1)

            def vector_values(v, st):
                if tag == "L0x":
                    v.wait_ge(par_in_1, 16)
                else:
                    v.wait_ge(kv_psum.sem, kv_psum.at(n_v + 1))
                if tag == "L1x":
                    nc.vector.tensor_tensor(v1[:, :, :], PS[0:K, bank(n_v), :].rearrange("k (b d) -> k b d", b=B),
                                            pc("L1x_bv", K).unsqueeze(1).to_broadcast([K, B, D]), ALU.add)\
                        .then_inc(kv_read.sem, 1)
                    return
                for b in range(B):
                    src = (pc("ctx", K) if tag == "L0x" else PS[0:K, bank(n_v), :])[:, b * D:b * D + D]
                    nc.vector.tensor_copy(vaug[:, b, 0:H, 0:HD], src.rearrange("k (h d) -> k h d", h=H))\
                        .then_inc(v_step, st.one())
                v.wait_ge(v_step, st.n)
                v.sem_inc(kv_read.sem, 1)

            def vector_blocks(v, st, which):
                for i in which:
                    n, width = first_vb + i, VB_COLUMNS[i]
                    v.wait_ge(kv_psum.sem, kv_psum.at(in_psum - total + n + 1))
                    by_block = PS[:, bank(n), 0:B * VB * VW].rearrange("p (b n w) -> p b n w", b=B, w=VW)
                    ms = pc("hmask")[:, VB * i:VB * i + width].unsqueeze(1).unsqueeze(3)
                    if i == 0:
                        nc.vector.tensor_tensor(vfull[:, :, 0:3 * VW].rearrange("p b (n w) -> p b n w", w=VW),
                                                by_block[:, :, 0:3, :], ms[:, :, 0:3, :].to_broadcast([P, B, 3, VW]),
                                                ALU.mult).then_inc(v_step, st.one())
                        v.wait_ge(v_step, st.n)
                    dst = vblk[:, :, VB * i * VW:(VB * i + width) * VW].rearrange("p b (n w) -> p b n w", w=VW)
                    nc.vector.tensor_tensor(dst, by_block[:, :, 0:width, :], ms.to_broadcast([P, B, width, VW]), ALU.mult)\
                        .then_inc(kv_read.sem, 1)

            parts = {}

            def part(step, **engines):
                for engine, f in engines.items():
                    parts.setdefault(engine, {})[step] = f

            if tag == "L3x":
                part(6, vector=vector_ctx)
                part(8, tensor=tensor_ctx)
                part(10, scalar=scalar_ctx)
            part(10, tensor=tensor_keys, vector=vector_keys)
            part(12, tensor=tensor_values, vector=vector_values)
            if multi:
                part(14, tensor=lambda pe: tensor_blocks(pe, (0, 1)), vector=lambda v, st: vector_blocks(v, st, (0, 1)))
                part(16, tensor=lambda pe: tensor_blocks(pe, (2,)), vector=lambda v, st: vector_blocks(v, st, (2,)))

            def tensor_start(pe):
                tensor_blocks(pe, (0, 1, 2))

            def vector_start(v, st):
                vector_values(v, st)
                for g in range(NG):
                    cols = slice(g * 512, g * 512 + 512)
                    v.wait_ge(kv_first["upper"].sem, kv_first["upper"].at(g + 1))
                    nc.vector.tensor_tensor(x_low[:, cols], xnT[:, cols], x_up[:, cols].bitcast(F32), ALU.subtract)\
                        .then_inc(kv_first["q_ready"].sem, 1)
                vector_blocks(v, st, (0, 1, 2))

            keys_ready = {"L0x": (kv_read, 1), "L1x": (kv_read, 1), "L2x": (kv_read, 2)}.get(tag)
            return dict(parts=parts, pool=pool_ctx if tag == "L3x" else None, tensor_start=tensor_start,
                        vector_start=vector_start, keysT=keysT, kT_ready=keys_ready or (kT_ready, 1),
                        all_read=(kv_read, total))

        def norm_stage(tag, x_ready, second=None, post=None, before=None):
            levels = 2 if second else 1
            var_ready = sem("var", levels * NG)
            rstd_ready = sem("rstd", levels * NG)
            xn_ready = sem("xn", NT)
            xT_psum = sem("xT_psum", NG)
            xT_ready = sem("xT", NG)
            upper = split_space(tag)[0] if tag in FFNS else x_up if tag == "L0x" else None
            upper_ready = sem("x_upper", NG) if upper is not None else None

            order = [(level, g) for level in range(levels) for g in range(NG)]
            if before == "ffn":
                order.sort(key=lambda level_g: level_g[1])
            bank = 6 if before == "ffn" else 0 if tag == "L1f" else 4
            taken = {None: 0, "attention": NG - 1, "ffn": NG}[before]

            def vector_functions(v, st):
                def statistics(level, g):
                    for t in range(TG * g, TG * g + TG):
                        if level == 0:
                            x_ready(v, t)
                            src = X[:, t, :]
                        else:
                            src = xn[:, t, :]
                        if level and second == "rms":
                            nc.vector.scalar_tensor_tensor(fin[:, t % 4, :], src, 1.0, src, ALU.mult, ALU.mult,
                                                                 accum_out=mv[:, t, 1:2]).then_inc(v_step, st.one())
                        else:
                            nc.vector.bn_stats(stats[:, t, :], src).then_inc(v_step, st.one())
                    v.wait_ge(v_step, st.n)
                    if level and second == "rms":
                        nc.vector.tensor_scalar(vare[:, TG * g:TG * g + TG], mv[:, TG * g:TG * g + TG, 1], 1.0 / D,
                                                RMS_EPS, ALU.mult, ALU.add).then_inc(var_ready.sem, 1)
                        return
                    for t in range(TG * g, TG * g + TG):
                        nc.vector.bn_aggr(mv[:, t, :], stats[:, t, :]).then_inc(v_step, st.one())
                    v.wait_ge(v_step, st.n)
                    nc.vector.tensor_scalar(vare[:, TG * g:TG * g + TG], mv[:, TG * g:TG * g + TG, 1], LN_EPS, None,
                                            ALU.add).then_inc(var_ready.sem, 1)

                def apply(level, g):
                    v.wait_ge(rstd_ready.sem, rstd_ready.at(order.index((level, g)) + 1))
                    for t in range(TG * g, TG * g + TG):
                        src = X[:, t, :] if level == 0 else xn[:, t, :]
                        dst = xn[:, t, :] if level == 0 else qa[:, t * D:t * D + D]
                        if level and second == "rms":
                            ins = nc.vector.tensor_scalar(dst, src, rstd[:, t:t + 1], None, ALU.mult)
                        else:
                            ins = nc.vector.tensor_scalar(dst, src, mv[:, t, 0:1], rstd[:, t:t + 1],
                                                          ALU.subtract, ALU.mult)
                        if level == levels - 1:
                            ins.then_inc(xn_ready.sem, 1)
                        else:
                            ins.then_inc(v_step, st.one())

                return statistics, apply

            def vector_tile(v, st, t):
                statistics, apply = vector_functions(v, st)
                if t % TG == TG - 1 and t < NT - 1:
                    statistics(0, t // TG)
                if t % TG == 0 and t:
                    apply(0, t // TG - 1)

            def vector_group(v, st, g):
                statistics, apply = vector_functions(v, st)
                for level in range(levels):
                    if level:
                        v.wait_ge(v_step, st.n)
                    statistics(level, g)
                    apply(level, g)

            def vector(v, st):
                statistics, apply = vector_functions(v, st)
                for level in range(levels if taken < NG else 0):
                    first = 0 if level else taken
                    if level:
                        v.wait_ge(v_step, st.n)
                    for g in range(first, NG + 1):
                        if g < NG:
                            statistics(level, g)
                        if g > first:
                            apply(level, g - 1)

            def pool_group(p, level, g):
                c = slice(TG * g, TG * g + TG)
                p.wait_ge(var_ready.sem, var_ready.at(order.index((level, g)) + 1))
                nc.gpsimd.tensor_tensor(rstd[:, c], vare[:, c], mhalf[:, c], ALU.pow).then_inc(rstd_ready.sem, 1)

            def pool(p, st):
                for level, g in order[taken if before == "attention" else 0:]:
                    pool_group(p, level, g)

            def transpose_group(pe, g):
                pe.wait_ge(xn_ready.sem, xn_ready.at(TG * (g + 1)))
                if g >= 2:
                    read = upper_ready or xT_ready
                    pe.wait_ge(read.sem, read.at(g - 1))
                for j in range(TG):
                    t = TG * g + j
                    src = xn[:, t, :] if levels == 1 else qa[:, t * D:t * D + D]
                    last = nc.tensor.transpose(PS[:, bank + g % 2, j * P:j * P + P], src, ident)
                last.then_inc(xT_psum.sem, 1)

            def tensor(pe, route=None):
                for g in range(NG - 1 if before == "ffn" else 0, NG):
                    transpose_group(pe, g)
                    if route and g:
                        route(pe, g - 1)
                if route:
                    route(pe, NG - 1)

            def scalar(a, st):
                for g in range(NG):
                    a.wait_ge(xT_psum.sem, xT_psum.at(g + 1))
                    cols = slice(g * 512, g * 512 + 512)
                    scale, bias = post or (1.0, 0.0)
                    nc.scalar.activation(xnT[:, cols], PS[:, bank + g % 2, :], ACT.Identity, scale=scale,
                                         bias=bias).then_inc(xT_ready.sem, 1)
                    if upper is not None:
                        nc.scalar.activation(upper[:, cols], PS[:, bank + g % 2, :], ACT.Identity,
                                             scale=scale, bias=bias).then_inc(upper_ready.sem, 1)
            return dict(vector=vector, pool=pool, tensor=tensor, scalar=scalar, ready=xT_ready, upper_ready=upper_ready,
                        vector_tile=vector_tile, vector_group=vector_group, pool_group=pool_group,
                        transpose_group=transpose_group)

        def proj_stage(tag, xT_ready):
            ws = {"L1x": ["L1x_wq"], "L2x": ["L2x_q1", "L2x_q2"], "L3x": ["L3x_q", "L3x_qr"]}[tag]
            n = len(ws)
            q_psum = sem("q_psum", n * NG)
            q_used = sem("q_rotated" if tag == "L3x" else "q_copied", n * NG)
            q_up = sem("q_upper", {"L1x": 0, "L2x": 2 * NG, "L3x": NG}[tag])
            q_sum = sem("q_sum", NG if tag == "L3x" else 0)
            q_ready = sem("q_ready", NG if tag == "L3x" else 0)

            def tensor(pe):
                for g in range(NG):
                    pe.wait_ge(xT_ready.sem, xT_ready.at(g + 1))
                    for s in range(n):
                        i = n * g + s
                        if i >= 2:
                            pe.wait_ge(q_used.sem, q_used.at(i - 1))
                        nc.tensor.matmul(PS[:, 4 + i % 2, :], pc(ws[s]), xnT[:, g * 512:g * 512 + 512],
                                         start=True, stop=True).then_inc(q_psum.sem, 1)

            if tag == "L1x":
                def scalar(a, st):
                    for i in range(NG):
                        a.wait_ge(q_psum.sem, q_psum.at(i + 1))
                        nc.scalar.activation(qa[:, i * 512:i * 512 + 512], PS[:, 4 + i % 2, :], ACT.Identity,
                                             bias=pc("L1x_bq")).then_inc(q_used.sem, 1)
                return dict(tensor=tensor, scalar=scalar, ready=q_used, per=n)

            if tag == "L2x":
                def scalar(a, st):
                    for i in range(2 * NG):
                        g, s = i // 2, i % 2
                        a.wait_ge(q_psum.sem, q_psum.at(i + 1))
                        nc.scalar.activation((x_up, q2_up)[s][:, g * 512:g * 512 + 512], PS[:, 4 + i % 2, :], ACT.Copy)\
                            .then_inc(q_up.sem, 1)

                def vector(v, st):
                    for i in range(2 * NG):
                        g, s = i // 2, i % 2
                        c = slice(g * 512, g * 512 + 512)
                        v.wait_ge(q_up.sem, q_up.at(i + 1))
                        v.wait_ge(q_psum.sem, q_psum.at(2 * g + 2))
                        nc.vector.tensor_tensor((x_low, q2_low)[s][:, c], PS[:, 4 + i % 2, :],
                                                (x_up, q2_up)[s][:, c].bitcast(F32), ALU.subtract).then_inc(q_used.sem, 1)
                return dict(tensor=tensor, scalar=scalar, vector=vector, ready=q_used, per=2)

            def scalar(a, st):
                for g in range(NG):
                    c = slice(g * 512, g * 512 + 512)
                    a.wait_ge(q_sum.sem, q_sum.at(g + 1))
                    nc.scalar.activation(x_up[:, c], qb[:, c], ACT.Copy).then_inc(q_up.sem, 1)

            def vector(v, st):
                def lower(g):
                    c = slice(g * 512, g * 512 + 512)
                    v.wait_ge(q_up.sem, q_up.at(g + 1))
                    nc.vector.tensor_tensor(x_low[:, c], qb[:, c], x_up[:, c].bitcast(F32), ALU.subtract)\
                        .then_inc(q_ready.sem, 1)

                for g in range(NG):
                    c = slice(g * 512, g * 512 + 512)
                    v.wait_ge(q_psum.sem, q_psum.at(2 * g + 1))
                    nc.vector.tensor_tensor(qa[:, c], PS[:, 4, :], pc("cos"), ALU.mult).then_inc(q_used.sem, 1)
                    v.wait_ge(q_psum.sem, q_psum.at(2 * g + 2))
                    nc.vector.tensor_tensor(qb[:, c], PS[:, 5, :], pc("sin"), ALU.mult).then_inc(q_used.sem, 1)
                    v.wait_ge(q_used.sem, q_used.at(2 * g + 2))
                    nc.vector.tensor_tensor(qb[:, c], qa[:, c], qb[:, c], ALU.add).then_inc(q_sum.sem, 1)
                    if g:
                        lower(g - 1)
                lower(NG - 1)
            return dict(tensor=tensor, scalar=scalar, vector=vector, ready=q_ready, per=1)

        def attention_stage(tag, q_ready, q_per, kv, after_nm):
            kb = kb_of[tag]
            sets = 2 if tag == "L2x" else 1
            units = NT * sets
            q = [(x_up, x_low), (q2_up, q2_low)]
            scale = {"L0x": float(D) ** -0.5, "L2x": float(HD) ** -0.5, "L3x": 1.0}[tag]
            key_halves = halves_of[tag][:, 0:2 * sets * B * K].rearrange("p (s u n) -> p s u n", s=sets, u=2)
            kb_ready = sem("kb_ready", 2 * sets * B)
            scores_ready = sem("scores", units)
            scores_used = sem("scores_used", units)
            to_shift = sem("to_shift", 0 if sets == 2 else units)
            shifted = sem("shifted_2" if sets == 2 else "shifted", units)
            exp_ready = sem("exp", units)
            pT_psum = sem("pT_psum", 3 * units)
            pT_ready = sem("pT", 3 * units)
            o_psum = sem("o_psum", units)
            o_used = sem("o_used", units)
            o_ready = sem("o", NT)
            oT_psum = sem("oT_psum", NT)
            oT_ready = sem("oT", NT)
            y_psum = sem("y_psum", NT)
            x_done = sem("x_done", NT)
            if tag == "L3x":
                aT_ready = sem("attT", NT)
                g_psum = sem("gate_psum", NT)
                g_in = sem("gate_in", NT)
                g_tanh = sem("gate_tanh", NT)
                residual = sem("residual", NT)
            if tag == "L2x":
                ss_ready = sem("square_sum", NT)
                rms_ready = sem("rms", NT)
            groups = [range(i, min(i + 4, NBLK)) for i in range(0, NBLK, 4)]

            def tile_of(u):
                return u // sets

            def exps_of(u):
                return score[:, u % 3, :, :].rearrange("p h k -> p (h k)")

            lag = 2 if tag == "L2x" else 1

            def after_unit(u):
                d = u - (sets - 1) - lag
                return d // sets if d >= 0 and d % sets == 0 else None

            def tensor(pe):
                def scores(u):
                    t, s = tile_of(u), u % sets
                    b = t // TG
                    pe.wait_ge(q_ready.sem, q_ready.at(q_per * (b + 1)))
                    pe.wait_ge(kb_ready.sem, kb_ready.at(2 * (sets * b + s + 1)))
                    if u:
                        pe.wait_ge(scores_used.sem, scores_used.at(u))
                    (up, low), c = q[s], slice(t * P, t * P + P)
                    for r in range(RG):
                        keys_up, keys_low = (kb[:, s, b % 2, i, HR * r:HR * r + HR, :] for i in range(2))
                        nc.tensor.matmul(PS[:, r, 0:HR * K], up[:, c], keys_up, start=True, stop=False)
                        nc.tensor.matmul(PS[:, r, 0:HR * K], up[:, c], keys_low, start=False, stop=False)
                        last = nc.tensor.matmul(PS[:, r, 0:HR * K], low[:, c], keys_up, start=False, stop=True)
                    last.then_inc(scores_ready.sem, 1)

                def transposes(u, parts=(0, 1, 2)):
                    pe.wait_ge(exp_ready.sem, exp_ready.at(u + 1))
                    for i in parts:
                        blocks = groups[i]
                        n = 3 * u + i
                        if n >= 2:
                            pe.wait_ge(pT_ready.sem, pT_ready.at(n - 1))
                        for j in blocks:
                            w = BLOCKS[j][2]
                            last = nc.tensor.transpose(PS[0:w, 4 + n % 2, (j % 4) * P:(j % 4) * P + P],
                                                       exps_of(u)[:, j * P:j * P + w], ident)
                        last.then_inc(pT_psum.sem, 1)

                def weighted(u):
                    b = tile_of(u) // TG
                    if u:
                        pe.wait_ge(o_used.sem, o_used.at(u))
                    for j, (h0, nh, w) in enumerate(BLOCKS):
                        if j % 4 == 0:
                            pe.wait_ge(pT_ready.sem, pT_ready.at(3 * u + j // 4 + 1))
                        pT = hT[0:w, u % 2, j // 4, (j % 4) * P:(j % 4) * P + P]
                        if j == 0:
                            nc.tensor.matmul(PS[:, 6, 0:H * VW], pT, vfull[:, b, :], start=True, stop=False)
                        else:
                            last = nc.tensor.matmul(PS[:, 6, h0 * VW:(h0 + nh) * VW], pT,
                                                    vblk[0:w, b, 3 * j * VW:(3 * j + nh) * VW],
                                                    start=False, stop=j == NBLK - 1)
                    last.then_inc(o_psum.sem, 1)

                def out_transpose(t):
                    pe.wait_ge(o_ready.sem, o_ready.at(t + 1))
                    if t:
                        free = g_in if tag == "L3x" else x_done
                        pe.wait_ge(free.sem, free.at(t))
                    nc.tensor.transpose(PS[:, 7, 0:P], (oc2 if tag == "L2x" else oc)[:, t % 2, :], ident)\
                        .then_inc(oT_psum.sem, 1)

                def out_project(t):
                    pe.wait_ge(oT_ready.sem, oT_ready.at(t + 1))
                    last = nc.tensor.matmul(PS[:, 7, P:2 * P], ocT[:, t % 2, :], pc(f"{tag}_wo"), start=True, stop=True)
                    if tag == "L3x":
                        last = nc.tensor.matmul(PS[:, 7, 2 * P:3 * P], pc("L3x_wo"), ocT[:, t % 2, :],
                                                start=True, stop=True)
                    last.then_inc(y_psum.sem, 1)

                def gate(t):
                    pe.wait_ge(aT_ready.sem, aT_ready.at(t + 1))
                    nc.tensor.matmul(PS[:, 7, 3 * P:4 * P], attT[:, t % 2, :], pc("L3x_wg"), start=True, stop=True)\
                        .then_inc(g_psum.sem, 1)

                read, n_read = kv["all_read"]
                pe.wait_ge(read.sem, read.at(n_read))
                scores(0)
                scores(1)
                for u in range(units + lag):
                    if u == 0:
                        transposes(0)
                    if u + 2 < units:
                        scores(u + 2)
                    done = after_unit(u)
                    if done is not None:
                        out_transpose(done)
                    if 0 < u < units:
                        transposes(u, (0, 1))
                    if done is not None:
                        out_project(done)
                    if 0 < u < units:
                        transposes(u, (2,))
                    if u < units:
                        weighted(u)
                    if done is not None and tag == "L3x":
                        gate(done)

            def vector(v, st):
                def maxima(u):
                    t = tile_of(u)
                    v.wait_ge(scores_ready.sem, scores_ready.at(u + 1))
                    ps = PS[:, 0:RG, 0:HR * K].rearrange("p r (h k) -> p r h k", h=HR)
                    dst = score[:, u % 3, :, :]
                    dst4 = dst.rearrange("p (r h) k -> p r h k", r=RG)
                    m = mx[:, u % 3, :]
                    if tag == "L2x":
                        nc.vector.tensor_reduce(m, ps, AX.X, ALU.max).then_inc(v_step, st.one())
                        v.wait_ge(v_step, st.n)
                        nc.vector.tensor_tensor(dst4, ps, m.rearrange("p (r h) -> p r h", r=RG).unsqueeze(3)
                                                .to_broadcast([P, RG, HR, K]), ALU.subtract).then_inc(scores_used.sem, 1)
                        return
                    if tag == "L0x":
                        other, op = bound[:, t, :], ALU.min
                    else:
                        other, op = pc("tbias")[:, (t % TG) * K:(t % TG) * K + K], ALU.add
                    nc.vector.tensor_tensor(dst4, ps, other.unsqueeze(1).unsqueeze(1).to_broadcast([P, RG, HR, K]), op)\
                        .then_inc(scores_used.sem, 1)
                    v.wait_ge(scores_used.sem, scores_used.at(u + 1))
                    nc.vector.tensor_reduce(m, dst, AX.X, ALU.max).then_inc(to_shift.sem, 1)

                def normalise(u):
                    t, s = tile_of(u), u % sets
                    v.wait_ge(o_psum.sem, o_psum.at(u + 1))
                    o = PS[:, 6, 0:H * VW].rearrange("p (h d) -> p h d", h=H)
                    r = rec[:, u % 2, :]
                    nc.vector.reciprocal(r, o[:, :, HD]).then_inc(v_step, st.one())
                    v.wait_ge(v_step, st.n)
                    if tag == "L2x" and s:
                        nc.vector.tensor_tensor(r, r, lam[:, :], ALU.mult).then_inc(v_step, st.one())
                        v.wait_ge(v_step, st.n)
                    rb = r.unsqueeze(2).to_broadcast([P, H, HD])
                    heads = oc[:, t % 2, :].rearrange("p (h d) -> p h d", h=H)
                    if tag != "L2x":
                        nc.vector.tensor_tensor(heads, o[:, :, 0:HD], rb, ALU.mult).then_inc(o_used.sem, 1)
                        v.wait_ge(o_used.sem, o_used.at(u + 1))
                        v.sem_inc(o_ready.sem, 1)
                        return
                    if s == 0:
                        nc.vector.tensor_tensor(heads, o[:, :, 0:HD], rb, ALU.mult).then_inc(o_used.sem, 1)
                        return
                    second = fin[:, 0, :].rearrange("p (h d) -> p h d", h=H)
                    nc.vector.tensor_tensor(second, o[:, :, 0:HD], rb, ALU.mult).then_inc(o_used.sem, 1)
                    v.wait_ge(o_used.sem, o_used.at(u + 1))
                    nc.vector.tensor_tensor(oc[:, t % 2, :], oc[:, t % 2, :], fin[:, 0, :], ALU.subtract)\
                        .then_inc(v_step, st.one())
                    v.wait_ge(v_step, st.n)
                    nc.vector.scalar_tensor_tensor(fin[:, 1, :], oc[:, t % 2, :], 1.0, oc[:, t % 2, :], ALU.mult,
                                                   ALU.mult, accum_out=oss[:, t % 2:t % 2 + 1]).then_inc(ss_ready.sem, 1)

                def root_mean_square(t):
                    v.wait_ge(rms_ready.sem, rms_ready.at(t + 1))
                    nc.vector.tensor_scalar(oc2[:, t % 2, :], oc[:, t % 2, :], osr[:, t % 2:t % 2 + 1], None, ALU.mult)\
                        .then_inc(o_ready.sem, 1)

                def evacuate_oT(t):
                    v.wait_ge(oT_psum.sem, oT_psum.at(t + 1))
                    if tag == "L2x":
                        nc.vector.tensor_scalar(ocT[:, t % 2, :], PS[:, 7, 0:P], pc("L2x_norm"), None, ALU.mult)\
                            .then_inc(oT_ready.sem, 1)
                    else:
                        nc.vector.tensor_copy(ocT[:, t % 2, :], PS[:, 7, 0:P]).then_inc(oT_ready.sem, 1)

                def finish(t):
                    v.wait_ge(y_psum.sem, y_psum.at(t + 1))
                    y, att, xt = PS[:, 7, P:2 * P], fin[:, 2, :], X[:, t, :]
                    if tag == "L3x":
                        nc.vector.tensor_scalar(attT[:, t % 2, :], PS[:, 7, 2 * P:3 * P], pc("L3x_boc"), None, ALU.add)\
                            .then_inc(v_step, st.one())
                    nc.vector.tensor_tensor(att, y, pc(f"{tag}_bo"), ALU.add).then_inc(v_step, st.one())
                    if tag != "L3x":
                        v.wait_ge(v_step, st.n)
                        nc.vector.tensor_tensor(xt, xt, att, ALU.add).then_inc(x_done.sem, 1)
                        return
                    v.wait_ge(v_step, st.n)
                    v.sem_inc(aT_ready.sem, 1)
                    nc.vector.tensor_tensor(gdiff[:, t % 2, :], att, xn[:, t, :], ALU.subtract).then_inc(v_step, st.one())

                def gate_in(t):
                    v.wait_ge(g_psum.sem, g_psum.at(t + 1))
                    nc.vector.tensor_tensor(gin[:, t % 2, :], PS[:, 7, 3 * P:4 * P], pc("L3x_bg"), ALU.add)\
                        .then_inc(g_in.sem, 1)

                def gate_out(t):
                    g, d = gin[:, t % 2, :], gdiff[:, t % 2, :]
                    v.wait_ge(g_tanh.sem, g_tanh.at(t + 1))
                    nc.vector.scalar_tensor_tensor(d, g, 1.0, d, ALU.add, ALU.mult).then_inc(v_step, st.one())
                    v.wait_ge(v_step, st.n)
                    v.wait_ge(residual.sem, residual.at(t + 1))
                    nc.vector.scalar_tensor_tensor(X[:, t, :], d, 0.5, X[:, t, :], ALU.mult, ALU.add)\
                        .then_inc(x_done.sem, 1)

                if tag == "L2x":
                    nc.vector.tensor_tensor(lam[:, :], pc("L2x_lam1"), pc("L2x_lam2"), ALU.subtract).then_inc(v_step, st.one())
                    v.wait_ge(v_step, st.n)
                    nc.vector.tensor_scalar(lam[:, :], lam[:, :], 0.1, None, ALU.add).then_inc(v_step, st.one())
                    v.wait_ge(v_step, st.n)
                maxima(0)
                maxima(1)
                for u in range(units + lag + (tag == "L3x")):
                    done = after_unit(u) if u < units + lag else None
                    if tag == "L3x" and u >= 2:
                        gate_in(u - 2)
                    if done is not None:
                        if tag == "L2x":
                            root_mean_square(done)
                        evacuate_oT(done)
                    if u + 2 < units:
                        maxima(u + 2)
                    if done is not None:
                        finish(done)
                    if tag == "L3x" and u >= 2:
                        gate_out(u - 2)
                    final = u - 2 if tag == "L3x" and u >= 2 else done if tag != "L3x" else None
                    if final is not None:
                        after_nm["vector_tile"](v, st, final)
                    if u < units:
                        normalise(u)

            def scalar(a, st):
                def exps(u):
                    ready = scores_used if sets == 2 else shifted
                    a.wait_ge(ready.sem, ready.at(u + 1))
                    nc.scalar.activation(score[:, u % 3, :, :], score[:, u % 3, :, :], ACT.Exp, scale=scale)\
                        .then_inc(exp_ready.sem, 1)

                exps(0)
                for u in range(units + lag + (tag == "L3x")):
                    if tag == "L3x" and u >= 2:
                        t = u - 2
                        a.wait_ge(g_in.sem, g_in.at(t + 1))
                        nc.scalar.activation(gin[:, t % 2, :], gin[:, t % 2, :], ACT.Tanh, scale=0.5).then_inc(g_tanh.sem, 1)
                    if u < units:
                        for i, blocks in enumerate(groups):
                            n, width = 3 * u + i, len(blocks) * P
                            a.wait_ge(pT_psum.sem, pT_psum.at(n + 1))
                            if i == 0 and u >= 2:
                                a.wait_ge(o_psum.sem, o_psum.at(u - 1))
                            full = width if blocks[-1] < NBLK - 1 else width - P
                            nc.scalar.activation(hT[:, u % 2, i, 0:full], PS[:, 4 + n % 2, 0:full], ACT.Copy)\
                                .then_inc(*((pT_ready.sem, 1) if full == width else (a_step, st.one())))
                            if full < width:
                                rows = BLOCKS[-1][2]
                                nc.scalar.activation(hT[0:rows, u % 2, i, full:width], PS[0:rows, 4 + n % 2, full:width],
                                                     ACT.Copy).then_inc(pT_ready.sem, 1)
                    if u + 1 < units:
                        exps(u + 1)

            def pool(p, st):
                def split_keys():
                    for s in range(sets):
                        src, (up, low) = kv["keysT"][s], (key_halves[:, s, i, :] for i in range(2))
                        if tag == "L3x":
                            nc.gpsimd.tensor_scalar(low, src, float(HD) ** -0.5, None, ALU.mult).then_inc(p_step, st.one())
                            p.wait_ge(p_step, st.n)
                            src = low
                        nc.gpsimd.tensor_scalar(up.bitcast(F32R), src, 1.0, None, ALU.mult).then_inc(p_step, st.one())
                        p.wait_ge(p_step, st.n)
                        nc.gpsimd.tensor_tensor(low, src, up, ALU.subtract).then_inc(p_step, st.one())
                    p.wait_ge(p_step, st.n)

                def spread_keys(b, s, i):
                    if b >= 2:
                        p.wait_ge(scores_ready.sem, scores_ready.at(sets * TG * (b - 1)))
                    keysT = key_halves[:, s, i, b * K:b * K + K].unsqueeze(1).to_broadcast([P, H, K])
                    nc.gpsimd.tensor_tensor(kb[:, s, b % 2, i, :, :], keysT,
                                            pc("heads").unsqueeze(2).to_broadcast([P, H, K]), ALU.mult)\
                        .then_inc(kb_ready.sem, 1)

                def shift(u):
                    p.wait_ge(to_shift.sem, to_shift.at(u + 1))
                    nc.gpsimd.tensor_tensor(score[:, u % 3, :, :], score[:, u % 3, :, :],
                                            mx[:, u % 3, :].unsqueeze(2).to_broadcast([P, H, K]), ALU.subtract)\
                        .then_inc(shifted.sem, 1)

                keys, n_keys = kv["kT_ready"]
                p.wait_ge(keys.sem, keys.at(n_keys))
                split_keys()
                for s in range(sets):
                    for i in range(2):
                        spread_keys(0, s, i)
                for t in range(NT):
                    b = t // TG + 1
                    if b < B and sets == 2 and t % TG < 2:
                        for i in range(2):
                            spread_keys(b, t % TG, i)
                    if b < B and sets == 1 and t > 1 and t % TG < 2:
                        spread_keys(b, 0, t % TG)
                    if sets == 1:
                        shift(t)
                        if tag == "L3x":
                            nc.gpsimd.tensor_tensor(X[:, t, :], X[:, t, :], xn[:, t, :], ALU.add).then_inc(residual.sem, 1)
                        if t < 2:
                            spread_keys(1, 0, t)
                    g, left = divmod(t - (7 if tag == "L3x" else 6), TG)
                    if sets == 1 and left == 0 and 0 <= g < NG - 1:
                        after_nm["pool_group"](p, 0, g)
                    if tag == "L2x":
                        p.wait_ge(ss_ready.sem, ss_ready.at(t + 1))
                        nc.gpsimd.tensor_scalar(oss[:, t % 2:t % 2 + 1], oss[:, t % 2:t % 2 + 1], 1.0 / D,
                                                RMS_EPS, ALU.mult, ALU.add).then_inc(p_step, st.one())
                        p.wait_ge(p_step, st.n)
                        nc.gpsimd.tensor_tensor(osr[:, t % 2:t % 2 + 1], oss[:, t % 2:t % 2 + 1], mhalf[:, 0:1],
                                                ALU.pow).then_inc(rms_ready.sem, 1)
                        if t % TG == TG - 1 and t < NT - 1:
                            after_nm["pool_group"](p, 0, t // TG)
            return dict(tensor=tensor, vector=vector, scalar=scalar, pool=pool, x_done=x_done)

        def single_stage(tag, q_ready, kv, after_nm):
            scores_ready = sem("scores", B)
            shifted = sem("shifted", B)
            exp_ready = sem("exp", B)
            pT_psum = sem("pT_psum", B)
            pT_ready = sem("pT", B)
            o_psum = sem("o_psum", B)
            x_done = sem("x_done", NT)

            def tensor(pe):
                def scores(b):
                    pe.wait_ge(q_ready.sem, q_ready.at(b + 1))
                    if b >= 2:
                        pe.wait_ge(shifted.sem, shifted.at(b - 1))
                    for j in range(TG):
                        t = TG * b + j
                        last = nc.tensor.matmul(PS[:, b % 2, j * K:j * K + K], qa[:, t * P:t * P + P],
                                                k1T[:, b * K:b * K + K], start=True, stop=True)
                    last.then_inc(scores_ready.sem, 1)

                read, n_read = kv["all_read"]
                pe.wait_ge(read.sem, read.at(n_read))
                scores(0)
                for b in range(B):
                    if b + 1 < B:
                        scores(b + 1)
                    pe.wait_ge(exp_ready.sem, exp_ready.at(b + 1))
                    for j in range(TG):
                        last = nc.tensor.transpose(PS[0:K, 2 + b % 2, j * P:j * P + P], score[:, b % 2, j, :], ident)
                    last.then_inc(pT_psum.sem, 1)
                    pe.wait_ge(pT_ready.sem, pT_ready.at(b + 1))
                    if b >= 2:
                        pe.wait_ge(x_done.sem, x_done.at(TG * (b - 1)))
                    for j in range(TG):
                        last = nc.tensor.matmul(PS[:, 4 + b % 2, j * P:j * P + P], hT[0:K, b % 2, 0, j * P:j * P + P],
                                                v1[:, b, :], start=True, stop=True)
                    last.then_inc(o_psum.sem, 1)

            def vector(v, st):
                def shift(b):
                    v.wait_ge(scores_ready.sem, scores_ready.at(b + 1))
                    ps = PS[:, b % 2, 0:TG * K].rearrange("p (j k) -> p j k", j=TG)
                    m = mx[:, b % 2, 0:TG]
                    nc.vector.tensor_reduce(m, ps, AX.X, ALU.max).then_inc(v_step, st.one())
                    v.wait_ge(v_step, st.n)
                    nc.vector.tensor_tensor(score[:, b % 2, 0:TG, :], ps, m.unsqueeze(2).to_broadcast([P, TG, K]),
                                            ALU.subtract).then_inc(shifted.sem, 1)

                shift(0)
                for b in range(B):
                    if b + 1 < B:
                        shift(b + 1)
                    v.wait_ge(exp_ready.sem, exp_ready.at(b + 1))
                    r = rec[:, b % 2, 0:TG]
                    nc.vector.tensor_reduce(r, score[:, b % 2, 0:TG, :], AX.X, ALU.add).then_inc(v_step, st.one())
                    v.wait_ge(v_step, st.n)
                    nc.vector.reciprocal(r, r).then_inc(v_step, st.one())
                    v.wait_ge(v_step, st.n)
                    v.wait_ge(o_psum.sem, o_psum.at(b + 1))
                    for j in range(TG):
                        t = TG * b + j
                        nc.vector.scalar_tensor_tensor(X[:, t, :], PS[:, 4 + b % 2, j * P:j * P + P], r[:, j:j + 1],
                                                       X[:, t, :], ALU.mult, ALU.add).then_inc(x_done.sem, 1)
                        after_nm["vector_tile"](v, st, t)

            def scalar(a, st):
                def exps(b):
                    a.wait_ge(shifted.sem, shifted.at(b + 1))
                    nc.scalar.activation(score[:, b % 2, 0:TG, :], score[:, b % 2, 0:TG, :], ACT.Exp,
                                         scale=float(D) ** -0.5).then_inc(exp_ready.sem, 1)
                exps(0)
                for b in range(B):
                    a.wait_ge(pT_psum.sem, pT_psum.at(b + 1))
                    nc.scalar.activation(hT[0:K, b % 2, 0, :], PS[0:K, 2 + b % 2, :], ACT.Copy).then_inc(pT_ready.sem, 1)
                    if b + 1 < B:
                        exps(b + 1)
            def pool(p, st):
                for g in range(NG - 1):
                    after_nm["pool_group"](p, 0, g)
            return dict(tensor=tensor, vector=vector, scalar=scalar, pool=pool, x_done=x_done)

        def route_stage(tag, xT_ready):
            logits_psum = sem("logits", NG)
            e_in = sem("route_in", 1)
            e_out = sem("route_exp", 1)
            w_ready = sem("w", 1)
            wT_psum = sem("wT_psum", 0 if tag == "L3f" else NG)
            wT_ready = sem("wT", 0 if tag == "L3f" else NG)
            b2_psum = sem("b2_psum", 0 if tag == "L3f" else NG)
            x_first = sem("x_first", NG)
            n_e = FFNS[tag]["experts"]
            if tag == "L2f":
                oh_ready = sem("L2f_onehots")
                count_psum = sem("L2f_counts")

            def tensor(pe, g):
                pe.wait_ge(xT_ready.sem, xT_ready.at(g + 1))
                for t in range(TG * g, TG * g + TG):
                    last = nc.tensor.matmul(PS[:, 6, t * E:t * E + E], xnT[:, t * P:t * P + P], pc(f"{tag}_wr"),
                                            start=True, stop=True)
                    if t % TG == TG - 1:
                        last.then_inc(logits_psum.sem, 1)

            def tensor_counts(pe):
                if tag == "L2f":
                    pe.wait_ge(oh_ready.sem, oh_ready.at(2))
                    for i in range(2):
                        oh = rt[:, 4 + i, :, :]
                        nc.tensor.matmul(PS[:, 7, i * P:i * P + P], pc("before"), oh, start=True, stop=True)
                        last = nc.tensor.matmul(PS[:, 7, (2 + i) * P:(3 + i) * P], pc("ones"), oh, start=True, stop=True)
                    last.then_inc(count_psum.sem, 1)

            def tensor_b2(pe):
                if tag == "L3f":
                    return
                pe.wait_ge(w_ready.sem, w_ready.at(1))
                for g in range(NG):
                    if g >= 2:
                        pe.wait_ge(wT_ready.sem, wT_ready.at(g - 1))
                    for j in range(TG):
                        last = nc.tensor.transpose(PS[0:n_e, 6 + g % 2, j * P:j * P + P], wts[:, TG * g + j, 0:n_e], ident)
                    last.then_inc(wT_psum.sem, 1)
                for g in range(NG):
                    pe.wait_ge(wT_ready.sem, wT_ready.at(min(g + 3, NG)))
                    if g >= 2:
                        pe.wait_ge(x_first.sem, x_first.at(g - 1))
                    for j in range(TG):
                        t = TG * g + j
                        last = nc.tensor.matmul(PS[:, 6 + g % 2, j * P:j * P + P], qb[0:n_e, t * P:t * P + P],
                                                pc(f"{tag}_b2", n_e), start=True, stop=True)
                    last.then_inc(b2_psum.sem, 1)

            def scalar(a, st):
                a.wait_ge(e_in.sem, e_in.at(1))
                nc.scalar.activation(rt[:, 1, :, :], rt[:, 1, :, :], ACT.Exp).then_inc(e_out.sem, 1)

            def scalar_b2(a, st):
                if tag == "L3f":
                    return
                for g in range(NG):
                    a.wait_ge(wT_psum.sem, wT_psum.at(g + 1))
                    nc.scalar.activation(qb[0:n_e, g * 512:g * 512 + 512], PS[0:n_e, 6 + g % 2, :], ACT.Copy)\
                        .then_inc(wT_ready.sem, 1)

            def vector(v, st, middle):
                def over_e(a):
                    return a.unsqueeze(2).to_broadcast([P, NT, E])

                iota = pc("iota").unsqueeze(1).to_broadcast([P, NT, E])
                lg, pr, eq, key, oh1, oh2, rest, w = (rt[:, i, :, :] for i in range(8))
                m1, m2, ssum, kmin, keep, g12 = (rs[:, i, 0:NT] for i in range(6))
                v.wait_ge(logits_psum.sem, logits_psum.at(NG))
                logits = PS[:, 6, 0:NT * E].rearrange("p (t e) -> p t e", e=E)
                if tag == "L3f":
                    nc.vector.tensor_copy(lg, logits).then_inc(v_step, st.one())
                    v.wait_ge(v_step, st.n)
                else:
                    nc.vector.tensor_tensor(lg, logits, pc(f"{tag}_br").unsqueeze(1).to_broadcast([P, NT, E]),
                                                    ALU.add).then_inc(v_step, st.one())
                    v.wait_ge(v_step, st.n)
                nc.vector.tensor_reduce(m1, lg, AX.X, ALU.max).then_inc(v_step, st.one())
                v.wait_ge(v_step, st.n)
                nc.vector.tensor_tensor(pr, lg, over_e(m1), ALU.subtract).then_inc(e_in.sem, 1)
                v.wait_ge(e_out.sem, e_out.at(1))

                def first_of_max(src, m, oh):
                    nc.vector.tensor_tensor(eq, src, over_e(m), ALU.is_equal).then_inc(v_step, st.one())
                    v.wait_ge(v_step, st.n)
                    nc.vector.scalar_tensor_tensor(key, eq, -1000.0, iota, ALU.mult, ALU.add).then_inc(v_step, st.one())
                    v.wait_ge(v_step, st.n)
                    nc.vector.tensor_reduce(kmin, key, AX.X, ALU.min).then_inc(v_step, st.one())
                    v.wait_ge(v_step, st.n)
                    return nc.vector.tensor_tensor(oh, key, over_e(kmin), ALU.is_equal)

                wv = wts[:, :, 0:E]
                if tag == "L0f":
                    first_of_max(lg, m1, oh1).then_inc(v_step, st.one())
                    v.wait_ge(v_step, st.n)
                    nc.vector.scalar_tensor_tensor(rest, oh1, -3.0e38, lg, ALU.mult, ALU.add).then_inc(v_step, st.one())
                    v.wait_ge(v_step, st.n)
                    nc.vector.tensor_reduce(m2, rest, AX.X, ALU.max).then_inc(v_step, st.one())
                    v.wait_ge(v_step, st.n)
                    nc.vector.tensor_tensor(eq, lg, over_e(m2), ALU.is_ge).then_inc(v_step, st.one())
                    v.wait_ge(v_step, st.n)
                    nc.vector.tensor_tensor(w, pr, eq, ALU.mult).then_inc(v_step, st.one())
                    v.wait_ge(v_step, st.n)
                    nc.vector.tensor_reduce(ssum, w, AX.X, ALU.add).then_inc(v_step, st.one())
                    v.wait_ge(v_step, st.n)
                    nc.vector.reciprocal(ssum, ssum).then_inc(v_step, st.one())
                    v.wait_ge(v_step, st.n)
                    nc.vector.tensor_tensor(wv, w, over_e(ssum), ALU.mult).then_inc(w_ready.sem, 1)
                else:
                    nc.vector.tensor_reduce(ssum, pr, AX.X, ALU.add).then_inc(v_step, st.one())
                    v.wait_ge(v_step, st.n)
                    nc.vector.reciprocal(ssum, ssum).then_inc(v_step, st.one())
                    v.wait_ge(v_step, st.n)
                    nc.vector.tensor_tensor(pr, pr, over_e(ssum), ALU.mult).then_inc(v_step, st.one())
                    v.wait_ge(v_step, st.n)
                    nc.vector.tensor_reduce(m1, pr, AX.X, ALU.max).then_inc(v_step, st.one())
                    v.wait_ge(v_step, st.n)
                    if tag == "L2f":
                        first_of_max(pr, m1, oh1).then_inc(oh_ready.sem, 1)
                        v.wait_ge(oh_ready.sem, oh_ready.at(1))
                    else:
                        first_of_max(pr, m1, oh1).then_inc(v_step, st.one())
                        v.wait_ge(v_step, st.n)
                    middle()
                    nc.vector.scalar_tensor_tensor(rest, oh1, -3.0, pr, ALU.mult, ALU.add).then_inc(v_step, st.one())
                    v.wait_ge(v_step, st.n)
                    nc.vector.tensor_reduce(m2, rest, AX.X, ALU.max).then_inc(v_step, st.one())
                    v.wait_ge(v_step, st.n)
                    middle()
                    if tag == "L2f":
                        first_of_max(rest, m2, oh2).then_inc(oh_ready.sem, 1)
                        v.wait_ge(oh_ready.sem, oh_ready.at(2))
                    else:
                        first_of_max(rest, m2, oh2).then_inc(v_step, st.one())
                        v.wait_ge(v_step, st.n)
                    middle()
                    if tag != "L1f":
                        nc.vector.tensor_tensor(g12, m1, m2, ALU.add).then_inc(v_step, st.one())
                        v.wait_ge(v_step, st.n)
                        nc.vector.reciprocal(g12, g12).then_inc(v_step, st.one())
                        v.wait_ge(v_step, st.n)
                    if tag == "L2f":
                        v.wait_ge(count_psum.sem, count_psum.at(1))
                        before = PS[:, 7, 0:2 * P].rearrange("p (t e) -> p t e", e=E)
                        nc.vector.memset(rc[:, 0, 0, :], 0.0).then_inc(v_step, st.one())
                        nc.vector.tensor_copy(rc[:, 0, 1:2 * NT, :],
                                                      PS[:, 7, 2 * P:4 * P].rearrange("p (t e) -> p t e", e=E)[:, 0:2 * NT - 1, :]).then_inc(v_step, st.one())
                        v.wait_ge(v_step, st.n)
                        side, step = 0, 1
                        while step < 2 * NT:
                            a, b = rc[:, side, :, :], rc[:, 1 - side, :, :]
                            nc.vector.tensor_copy(b[:, 0:step, :], a[:, 0:step, :]).then_inc(v_step, st.one())
                            nc.vector.tensor_tensor(b[:, step:, :], a[:, step:, :], a[:, 0:2 * NT - step, :], ALU.add).then_inc(v_step, st.one())
                            v.wait_ge(v_step, st.n)
                            side, step = 1 - side, 2 * step
                        pos, work = rc[:, side, :, :], rc[:, 1 - side, :, :]
                        nc.vector.tensor_tensor(work, pos, before, ALU.add).then_inc(v_step, st.one())
                        v.wait_ge(v_step, st.n)
                        oh12 = rt[:, 4:6, :, :].rearrange("p a t e -> p (a t) e")
                        nc.vector.tensor_tensor(pos, work, oh12, ALU.mult).then_inc(v_step, st.one())
                        v.wait_ge(v_step, st.n)
                        both = rs[:, 4, :]
                        nc.vector.tensor_reduce(both, pos, AX.X, ALU.add).then_inc(v_step, st.one())
                        v.wait_ge(v_step, st.n)
                        nc.vector.tensor_scalar(both, both, float(CAPACITY), None, ALU.is_lt).then_inc(v_step, st.one())
                        v.wait_ge(v_step, st.n)
                        nc.vector.tensor_tensor(work, oh12, both.unsqueeze(2).to_broadcast([P, 2 * NT, E]), ALU.mult).then_inc(v_step, st.one())
                        v.wait_ge(v_step, st.n)
                        nc.vector.tensor_tensor(eq, work[:, 0:NT, :], work[:, NT:2 * NT, :], ALU.add).then_inc(v_step, st.one())
                        v.wait_ge(v_step, st.n)
                    else:
                        nc.vector.tensor_tensor(eq, oh1, oh2, ALU.add).then_inc(v_step, st.one())
                        v.wait_ge(v_step, st.n)
                    if tag == "L1f":
                        nc.vector.memset(wts[:, :, E:E + 1], 1.0).then_inc(v_step, st.one())
                        nc.vector.tensor_tensor(wv, pr, eq, ALU.mult).then_inc(w_ready.sem, 1)
                    else:
                        nc.vector.tensor_tensor(w, pr, eq, ALU.mult).then_inc(v_step, st.one())
                        v.wait_ge(v_step, st.n)
                        nc.vector.tensor_tensor(wv, w, over_e(g12), ALU.mult).then_inc(w_ready.sem, 1)

            def vector_first(v):
                for g in range(NG):
                    xs = X[:, TG * g:TG * g + TG, :]
                    if tag == "L3f":
                        other = xn[:, TG * g:TG * g + TG, :]
                    else:
                        v.wait_ge(b2_psum.sem, b2_psum.at(g + 1))
                        other = PS[:, 6 + g % 2, :].rearrange("p (t d) -> p t d", d=D)
                    nc.vector.tensor_tensor(xs, xs, other, ALU.add).then_inc(x_first.sem, 1)
            return dict(tensor=tensor, tensor_counts=tensor_counts, tensor_b2=tensor_b2, vector=vector,
                        vector_first=vector_first, scalar=scalar, scalar_b2=scalar_b2, w_ready=w_ready, x_first=x_first,
                        logits=logits_psum)

        def ffn_stage(tag, nm, ro, kv=None, after_nm=None):
            kv_parts = kv["parts"] if kv else {}

            def kv_part(engine, step, *args):
                f = kv_parts.get(engine, {}).get(step)
                if f:
                    f(*args)

            upper_ready, logits_read, x_first = nm["upper_ready"], ro["logits"], ro["x_first"]
            c = FFNS[tag]
            n_e, chunks, rows, gated = c["experts"], c["chunks"], c["rows"], c["gated"]
            w1, w3, w2 = views(tag)
            steps = n_e * NG
            h_psum = sem("h_psum", steps * chunks)
            h_ready = sem("h_gated" if gated else "h", steps * chunks)
            x_split = sem("x_lower", NG)
            w_split = sem("w_halves", n_e)
            upper, halves = split_space(tag)
            y_psum = sem("y_psum", steps)
            y_used = sem("y_used", TG * steps)
            if gated:
                s_ready = sem("silu", steps * chunks)

            def tensor(pe):
                if tag == "L0f":
                    pe.wait_ge(par_in_2, 16)

                def hidden(n):
                    e, g = n // NG, n % NG
                    if g == 0:
                        pe.wait_ge(w_split.sem, w_split.at(e + 1))
                    if e == 0:
                        pe.wait_ge(x_split.sem, x_split.at(g + 1))
                    cols = slice(g * 512, g * 512 + 512)
                    banks = 2 if gated else 4
                    for k in range(chunks):
                        i = n * chunks + k
                        if i >= banks:
                            pe.wait_ge(h_ready.sem, h_ready.at(i - banks + 1))
                        for m in range(2 if gated else 1):
                            w_up, w_low = (halves[:, e % 2, m, u, k * rows:(k + 1) * rows] for u in range(2))
                            dst = PS[0:rows, 2 * m + i % banks, :]
                            nc.tensor.matmul(dst, w_up, upper[:, cols], start=True, stop=False)
                            nc.tensor.matmul(dst, w_up, x_low[:, cols], start=False, stop=False)
                            last = nc.tensor.matmul(dst, w_low, upper[:, cols], start=False, stop=True)
                        last.then_inc(h_psum.sem, 1)

                def output(n):
                    e = n // NG
                    if n % NG == 0:
                        pe.wait_ge(w_loaded[tag][w_third(tag, e)], 48 if gated else 32)
                    if n >= 2:
                        pe.wait_ge(y_used.sem, y_used.at(TG * (n - 1)))
                    pe.wait_ge(h_ready.sem, h_ready.at(chunks * (n + 1)))
                    for j in range(TG):
                        for k in range(chunks):
                            last = nc.tensor.matmul(PS[:, 4 + n % 2, j * P:j * P + P],
                                                    hT[0:rows, n % 2, k, j * P:j * P + P], w2[0:rows, e, k, :],
                                                    start=k == 0, stop=k == chunks - 1)
                    last.then_inc(y_psum.sem, 1)

                nm["tensor"](pe, ro["tensor"])
                pe.wait_ge(upper_ready.sem, upper_ready.at(NG))
                hidden(0)
                ro["tensor_counts"](pe)
                for n in range(steps):
                    if n + 1 < steps:
                        hidden(n + 1)
                    output(n)
                    if n == 1:
                        ro["tensor_b2"](pe)
                    kv_part("tensor", n, pe)
                    if after_nm and n - (steps - NG) >= 1:
                        after_nm["transpose_group"](pe, n - (steps - NG) - 1)
                if tag in w_done:
                    pe.wait_ge(y_used.sem, y_used.at(TG * steps))
                    pe.sem_inc(w_done[tag], 1)

            def scalar(a, st):
                if tag == "L0f":
                    a.wait_ge(par_in_2, 16)
                ro["scalar"](a, st)
                for i in range(steps * chunks):
                    n, k = i // chunks, i % chunks
                    if n == 3 and k == 0:
                        ro["scalar_b2"](a, st)
                    if k == 0:
                        kv_part("scalar", n, a, st)
                    a.wait_ge(h_psum.sem, h_psum.at(i + 1))
                    if gated:
                        if i >= 2:
                            a.wait_ge(h_ready.sem, h_ready.at(i - 1))
                        nc.scalar.activation(gact[0:rows, i % 2, :], PS[0:rows, i % 2, :], c["act"]).then_inc(s_ready.sem, 1)
                    else:
                        if k == 0 and n >= 2:
                            a.wait_ge(y_psum.sem, y_psum.at(n - 1))
                        col = (n // NG) * chunks + k
                        nc.scalar.activation(hT[:, n % 2, k, :], PS[:, i % 4, :], c["act"],
                                             bias=pc(f"{tag}_b1")[:, col:col + 1]).then_inc(h_ready.sem, 1)

            def vector(v, st):
                def gate(n, ks=range(chunks)):
                    for k in ks:
                        i = n * chunks + k
                        v.wait_ge(s_ready.sem, s_ready.at(i + 1))
                        if k == 0 and n >= 2:
                            v.wait_ge(y_psum.sem, y_psum.at(n - 1))
                        nc.vector.tensor_tensor(hT[0:rows, n % 2, k, :], gact[0:rows, i % 2, :], PS[0:rows, 2 + i % 2, :],
                                                ALU.mult).then_inc(h_ready.sem, 1)

                if tag == "L0f":
                    v.wait_ge(par_in_2, 16)
                early = [(0, k) for k in range(chunks)] if gated else []

                def middle():
                    if early:
                        n, k = early.pop(0)
                        gate(n, [k])

                ro["vector"](v, st, middle)
                while early:
                    middle()
                v.wait_ge(ro["w_ready"].sem, ro["w_ready"].at(1))
                for n in range(steps):
                    e, g = n // NG, n % NG
                    if n == 2:
                        v.wait_ge(y_used.sem, y_used.at(2 * TG))
                        ro["vector_first"](v)
                        v.wait_ge(x_first.sem, x_first.at(NG))
                    if gated and n + 1 < steps:
                        gate(n + 1)
                    v.wait_ge(y_psum.sem, y_psum.at(n + 1))
                    for j in range(TG):
                        t = TG * g + j
                        if n >= NG:
                            v.wait_ge(y_used.sem, y_used.at(TG * (n - NG) + j + 1))
                        nc.vector.scalar_tensor_tensor(X[:, t, :], PS[:, 4 + n % 2, j * P:j * P + P],
                                                       wts[:, t, e:e + 1], X[:, t, :], ALU.mult, ALU.add)\
                            .then_inc(y_used.sem, 1)
                    kv_part("vector", n, v, st)
                    if after_nm and n >= steps - NG:
                        after_nm["vector_group"](v, st, g)
            def split_weights(p, st, e):
                p.wait_ge(w_loaded[tag][w_third(tag, e)], 48 if gated else 32)
                if e >= 2:
                    p.wait_ge(h_psum.sem, h_psum.at(chunks * NG * (e - 1)))
                ws = [w1, w3] if gated else [w1]
                for m, w in enumerate(ws):
                    nc.gpsimd.tensor_copy(halves[:, e % 2, m, 0, :], w[:, e, :]).then_inc(p_step, st.one())
                p.wait_ge(p_step, st.n)
                for m, w in enumerate(ws):
                    ins = nc.gpsimd.tensor_tensor(halves[:, e % 2, m, 1, :], w[:, e, :],
                                                  halves[:, e % 2, m, 0, :].bitcast(F32), ALU.subtract)
                    ins.then_inc(*((w_split.sem, 1) if w is ws[-1] else (p_step, st.one())))
                p.wait_ge(p_step, st.n)

            def pool_early(p, st):
                split_weights(p, st, 0)

            def pool(p, st):
                for g in range(NG):
                    p.wait_ge(upper_ready.sem, upper_ready.at(g + 1))
                    p.wait_ge(logits_read.sem, logits_read.at(g + 1))
                    cols = slice(g * 512, g * 512 + 512)
                    nc.gpsimd.tensor_tensor(x_low[:, cols], xnT[:, cols], upper[:, cols].bitcast(F32), ALU.subtract)\
                        .then_inc(x_split.sem, 1)
                for e in range(1, n_e):
                    split_weights(p, st, e)
                    if e == 3 and kv and kv["pool"]:
                        kv["pool"](p, st)
            return dict(tensor=tensor, vector=vector, scalar=scalar, pool=pool, pool_early=pool_early, x_done=y_used, base=TG * NG * (n_e - 1))

        stages = []

        def constants_vector(v, st):
            nc.vector.memset(vaug[:, :, :, HD:VW], 1.0).then_inc(v_step, st.one())
            nc.vector.memset(vaug[:, :, H:H + 1, 0:HD], 0.0).then_inc(v_step, st.one())
            nc.vector.memset(vfull[:, :, 3 * VW:], 0.0).then_inc(v_step, st.one())
            nc.vector.memset(mhalf[:, :], -0.5).then_inc(v_step, st.one())
            v.wait_ge(v_step, st.n)
            v.sem_inc(const_ready, 1)

        def bound_vector(v, st):
            v.wait_ge(mask_loaded, 16)
            m = qb[:, 0:NT * K].bitcast(I32).rearrange("p (t k) -> p t k", t=NT)
            nc.vector.tensor_scalar(bound[:, :, :], m, 0, 3.0e38, ALU.not_equal, ALU.mult).then_inc(v_step, st.one())
            v.wait_ge(v_step, st.n)
            nc.vector.tensor_scalar(bound[:, :, :], bound[:, :, :], NEG, None, ALU.add).then_inc(v_step, st.one())
            v.wait_ge(v_step, st.n)

        def constants_pool(p, st):
            p.wait_ge(const_ready, 1)

        stages.append(dict(vector=constants_vector, pool=constants_pool))
        def loaded(v, t):
            if t % TG == 0:
                v.wait_ge(x_loaded[t // TG], 16)

        def tensor_start(pe):
            pe.wait_ge(par_in_1, 16)
        stages.append(dict(tensor=tensor_start))

        def after(sm, base=0):
            def x_is_ready(v, t):
                v.wait_ge(sm.sem, sm.at(base + t + 1))
            return x_is_ready

        def add(st):
            stages.append({k: st.get(k) for k in ("tensor", "vector", "scalar", "pool")})
            return st

        x_ready = loaded
        x_dones = []
        for layer in range(4):
            tag = f"L{layer}x"
            next_norm = {}
            if layer == 0:
                kv = kv_stage(tag)
                nm = add(norm_stage(tag, x_ready))
                kv_first.update(upper=nm["upper_ready"], q_ready=sem("x_lower", NG))
                add(dict(tensor=kv["tensor_start"], vector=kv["vector_start"]))
                add(dict(vector=bound_vector))
                at = add(attention_stage(tag, kv_first["q_ready"], 1, kv, next_norm))
            else:
                nm = norm_stage(tag, x_ready, "ln" if layer == 3 else None,
                                (pc("L3x_gamma"), pc("L3x_beta")) if layer == 3 else None, before="ffn")
                norm_after_ffn.update(nm)
                add(nm)
                pj = add(proj_stage(tag, nm["ready"]))
                at = add(single_stage(tag, pj["ready"], kv, next_norm) if layer == 1 else
                         attention_stage(tag, pj["ready"], pj["per"], kv, next_norm))
            x_dones.append(at["x_done"])
            x_ready = after(at["x_done"])
            tag = f"L{layer}f"
            nm = norm_stage(tag, x_ready, "rms" if layer == 3 else None,
                            (pc("L3f_rms"), 0.0) if layer == 3 else None, before="attention")
            next_norm.update(nm)
            kv = kv_stage(f"L{layer + 1}x") if layer < 3 else None
            norm_after_ffn = {} if layer < 3 else None
            ff = ffn_stage(tag, nm, route_stage(tag, nm["ready"]), kv, norm_after_ffn)
            add(dict(pool=ff["pool_early"]))
            add({k: nm[k] for k in ("vector", "scalar", "pool")})
            add(ff)
            x_ready = after(ff["x_done"], ff["base"])
        final = sem("x_final", NT)

        block = ctx.enter_context(nc.Block())

        @block.sync
        def _(sp):
            sync_program(sp, final, x_dones)

        @block.tensor
        def _(pe):
            for s in stages:
                if s.get("tensor"):
                    s["tensor"](pe)

        @block.vector
        def _(v):
            st = Steps()
            for s in stages:
                if s.get("vector"):
                    s["vector"](v, st)
            for t in range(NT):
                x_ready(v, t)
                v.sem_inc(final.sem, 1)

        @block.scalar
        def _(a):
            st = Steps()
            for s in stages:
                if s.get("scalar"):
                    s["scalar"](a, st)

        @block.gpsimd
        def _(p):
            st = Steps()
            for s in stages:
                if s.get("pool"):
                    s["pool"](p, st)


def bilinear(n_in, n_out):
    scale = n_out / n_in
    inv = 1.0 / scale
    kernel_scale = max(inv, 1.0)
    at = (np.arange(n_out, dtype=np.float64) + 0.5) * inv - 0.5
    x = np.abs(at[None, :] - np.arange(n_in, dtype=np.float64)[:, None]) / kernel_scale
    w = np.maximum(0.0, 1.0 - x)
    total = w.sum(axis=0, keepdims=True)
    w = np.where(np.abs(total) > 1000.0 * np.finfo(np.float32).eps, w / np.where(total != 0, total, 1), 0)
    inside = (at >= -0.5) & (at <= n_in - 0.5)
    return np.where(inside[None, :], w, 0.0)


def tables():
    pos = np.arange(128, dtype=np.float64)
    dist = np.abs(pos[None, :] - pos[:, None])
    bias = np.exp(-dist * 0.1) - dist * 0.05
    tb = bilinear(128, S).T @ bias @ bilinear(128, K)
    tb = tb.reshape(TG, P, K).transpose(1, 0, 2).reshape(P, TG * K).astype(np.float32)
    half = HD // 2
    inv = (1.0 / np.float32(10000.0) ** (np.arange(0, HD, 2, dtype=np.float32) / np.float32(HD))).astype(np.float32)
    ang = (np.arange(S, dtype=np.float32)[:, None] * inv[None, :]).astype(np.float32).astype(np.float64)
    d = np.arange(P) % HD
    cos = np.cos(ang)[:, d % half].T
    sin = np.sin(ang)[:, d % half].T * np.where(d < half, -1.0, 1.0)[:, None]
    heads = np.arange(P)[:, None] // HD == np.arange(H)[None, :]
    hmask = np.concatenate([(np.arange(P)[:, None] + j * P) // K == h0 + np.arange(min(3, NHM - 3 * j))[None, :]
                            for j, (h0, _, _) in enumerate(BLOCKS)], axis=1)
    wrap = np.arange(K + P)[None, :] % K == np.arange(K)[:, None]
    before = np.arange(P)[:, None] < np.arange(P)[None, :]
    return dict(ident=np.eye(P), heads=heads, headsc=heads * float(HD) ** -0.5, hmask=hmask, wrap=wrap, before=before, ones=np.ones((P, P)), cos=cos, sin=sin, tbias=tb,
                iota=np.tile(np.arange(E), (P, 1)))


def rotated_rows(w):
    return np.concatenate([w.reshape(H, 2, HD // 2, D)[:, 1:2], w.reshape(H, 2, HD // 2, D)[:, 0:1]], axis=1).reshape(D, D)


def kernel(**inp):
    import concourse.bacc as bacc
    from concourse.bass_utils import run_bass_kernel_spmd

    a = {k: np.asarray(v) for k, v in inp.items()}

    def row(v):
        return np.broadcast_to(v.reshape(1, -1), (P, v.size))

    def col(v):
        return v.reshape(-1, 1)

    def chunks(b, n):
        return b.reshape(b.shape[0], n, P).transpose(2, 0, 1).reshape(P, -1)

    ctx = a["ctx_1024"]
    kv1, kv2, qkv = a["L2_xattn_kv1_w"], a["L2_xattn_kv2_w"], a["L3_xattn_Wqkv"]
    L1b1 = np.concatenate([a["L1_ffn_rb1"], a["L1_ffn_sb1"][None]], 0)
    L1b2 = np.concatenate([a["L1_ffn_rb2"], a["L1_ffn_sb2"][None]], 0)
    p = dict(tables())
    p.update(
        ctxT=ctx.transpose(2, 0, 1).reshape(D, B * K), ctx=ctx.transpose(1, 0, 2).reshape(K, B * D),
        L0x_wo=a["L0_xattn_W_out"].T, L0x_bo=row(a["L0_xattn_b_out"]),
        L0f_wr=a["L0_ffn_Wr"], L0f_br=row(a["L0_ffn_br"]), L0f_b1=chunks(a["L0_ffn_b1"], 4), L0f_b2=a["L0_ffn_b2"],
        L1x_wq=a["L1_xattn_W_q"], L1x_wk=a["L1_xattn_W_k"], L1x_wv=a["L1_xattn_W_v"],
        L1x_bq=col(a["L1_xattn_b_q"]), L1x_bk=col(a["L1_xattn_b_k"]), L1x_bv=row(a["L1_xattn_b_v"]),
        L1f_wr=a["L1_ffn_router_w"], L1f_br=row(a["L1_ffn_router_b"]), L1f_b1=chunks(L1b1, 2), L1f_b2=L1b2,
        L2x_q1=a["L2_xattn_q1_w"].T, L2x_q2=a["L2_xattn_q2_w"].T, L2x_k1=kv1[:D].T, L2x_v1=kv1[D:].T,
        L2x_k2=kv2[:D].T, L2x_wo=a["L2_xattn_proj_w"].T, L2x_bo=row(a["L2_xattn_proj_b"]),
        L2x_norm=col(a["L2_xattn_norm_w"]), L2x_lam1=row(a["L2_xattn_lambda_1"]), L2x_lam2=row(a["L2_xattn_lambda_2"]),
        L2f_wr=a["L2_ffn_Wg"], L2f_br=row(a["L2_ffn_bg"]), L2f_b1=chunks(a["L2_ffn_b1"], 4), L2f_b2=a["L2_ffn_b2"],
        L3x_q=qkv[:D].T, L3x_qr=rotated_rows(qkv[:D]).T, L3x_k=qkv[D:2 * D].T, L3x_kr=rotated_rows(qkv[D:2 * D]).T,
        L3x_v=qkv[2 * D:].T, L3x_wo=a["L3_xattn_Wout"].T, L3x_bo=row(a["L3_xattn_b_out"]),
        L3x_boc=col(a["L3_xattn_b_out"]), L3x_wg=a["L3_xattn_Wgate"].T, L3x_bg=row(a["L3_xattn_b_gate"]),
        L3x_gamma=col(a["L3_xattn_gamma"]), L3x_beta=col(a["L3_xattn_beta"]),
        L3f_rms=col(a["L3_ffn_rms_weight"]), L3f_wr=a["L3_ffn_gate_w"].T,
    )
    pack = np.zeros((P, NPAR), np.float32)
    for name, (at, n) in COLUMN.items():
        v = np.asarray(p[name], np.float32)
        pack[:v.shape[0], at:at + n] = v

    def first(w):
        return np.ascontiguousarray(w.transpose(1, 0, 2))

    def second(w, n):
        e, h, d = w.shape
        return np.ascontiguousarray(w.reshape(e, n, h // n, d).transpose(2, 0, 1, 3))

    w = {
        "L0f": [first(a["L0_ffn_W1"]), second(a["L0_ffn_W2"], 4)],
        "L1f": [first(np.concatenate([a["L1_ffn_rw1"], a["L1_ffn_sw1"][None]], 0)),
                second(np.concatenate([a["L1_ffn_rw2"], a["L1_ffn_sw2"][None]], 0), 2)],
        "L2f": [first(a["L2_ffn_W1"]), second(a["L2_ffn_W2"], 4)],
        "L3f": [first(a["L3_ffn_w1"].transpose(0, 2, 1)), second(a["L3_ffn_w2"].transpose(0, 2, 1), 4),
                first(a["L3_ffn_w3"].transpose(0, 2, 1))],
    }
    arrays = {
        "x_tiles": np.ascontiguousarray(a["x"].reshape(NT, P, D).transpose(1, 0, 2)),
        "params": pack,
        "mask": np.ascontiguousarray(a["mask_Bx1xSxS2_if1"].reshape(NT, P, K).transpose(1, 0, 2).reshape(P, NT * K)),
    }
    for f, ws in w.items():
        for i, m in enumerate(ws):
            arrays[f"{f}_w{i}"] = m

    nc = bacc.Bacc("TRN2", target_bir_lowering=False, num_devices=1)
    aps = {k: nc.dram_tensor(k, v.shape, mybir.dt.from_np(v.dtype), kind="ExternalInput").ap() for k, v in arrays.items()}
    out = nc.dram_tensor("x_out", (P, NT, D), F32, kind="ExternalOutput").ap()
    build(nc, aps["x_tiles"], aps["params"], aps["mask"],
          {f: [aps[f"{f}_w{i}"] for i in range(len(ws))] for f, ws in w.items()}, out)
    r = run_bass_kernel_spmd(nc, [arrays], core_ids=[0])
    got = r.results[0]["x_out"]
    return np.ascontiguousarray(got.reshape(P, NT, D).transpose(1, 0, 2)).reshape(B, S, D)
```
